# Optimizing a Trainium2 kernel written in Bass

```python
import numpy as np
import jax
import jax.numpy as jnp

def _softmax(x, axis=-1):
    return jax.nn.softmax(x, axis=axis)

def _gelu(x):
    return jax.nn.gelu(x, approximate=True)

def _silu(x):
    return jax.nn.silu(x)

def _sigmoid(x):
    return jax.nn.sigmoid(x)

def _layernorm(x, axis=-1, eps=1e-05):
    m = jnp.mean(x, axis=axis, keepdims=True)
    v = jnp.var(x, axis=axis, keepdims=True)
    return (x - m) / jnp.sqrt(v + eps)

def _scatter_add(tgt, idx, src, axis=0):
    return tgt.at[idx].add(src)

def _segment_sum(src, seg, n):
    return jax.ops.segment_sum(src, seg, n)
kernel_name = 'mk_gps_d1_gnn_r8_4bd44c'

def setup_inputs(seed: int=0):
    np.random.seed(seed)
    _w = jnp.asarray

    def _rec_inputs():
        import jax
        import jax.numpy as jnp
        _gk = jax.random.key(seed)
        x = -0.0003713 + 1 * jax.random.normal(jax.random.fold_in(_gk, 1), (6250, 256), jnp.float32)
        _s = jax.random.randint(jax.random.fold_in(_gk, 2), (100000,), 0, 6250, jnp.int32)
        _d = jax.random.randint(jax.random.fold_in(_gk, 3), (100000,), 0, 6250, jnp.int32)
        _loop = jnp.arange(6250, dtype=jnp.int32)
        src = jnp.concatenate([_s, _d, _loop])
        dst = jnp.concatenate([_d, _s, _loop])
        _o = jnp.argsort(dst, stable=True)
        src = src[_o]
        dst = dst[_o]
        edge_type_16 = jax.random.randint(jax.random.fold_in(_gk, 12), (206250,), 0, 16, jnp.int32)
        return (x, src, dst, edge_type_16)
    x, src, dst, edge_type_16 = _rec_inputs()

    def _L0_gnn_setup():
        import jax, jax.numpy as jnp
        import numpy as np
        NUM_NODES = 6250
        NUM_RELATIONS = 16
        HIDDEN_DIM = 256
        NUM_EDGES = 100000
        key = jax.random.key(seed)
        k_x, k_ei, k_et, k_wr, k_ws, k_b = jax.random.split(key, 6)
        x = jax.random.normal(k_x, (NUM_NODES, HIDDEN_DIM), dtype=jnp.float32)
        edge_index = jax.random.randint(k_ei, (2, NUM_EDGES), 0, NUM_NODES, dtype=jnp.int64)
        edge_type = jax.random.randint(k_et, (NUM_EDGES,), 0, NUM_RELATIONS, dtype=jnp.int64)
        lim = float(np.sqrt(6.0 / (HIDDEN_DIM + HIDDEN_DIM)))
        W_rel = jax.random.uniform(k_wr, (NUM_RELATIONS, HIDDEN_DIM, HIDDEN_DIM), minval=-lim, maxval=lim, dtype=jnp.float32)
        W_self = jax.random.uniform(k_ws, (HIDDEN_DIM, HIDDEN_DIM), minval=-lim, maxval=lim, dtype=jnp.float32)
        bias = jnp.zeros((HIDDEN_DIM,), dtype=jnp.float32)
        return {'x': x, 'edge_index': edge_index, 'edge_type': edge_type, 'W_rel': W_rel, 'W_self': W_self, 'bias': bias}
    _L0_gnn_all = _L0_gnn_setup()
    _L0_gnn_in = {k: v for k, v in _L0_gnn_all.items() if k in ('W_rel', 'W_self', 'bias')}
    del _L0_gnn_all

    def _L0_mix_setup():
        import math
        import jax, jax.numpy as jnp
        import numpy as np
        EPS_DIV = 1e-07
        EPS_NORM = 1e-12

        def _l2_normalize(x, axis):
            n = jnp.sqrt(jnp.sum(x * x, axis=axis, keepdims=True))
            return x / jnp.maximum(n, EPS_NORM)
        key = jax.random.key(seed)
        ks = jax.random.split(key, 5)
        b, N, C = (8, 512, 256)
        x = jax.random.normal(ks[0], (b, N, C), dtype=jnp.float32)
        W_qkv = jax.random.normal(ks[1], (C, 3 * C), dtype=jnp.float32) * (1.0 / math.sqrt(C))
        b_qkv = jax.random.normal(ks[2], (3 * C,), dtype=jnp.float32) * 0.02
        W_out = jax.random.normal(ks[3], (C, C), dtype=jnp.float32) * (1.0 / math.sqrt(C))
        b_out = jax.random.normal(ks[4], (C,), dtype=jnp.float32) * 0.02
        return {'x': x, 'W_qkv': W_qkv, 'b_qkv': b_qkv, 'W_out': W_out, 'b_out': b_out}
    _L0_mix_all = _L0_mix_setup()
    _L0_mix_in = {k: v for k, v in _L0_mix_all.items() if k in ('W_qkv', 'b_qkv', 'W_out', 'b_out')}
    del _L0_mix_all

    def _L0_ffn_setup():
        import jax, jax.numpy as jnp
        import numpy as np
        B, A = (512, 8)
        IN, OUT = (256, 256)
        SH1, SH2 = (256, 128)
        EH1, EH2 = (128, 64)
        E, TOPK = (4, 2)

        def _shared_mlp(x, W1, b1, W2, b2, W3, b3):
            h = jax.nn.relu(x @ W1 + b1)
            h = jax.nn.relu(h @ W2 + b2)
            return h @ W3 + b3

        def _experts_mlp(x, eW1, eb1, eW2, eb2, eW3, eb3):
            h = jax.nn.relu(jnp.einsum('baf,efh->ebah', x, eW1) + eb1[:, None, None, :])
            h = jax.nn.relu(jnp.einsum('ebah,ehg->ebag', h, eW2) + eb2[:, None, None, :])
            o = jnp.einsum('ebag,ego->ebao', h, eW3) + eb3[:, None, None, :]
            return jnp.moveaxis(o, 0, -1)
        key = jax.random.key(seed)
        ks = jax.random.split(key, 16)
        s = 0.05
        return {'x': jax.random.normal(ks[0], (B, A, IN), jnp.float32), 'sW1': jax.random.normal(ks[1], (IN, SH1), jnp.float32) * s, 'sb1': jnp.zeros((SH1,), jnp.float32), 'sW2': jax.random.normal(ks[2], (SH1, SH2), jnp.float32) * s, 'sb2': jnp.zeros((SH2,), jnp.float32), 'sW3': jax.random.normal(ks[3], (SH2, OUT), jnp.float32) * s, 'sb3': jnp.zeros((OUT,), jnp.float32), 'eW1': jax.random.normal(ks[4], (E, IN, EH1), jnp.float32) * s, 'eb1': jnp.zeros((E, EH1), jnp.float32), 'eW2': jax.random.normal(ks[5], (E, EH1, EH2), jnp.float32) * s, 'eb2': jnp.zeros((E, EH2), jnp.float32), 'eW3': jax.random.normal(ks[6], (E, EH2, OUT), jnp.float32) * s, 'eb3': jnp.zeros((E, OUT), jnp.float32), 'gW': jax.random.normal(ks[7], (IN, E), jnp.float32) * s, 'gb': jnp.zeros((E,), jnp.float32)}
    _L0_ffn_all = _L0_ffn_setup()
    _L0_ffn_in = {k: v for k, v in _L0_ffn_all.items() if k in ('sW1', 'sb1', 'sW2', 'sb2', 'sW3', 'sb3', 'eW1', 'eb1', 'eW2', 'eb2', 'eW3', 'eb3', 'gW', 'gb')}
    del _L0_ffn_all
    return {'x': x, 'src': src, 'dst': dst, 'edge_type_16': edge_type_16, 'L0_gnn_W_rel': _L0_gnn_in['W_rel'], 'L0_gnn_W_self': _L0_gnn_in['W_self'], 'L0_gnn_bias': _L0_gnn_in['bias'], 'L0_mix_W_qkv': _L0_mix_in['W_qkv'], 'L0_mix_b_qkv': _L0_mix_in['b_qkv'], 'L0_mix_W_out': _L0_mix_in['W_out'], 'L0_mix_b_out': _L0_mix_in['b_out'], 'L0_ffn_sW1': _L0_ffn_in['sW1'], 'L0_ffn_sb1': _L0_ffn_in['sb1'], 'L0_ffn_sW2': _L0_ffn_in['sW2'], 'L0_ffn_sb2': _L0_ffn_in['sb2'], 'L0_ffn_sW3': _L0_ffn_in['sW3'], 'L0_ffn_sb3': _L0_ffn_in['sb3'], 'L0_ffn_eW1': _L0_ffn_in['eW1'], 'L0_ffn_eb1': _L0_ffn_in['eb1'], 'L0_ffn_eW2': _L0_ffn_in['eW2'], 'L0_ffn_eb2': _L0_ffn_in['eb2'], 'L0_ffn_eW3': _L0_ffn_in['eW3'], 'L0_ffn_eb3': _L0_ffn_in['eb3'], 'L0_ffn_gW': _L0_ffn_in['gW'], 'L0_ffn_gb': _L0_ffn_in['gb']}

def reference(x, src, dst, edge_type_16, L0_gnn_W_rel, L0_gnn_W_self, L0_gnn_bias, L0_mix_W_qkv, L0_mix_b_qkv, L0_mix_W_out, L0_mix_b_out, L0_ffn_sW1, L0_ffn_sb1, L0_ffn_sW2, L0_ffn_sb2, L0_ffn_sW3, L0_ffn_sb3, L0_ffn_eW1, L0_ffn_eb1, L0_ffn_eW2, L0_ffn_eb2, L0_ffn_eW3, L0_ffn_eb3, L0_ffn_gW, L0_ffn_gb):
    import jax
    import jax.numpy as jnp

    def _L0_gnn_ref(x, edge_index, edge_type, W_rel, W_self, bias):
        import jax, jax.numpy as jnp
        import numpy as np
        NUM_NODES = 6250
        NUM_RELATIONS = 16
        HIDDEN_DIM = 256
        NUM_EDGES = 100000
        xw = jnp.einsum('nd,rdh->nrh', x, W_rel)
        src = edge_index[0]
        dst = edge_index[1]
        messages = xw[src, edge_type]
        agg = jax.ops.segment_sum(messages, dst, num_segments=NUM_NODES)
        out = agg + x @ W_self + bias
        return jax.nn.relu(out)

    def _L0_mix_ref(x, W_qkv, b_qkv, W_out, b_out):
        import math
        import jax, jax.numpy as jnp
        import numpy as np
        EPS_DIV = 1e-07
        EPS_NORM = 1e-12

        def _l2_normalize(x, axis):
            n = jnp.sqrt(jnp.sum(x * x, axis=axis, keepdims=True))
            return x / jnp.maximum(n, EPS_NORM)
        b, N, C = x.shape
        qkv = x @ W_qkv + b_qkv
        q, k, v = jnp.split(qkv, 3, axis=2)
        q = q - jnp.mean(q, axis=2, keepdims=True)
        k = k - jnp.mean(k, axis=2, keepdims=True)
        q2 = q * q
        k2 = k * k
        q2s = jnp.sum(q2, axis=2, keepdims=True)
        k2s = jnp.sum(k2, axis=2, keepdims=True)
        k2 = _l2_normalize(k2 / (k2s + EPS_DIV), axis=-2)
        q2 = _l2_normalize(q2 / (q2s + EPS_DIV), axis=-1)
        kv = jnp.einsum('bnc,bnd->bcd', k2, v)
        t2 = jnp.einsum('bnc,bcd->bnd', q2, kv) / math.sqrt(N)
        attn = v + t2
        return attn @ W_out + b_out

    def _L0_ffn_ref(x, sW1, sb1, sW2, sb2, sW3, sb3, eW1, eb1, eW2, eb2, eW3, eb3, gW, gb):
        import jax, jax.numpy as jnp
        import numpy as np
        B, A = (512, 8)
        IN, OUT = (256, 256)
        SH1, SH2 = (256, 128)
        EH1, EH2 = (128, 64)
        E, TOPK = (4, 2)

        def _shared_mlp(x, W1, b1, W2, b2, W3, b3):
            h = jax.nn.relu(x @ W1 + b1)
            h = jax.nn.relu(h @ W2 + b2)
            return h @ W3 + b3

        def _experts_mlp(x, eW1, eb1, eW2, eb2, eW3, eb3):
            h = jax.nn.relu(jnp.einsum('baf,efh->ebah', x, eW1) + eb1[:, None, None, :])
            h = jax.nn.relu(jnp.einsum('ebah,ehg->ebag', h, eW2) + eb2[:, None, None, :])
            o = jnp.einsum('ebag,ego->ebao', h, eW3) + eb3[:, None, None, :]
            return jnp.moveaxis(o, 0, -1)
        all_out = _experts_mlp(x, eW1, eb1, eW2, eb2, eW3, eb3)
        shared = _shared_mlp(x, sW1, sb1, sW2, sb2, sW3, sb3)
        gates = jax.nn.softmax(x @ gW + gb, axis=-1)
        topv, topi = jax.lax.top_k(gates, TOPK)
        topw = jax.nn.softmax(topv, axis=-1)
        sel = jnp.take_along_axis(all_out, topi[:, :, None, :], axis=-1)
        gated = jnp.sum(sel * topw[:, :, None, :], axis=-1)
        return shared + gated
    edge_index = jnp.stack([src, dst])
    xn = _layernorm(x, axis=-1)
    x = x + _L0_gnn_ref(xn, edge_index, edge_type_16, L0_gnn_W_rel, L0_gnn_W_self, L0_gnn_bias) + _L0_mix_ref(xn[None], L0_mix_W_qkv, L0_mix_b_qkv, L0_mix_W_out, L0_mix_b_out)[0]
    x = x + _L0_ffn_ref(_layernorm(x, axis=-1)[None], L0_ffn_sW1, L0_ffn_sb1, L0_ffn_sW2, L0_ffn_sb2, L0_ffn_sW3, L0_ffn_sb3, L0_ffn_eW1, L0_ffn_eb1, L0_ffn_eW2, L0_ffn_eb2, L0_ffn_eW3, L0_ffn_eb3, L0_ffn_gW, L0_ffn_gb)[0]
    return x

_drawn_inputs = setup_inputs


def setup_inputs(seed=0):
    import zlib

    import numpy as np

    out = dict(_drawn_inputs(seed))
    spreads = {'L0_gnn_bias': (0.0, 0.491),
     'L0_ffn_sb1': (0.0, 2.0),
     'L0_ffn_sb2': (0.0, 0.8),
     'L0_ffn_sb3': (0.0, 0.367),
     'L0_ffn_eb1': (0.0, 0.8),
     'L0_ffn_eb2': (0.0, 0.8),
     'L0_ffn_eb3': (0.0, 0.516),
     'L0_ffn_gb': (0.0, 0.8)}
    factors = {'L0_mix_b_out': 8.0,
     'L0_ffn_eW1': 5.64,
     'L0_ffn_eW2': 4.906,
     'L0_ffn_eW3': 3.939,
     'L0_ffn_gW': 3.75,
     'L0_ffn_sW1': 3.101}
    for name, (base, spread) in spreads.items():
        noise = np.random.default_rng([zlib.crc32(name.encode()), seed]).standard_normal(out[name].shape)
        drawn = base * np.exp(spread * noise) if base else spread * noise
        out[name] = jnp.asarray(drawn.astype(out[name].dtype))
    for name, factor in factors.items():
        out[name] = (out[name] * factor).astype(out[name].dtype)
    return out
```

```python
from contextlib import ExitStack
from math import ceil, floor, sqrt

import numpy as np
import concourse.bass as bass
from concourse import mybir
from concourse.alu_op_type import AluOpType as ALU

F32 = mybir.dt.float32
F16 = mybir.dt.float16
I32 = mybir.dt.int32
ACT = mybir.ActivationFunctionType
AX = mybir.AxisListType

P = 128
D = 256
H = D // P
R = 16
N = 6250
E = 206250
T = -(-N // P)
TAIL = N - (T - 1) * P
NP = T * P
GN = 64
GT = P // GN
NG = T * GT
PAIRS = GN * R
DEG = E / N
BLOCKS = 18
CAP = BLOCKS * P
TB = GT * BLOCKS
BANK_N = 32
ROWS, ROW = 125, E // 125
EPAD = E + CAP
PADDST = 8191
SCALE = 64.0
EPS_LN, EPS_DIV, EPS_NORM = 1e-5, 1e-7, 1e-12
Z = 4.3
CH = 7
NEB = -(-E // P)
MS = 3
L1 = 1 + -(-(T - 1) // MS)
PS = 3
J2 = (T - L1) // 2
EX, EH1, EH2 = 4, 128, 64
BIAS = 4 * D + EX
POST_C = 16 + P * H + 1 + P
RB = 6
OH = 12
U_AT = 2
AHEAD = 8
MSLOT = TB // MS
PSLOT = 2 * TB // PS


def windows():
    out = []
    for b in range(BLOCKS):
        lo = floor(P * b / DEG - Z * sqrt((DEG - 1) * P * b / DEG) / DEG)
        hi = ceil(P * (b + 1) / DEG + Z * sqrt((DEG - 1) * P * (b + 1) / DEG) / DEG) + 1
        if b < 2 * (GN // 8):
            lo, hi = min(lo, 8 * (b // 2)), max(hi, 8 * (b // 2) + 8)
        out.append((max(lo, 0), min(hi, GN)))
    return out


WIN = windows()
WMAX = max(hi - lo for lo, hi in WIN) * R
LAST0 = max(b for b, (lo, hi) in enumerate(WIN) if lo < BANK_N)
FIRST1 = min(b for b, (lo, hi) in enumerate(WIN) if hi > BANK_N)


def build(nc, x, src, dst, etype, w_rel, w_self, g_bias, w_qkv, b_qkv, w_out, b_out, s_w1, s_b1,
          s_w2, s_b2, s_w3, s_b3, e_w1, e_b1, e_w2, e_b2, e_w3, e_b3, g_w, g_b,
          c_ident, c_iota, c_group, c_post, out):
    ctx = ExitStack()
    with ctx:
        def sb(name, shape, dt=F32):
            return ctx.enter_context(nc.sbuf_tensor(name, shape, dt))

        def sem(name):
            return ctx.enter_context(nc.semaphore(name))

        table = nc.dram_tensor("table", (NP, 2 * D), F16).ap()
        sums_t = nc.dram_tensor("sums_t", (2 * NG * PAIRS, 2 * D), F16).ap()
        sums_d = nc.dram_tensor("sums_d", (NG * PAIRS, D), F32).ap()
        xn_d = nc.dram_tensor("xn_d", (NP, D), F32).ap()
        xnt_d = nc.dram_tensor("xnt_d", (T, P, D), F32).ap()
        q2nt_d = nc.dram_tensor("q2nt_d", (T, P, D), F32).ap()
        u_d = nc.dram_tensor("u_d", (T, P, D), F32).ap()
        src_p = nc.dram_tensor("src_p", (EPAD,), I32).ap()
        dst_p = nc.dram_tensor("dst_p", (EPAD,), I32).ap()
        typ_p = nc.dram_tensor("typ_p", (EPAD,), I32).ap()

        ident = sb("ident", [P, P])
        iota16 = sb("iota16", [P, PAIRS], F16)
        group_c = sb("group_c", [P, 2 * BLOCKS + 1])
        post_c = sb("post_c", [P, POST_C])
        ones = sb("ones", [P, P])
        zeros = sb("zeros", [P, 512])
        eps_ln = sb("eps_ln", [P, 1])
        wr = sb("wr", [P, 3, H, R, D], F16)
        wown = sb("wown", [P, H, 2 * D])
        wvo = wown[:, :, 0:D]
        wkq = sb("wkq", [P, H, 2 * D])
        m1 = sb("m1", [P, H, D])
        sw1 = sb("sw1", [P, H, D])
        ew1 = sb("ew1", [P, H, EX, EH1])
        sw2 = sb("sw2", [P, H, P])
        ew2 = sb("ew2", [P, EX, EH2])
        sw3 = sb("sw3", [P, D])
        ew3 = sb("ew3", [P, H, D])
        gw = sb("gw", [P, H, EX])
        bias_row = sb("bias_row", [1, BIAS])
        bias_left = sb("bias_left", [1, BIAS])
        bias_part = sb("bias_part", [1, 3, BIAS], F16)
        bias16 = sb("bias16", [3, BIAS], F16)
        ones16 = sb("ones16", [3, P], F16)
        b3 = sb("b3", [EX + 1, D])
        b1_col = sb("b1_col", [P, H + EX])
        b2_col = sb("b2_col", [P, 1 + H])

        idx_t = sb("idx_t", [P, NG, BLOCKS], I32)
        key_t = sb("key_t", [P, NG + GT, BLOCKS])
        hot_v = sb("hot_v", [P, BLOCKS])
        idx_now = sb("idx_now", [P, TB], I32)
        key_now = sb("key_now", [P, TB])
        ring = sb("ring", [P, TB, 2 * D], F16)
        hot = sb("hot", [P, OH, WMAX], F16)
        s_hi = sb("s_hi", [P, H, R, P], F16)
        s_lo = sb("s_lo", [P, H, R, P], F16)
        xnt_g = sb("xnt_g", [P, H, P])
        x_g = sb("x_g", [P, D])
        u_g = sb("u_g", [P, D])

        work = sb("work", [P, 20, D])
        (xn_m, xnt_m, k2, k2n, k4, q2, q4, q2n, q2nt, k2n_sum, k4_sum) = (work[:, j, :] for j in range(11))
        (u_p, q2nt_p, x1, xn2, xn2t, h2, h2g, o_p) = (work[:, j, :] for j in range(8))
        h1 = work[:, 12:15, :].rearrange("p a (b n) -> p (a b) n", n=P)
        h2s = work[:, 15, 0:P]
        stat = sb("stat", [P, 32])
        gate = sb("gate", [P, 96])
        w5t = sb("w5t", [EX + 1, P])

        ring_f = ring[:, :, :].rearrange("p a b -> p (a b)").bitcast(F32)
        xc = ring_f[:, 0:CH * D].rearrange("p (a b) -> p a b", b=D)
        xnc = ring_f[:, CH * D:2 * CH * D].rearrange("p (a b) -> p a b", b=D)
        tabc = ring[:, :, :].rearrange("p a b -> p (a b)")[:, 4 * CH * D:6 * CH * D]\
            .rearrange("p (a b) -> p a b", b=2 * D)
        rows = ring_f[0:ROWS, 3 * CH * D:3 * CH * D + ROW].bitcast(I32)
        nxt = ring_f[0:ROWS, 3 * CH * D + ROW:3 * CH * D + 2 * ROW].bitcast(I32)
        wr_f = wr[:, :, :, :, :].rearrange("p a b c d -> p (a b c d)").bitcast(F32)
        src_g, dst_g, typ_g = (wr_f[0:NG, j * CAP:(j + 1) * CAP].bitcast(I32) for j in range(3))
        key_g, srcf_g = (wr_f[0:NG, j * CAP:(j + 1) * CAP] for j in (3, 4))
        s_f = s_hi[:, :, :, :].rearrange("p a b c -> p (a b c)").bitcast(F32)
        wstage = s_f.rearrange("p (a d) -> p a d", d=D)
        pad_t = sb("pad_t", [BLOCKS, 2 * P], I32)
        st = sb("st", [P, CH, 6])
        mv = sb("mv", [P, CH, 2])
        rstd = sb("rstd", [P, CH])
        ec = sb("ec", [P, 8])
        ei = sb("ei", [P, 2], I32)
        rfb = sb("rfb", [ROWS, NG])
        bad = sb("bad", [P, 4])
        wv_s = work[:, 0:2, :]
        wvt_s = work[:, 2:4, :]
        wo_s = work[:, 4:6, :]
        wq_s = work[:, 6:12, :].rearrange("p (h c) d -> p h (c d)", h=H)
        bv_col = sb("bv_col", [P, H])
        bvb = sb("bvb", [P, H, P])
        bvo_b = sb("bvo_b", [P, D])
        pcol = sb("pcol", [P, 8])
        carrier = sb("carrier", [P, 1])
        flag = sb("flag", [1, 1], I32)
        flag_f = sb("flag_f", [1, 1])

        gp_i = sb("gp_i", [P, 5], I32)
        gp_f = sb("gp_f", [P, 3])
        gp_rows = ring[:, 0, :]
        gp_was, gp_new = ring_f[:, D:2 * D], ring_f[:, 2 * D:3 * D]
        gp_same = ring[:, 3, 0:P]
        gp_earlier = ring_f[:, 4 * D:4 * D + P]
        gp_keys = ring_f[:, 4 * D + P:5 * D]
        gp_parts = ring[:, 6:8, :]
        gp_left = ring_f[:, 8 * D:9 * D]

        banks = [ctx.enter_context(nc.psum_tensor(f"bank{i}", [P, 512], F32)) for i in range(8)]
        GB = banks[4]
        B5, B6, B7 = banks[5:8]

        names = """consts_in x_in weights_in bias_in rel_in pad_made pads_in edges_pad rows_in next_in
            ln_done sd_ready xn_ready hi_ready lo_ready xn_out tab_out
            rf_ready rf_wide row_ready row_got start_ready edges_got edges_kf srcf_ready
            turned turned_k turned_s prep_dve prep_act rel_lo mixw_pe
            idx_ready keys_ready hot_ready blocks_used hi_done lo_done w_done xg_in u_half u_ready u_out
            bias_parts batches bad_ready flag_sum flag_ready gp_clear gp_in0 gp_in1 gp_in2 gp_key gp_wide gp_made gp_got gp_sum gp_new gp_out
            gp_row_in gp_row_made gp_row_out gp_done dve_g m_qtc m_q_out m_qt m_q2 m_q4 m_nb m_q2n m_sum m_in m_turned m_xnt m_xnt_out m_k m_k2 m_k2n m_k4 m_used m_all
            mix_dve mix_act mix_pe
            p_in p_q p_q2 p_q4 p_nb p_sd p_q2n p_qt p_qtc p_mix p_x1 p_ln p_xn2 p_xt p_xtc p_log p_h1s p_h1e p_h1 p_max p_exp
            p_gmax p_exp2 p_w5 p_wt p_wtc p_wb p_l2 p_h2 p_h2g p_l3 p_out out_done
            dve_c dve_c2 dve_p dve_m act_c""".split()
        s = {n: sem(n) for n in names}
        got = [sem(f"got{i}") for i in range(TB // RB)]

        block = ctx.enter_context(nc.Block())

        def chunk_rows(c):
            return slice(c * CH * P, (c + 1) * CH * P)

        NC_P = T // CH

        @block.sync
        def _(sp):
            sp.dma_start(ident[:, :], c_ident).then_inc(s["consts_in"], 16)
            sp.dma_start(iota16[:, :], c_iota).then_inc(s["consts_in"], 16)
            sp.dma_start(group_c[:, :], c_group).then_inc(s["consts_in"], 16)
            sp.dma_start(post_c[:, :], c_post).then_inc(s["consts_in"], 16)
            sp.dma_start(rows, dst.rearrange("(r c) -> r c", c=ROW)).then_inc(s["rows_in"], 16)
            for full, own in ((dst_p, dst), (src_p, src), (typ_p, etype)):
                sp.dma_start(full[0:E].rearrange("(r c) -> r c", c=ROW),
                             own.rearrange("(r c) -> r c", c=ROW)).then_inc(s["edges_pad"], 16)
            sp.wait_ge(s["pad_made"], 1)
            for k, full in enumerate((dst_p, src_p, typ_p)):
                sp.dma_start(full[E:EPAD].rearrange("(r c) -> r c", c=P),
                             pad_t[:, P * min(k, 1):P * min(k, 1) + P]).then_inc(s["edges_pad"], 16)
            sp.wait_ge(s["edges_pad"], 96)
            sp.dma_start(nxt, dst_p[1:E + 1].rearrange("(r c) -> r c", c=ROW)).then_inc(s["next_in"], 16)

            def ln_in(c):
                if not isinstance(c, int) or c:
                    sp.wait_ge(s["xn_ready"], c)
                if isinstance(c, int) and c == NC_P - 1:
                    sp.dma_start(xc[:, 0:CH - 1, :], x[c * CH * P:(T - 1) * P, :]
                                 .rearrange("(j p) d -> p j d", p=P)).then_inc(s["x_in"], 16)
                    sp.wait_ge(s["pad_made"], 2)
                    sp.dma_start(xc[0:TAIL, CH - 1, :], x[(T - 1) * P:N, :]).then_inc(s["x_in"], 16)
                else:
                    sp.dma_start(xc, x[bass.ds(c * (CH * P), CH * P), :]
                                 .rearrange("(j p) d -> p j d", p=P)).then_inc(s["x_in"], 16)

            def ln_out(c):
                sp.wait_ge(s["xn_ready"], c + 1)
                sp.dma_start(xn_d[bass.ds(c * (CH * P), CH * P), :].rearrange("(j p) d -> p j d", p=P),
                             xnc).then_inc(s["xn_out"], 16)
                sp.wait_ge(s["lo_ready"], c + 1)
                sp.wait_ge(s["hi_ready"], c + 1)
                sp.dma_start(table[bass.ds(c * (CH * P), CH * P), :].rearrange("(j p) d -> p j d", p=P),
                             tabc).then_inc(s["tab_out"], 16)

            ln_in(0)
            with sp.Fori(0, NC_P - 2) as c:
                ln_in(c + 1)
                ln_out(c)
            ln_in(NC_P - 1)
            ln_out(NC_P - 2)
            ln_out(NC_P - 1)

            def m_load(m):
                if not isinstance(m, int) or m:
                    sp.wait_ge(s["m_used"], m)
                sp.dma_start(xn_m, xn_d[bass.ds(m * P, P), :]).then_inc(s["m_in"], 16)

            def m_store(m):
                sp.wait_ge(s["m_xnt"], m + 1)
                sp.dma_start(xnt_d[bass.ds(m, 1), :, :].rearrange("o p d -> (o p) d"), xnt_m)\
                  .then_inc(s["m_xnt_out"], 16)

            def m_store_q(m):
                sp.wait_ge(s["m_qtc"], m + 1)
                sp.dma_start(q2nt_d[bass.ds(m, 1), :, :].rearrange("o p d -> (o p) d"), q2nt)\
                  .then_inc(s["m_q_out"], 16)

            def g_load(t, m_now):
                sp.wait_ge(s["m_xnt_out"], m_now * 16)
                if not isinstance(t, int) or t:
                    sp.wait_ge(s["u_ready"], t)
                sp.dma_start(xnt_g[:, :, :].rearrange("p h n -> p (h n)"),
                             xnt_d[bass.ds(t, 1), :, :].rearrange("o p d -> (o p) d"))\
                  .then_inc(s["xg_in"], 16)
                if isinstance(t, int) and t == T - 1:
                    sp.dma_start(x_g[0:TAIL, :], x[(T - 1) * P:N, :]).then_inc(s["xg_in"], 16)
                else:
                    sp.dma_start(x_g[:, :], x[bass.ds(t * P, P), :]).then_inc(s["xg_in"], 16)

            def g_store(t):
                sp.wait_ge(s["u_ready"], t + 1)
                sp.dma_start(u_d[bass.ds(t, 1), :, :].rearrange("o p d -> (o p) d"), u_g[:, :])\
                  .then_inc(s["u_out"], 16)

            for dram, tile in ((w_self, wown[:, :, D:2 * D]), (s_w1, sw1[:, :, :]), (s_w2, sw2[:, :, :]),
                               (g_w, gw[:, :, :])):
                sp.dma_start(tile, dram.rearrange("(h p) c -> p h c", p=P))\
                  .then_inc(s["weights_in"], 16)
            for h in range(H):
                sp.dma_start(ew1[:, h, :, :], e_w1[:, h * P:(h + 1) * P, :].rearrange("e p c -> p e c"))\
                  .then_inc(s["weights_in"], 16)
            sp.dma_start(ew2[:, :, :], e_w2.rearrange("e p c -> p e c")).then_inc(s["weights_in"], 16)
            sp.dma_start(sw3[:, :], s_w3).then_inc(s["weights_in"], 16)
            sp.dma_start(ew3[:, :, :], e_w3.rearrange("(h a) p c -> (a p) h c", h=H)
                         if False else e_w3.rearrange("e p c -> (e p) c").rearrange("(h q) c -> q h c", h=H))\
              .then_inc(s["weights_in"], 16)
            sp.wait_ge(s["prep_dve"], 1)
            sp.dma_start(wq_s, w_qkv.rearrange("(h p) c -> p h c", p=P)).then_inc(s["weights_in"], 16)
            sp.dma_start(wo_s, w_out.rearrange("(h p) c -> p h c", p=P)).then_inc(s["weights_in"], 16)
            RH = R // 2
            for k in range(4):
                h, r0 = k // 2, (k % 2) * RH
                if k >= 1:
                    sp.wait_ge(s["rel_lo"], k)
                sp.dma_start(wstage[:, 0:RH, :], w_rel[r0:r0 + RH, h * P:(h + 1) * P, :]
                             .rearrange("r p c -> p r c")).then_inc(s["rel_in"], 16)

            sp.wait_ge(s["mix_dve"], 1)
            for k in range(3):
                sp.dma_start(bias16[k:k + 1, :], bias_part[0:1, k, :]).then_inc(s["bias_parts"], 16)
            sp.wait_ge(s["xn_out"], NC_P * 16)
            sp.wait_ge(s["mixw_pe"], 3)

            def sp_g_and_m(t):
                m = MS * t - 2
                m_store(m)
                m_load(m + 1)
                m_store_q(m)
                m_store(m + 1)
                g_load(t, m + 2)
                m_load(m + 2)
                m_store_q(m + 1)
                m_store(m + 2)
                if not isinstance(t, int) or t < L1 - 1:
                    m_load(m + 3)
                m_store_q(m + 2)
                g_store(t)

            m_load(0)
            m_store(0)
            g_load(0, 1)
            m_load(1)
            m_store_q(0)
            g_store(0)
            with sp.Fori(1, L1 - 1) as i:
                sp_g_and_m(i)
            sp_g_and_m(L1 - 1)

            def p_load(p, stored):
                if not isinstance(p, int) or p:
                    sp.wait_ge(s["p_x1"], p)
                sp.dma_start(q2nt_p, q2nt_d[bass.ds(p, 1), :, :].rearrange("o p d -> (o p) d"))\
                  .then_inc(s["p_in"], 16)
                sp.wait_ge(s["u_out"], stored * 16)
                sp.dma_start(u_p, u_d[bass.ds(p, 1), :, :].rearrange("o p d -> (o p) d"))\
                  .then_inc(s["p_in"], 16)

            def p_store(p):
                sp.wait_ge(s["p_out"], p + 1)
                if isinstance(p, int) and p == T - 1:
                    sp.dma_start(out[(T - 1) * P:N, :], o_p[0:TAIL, :]).then_inc(s["out_done"], 16)
                else:
                    sp.dma_start(out[bass.ds(p * P, P), :], o_p).then_inc(s["out_done"], 16)

            sp.wait_ge(s["mix_dve"], 5)
            sp.wait_ge(s["m_q_out"], T * 16)

            def sp_g_and_p(j):
                t, p = 2 * j + L1, PS * j
                g_load(t, T)
                p_load(p + 1, t)
                p_store(p)
                g_store(t)
                g_load(t + 1, T)
                p_load(p + 2, t + 1)
                p_store(p + 1)
                if not isinstance(j, int) or j < J2 - 1:
                    p_load(p + 3, t + 1)
                p_store(p + 2)
                g_store(t + 1)

            p_load(0, L1)
            sp_g_and_p(0)
            with sp.Fori(1, J2 - 1) as j:
                sp_g_and_p(j)
            sp_g_and_p(J2 - 1)
            p_load(T - 1, T)
            p_store(T - 1)
            sp.wait_ge(s["out_done"], T * 16)
            sp.wait_ge(s["tab_out"], NC_P * 16)

        @block.gpsimd
        def _(pool):
            pool.memset(pad_t[:, 0:P], PADDST)
            pool.memset(pad_t[:, P:2 * P], 0).then_inc(s["pad_made"], 1)
            pool.memset(ones[:, :], 1.0).then_inc(s["idx_ready"], 1)
            pool.memset(zeros[:, :], 0.0).then_inc(s["idx_ready"], 1)
            pool.memset(hot_v[:, :], 1.0).then_inc(s["idx_ready"], 1)
            pool.memset(bad[:, :], 0.0).then_inc(s["idx_ready"], 1)
            pool.memset(gate[:, :], 1.0).then_inc(s["idx_ready"], 1)
            pool.memset(eps_ln[:, :], EPS_LN).then_inc(s["idx_ready"], 1)

            pool.wait_ge(s["row_ready"], 1)
            pool.indirect_dma_start(nxt_g := key_g[:, 0:ROW].bitcast(I32), None,
                                    dst.rearrange("(r c) -> r c", c=ROW),
                                    bass.IndirectOffsetOnAxis(ap=ei[0:NG, 0:1], axis=0),
                                    bounds_check=ROWS - 1, oob_is_err=False).then_inc(s["row_got"], 16)
            pool.wait_ge(s["start_ready"], 1)
            for full, own in ((dst_p, dst_g), (src_p, src_g), (typ_p, typ_g)):
                pool.indirect_dma_start(own, None,
                                        full[0:(EPAD // CAP) * CAP].rearrange("(r c) -> r c", c=CAP),
                                        bass.IndirectOffsetOnAxis(ap=ei[0:NG, 1:2], axis=1),
                                        bounds_check=E, oob_is_err=False).then_inc(s["edges_got"], 16)
            pool.wait_ge(s["turned_s"], 5)
            pool.wait_ge(s["tab_out"], NC_P * 16)

            def gather(t, own):
                for g in range(GT):
                    if not isinstance(t, int) or t:
                        for r in range(g * BLOCKS // RB, (g + 1) * BLOCKS // RB):
                            pool.wait_ge(got[r], t * (RB * 16))
                    pool.tensor_copy(idx_now[:, g * BLOCKS:(g + 1) * BLOCKS],
                                     idx_t[:, bass.ds(GT * t + g, 1), :].rearrange("p o b -> p (o b)"))\
                        .then_inc(s["idx_ready"], 1)
                    pool.wait_ge(s["idx_ready"], GT * t + g + 7)
                    for b in range(g * BLOCKS, (g + 1) * BLOCKS):
                        if b % RB == 0:
                            if not isinstance(t, int) or t:
                                pool.wait_ge(s["blocks_used"], (t - 1) * TB + b + RB)
                                pool.sem_inc(s["batches"], 1)
                        pool.indirect_dma_start(ring[:, b, :], None, own,
                                                bass.IndirectOffsetOnAxis(ap=idx_now[:, b:b + 1], axis=0),
                                                bounds_check=own.shape[0] - 1, oob_is_err=False)\
                            .then_inc(got[b // RB], 16)

            pool.wait_ge(s["flag_ready"], 1)
            general = pool.value_load(flag[0:1, 0:1])
            with pool.If(general > 0):
                with pool.Fori(0, NG * PAIRS // (2 * P)) as k:
                    pool.dma_start(sums_d[bass.ds(k * (2 * P), 2 * P), :].rearrange("(p a) d -> p (a d)", a=2),
                                   zeros[:, :]).then_inc(s["gp_clear"], 16)
                pool.wait_ge(s["gp_clear"], NG * PAIRS // (2 * P) * 16)
                with pool.Fori(0, NEB) as k:
                    for j, full in enumerate((src_p, dst_p, typ_p)):
                        pool.dma_start(gp_i[:, j:j + 1], full[bass.ds(k * P, P)].rearrange("(p a) -> p a", a=1))\
                            .then_inc(s[f"gp_in{j}"], 16)
                    pool.wait_ge(s["gp_key"], k + 1)
                    pool.sem_inc(s["batches"], 1)
                    pool.indirect_dma_start(gp_rows, None, table[:, :],
                                            bass.IndirectOffsetOnAxis(ap=gp_i[:, 0:1], axis=0),
                                            bounds_check=NP - 1, oob_is_err=False).then_inc(s["gp_got"], 16)
                    pool.indirect_dma_start(gp_was, None, sums_d[:, :],
                                            bass.IndirectOffsetOnAxis(ap=gp_i[:, 3:4], axis=0),
                                            bounds_check=NG * PAIRS - 1, oob_is_err=False).then_inc(s["gp_got"], 16)
                    pool.wait_ge(s["gp_new"], k + 1)
                    pool.sem_inc(s["batches"], 1)
                    pool.indirect_dma_start(sums_d[:, :], bass.IndirectOffsetOnAxis(ap=gp_i[:, 4:5], axis=0), gp_new,
                                            None, bounds_check=NG * PAIRS - 1, oob_is_err=False)\
                        .then_inc(s["gp_out"], 16)
                    pool.wait_ge(s["gp_out"], k * 16 + 16)
                    pool.sem_inc(s["batches"], 1)
                with pool.Fori(0, NG * PAIRS // P) as k:
                    pool.dma_start(gp_was, sums_d[bass.ds(k * P, P), :]).then_inc(s["gp_row_in"], 16)
                    pool.wait_ge(s["gp_row_made"], k + 1)
                    pool.sem_inc(s["batches"], 1)
                    pool.dma_start(sums_t[bass.ds(k * (2 * P), 2 * P), :].rearrange("(p a) d -> p a d", a=2),
                                   gp_parts).then_inc(s["gp_row_out"], 16)
                    pool.wait_ge(s["gp_row_out"], k * 16 + 16)
                    pool.sem_inc(s["batches"], 1)
                blocks8 = idx_t[:, :, 0:2 * (GN // 8)].rearrange("p g (c a) -> p g c a", a=2)
                pool.iota(blocks8, [[2 * PAIRS, NG], [2 * P, GN // 8], [1, 2]], base=0, channel_multiplier=2)
                pool.iota(key_t[:, 0:NG, 0:2 * (GN // 8)].rearrange("p g (c a) -> p g c a", a=2),
                          [[0, NG], [P, GN // 8], [0, 2]], base=0, channel_multiplier=1,
                          allow_small_or_imprecise_dtypes=True)
                pool.memset(idx_t[:, :, 2 * (GN // 8):BLOCKS], 0)
                pool.memset(key_t[:, 0:NG, 2 * (GN // 8):BLOCKS], -1.0)
                pool.memset(hot_v[:, 0:2 * (GN // 8):2], SCALE)
                pool.drain().then_inc(s["gp_done"], 1)
                pool.wait_ge(s["gp_done"], 1)

                gather(0, sums_t)
                with pool.Fori(1, T) as t:
                    gather(t, sums_t)
            with pool.If(general < 1):
                gather(0, table)
                with pool.Fori(1, T) as t:
                    gather(t, table)

        @block.scalar
        def _(act):
            for row, tile in ((b_qkv[D:2 * D], bias_row[0:1, 0:D]), (b_qkv[0:D], bias_row[0:1, D:2 * D]),
                              (b_out, bias_row[0:1, 2 * D:3 * D]), (g_bias, bias_row[0:1, 3 * D:4 * D]),
                              (g_b, bias_row[0:1, 4 * D:BIAS]), (s_b3, b3[EX:EX + 1, :])):
                act.dma_start(tile, row.rearrange("(a c) -> a c", a=1)).then_inc(s["bias_in"], 16)
            act.dma_start(b3[0:EX, :], e_b3).then_inc(s["bias_in"], 16)
            with nc.allow_non_contiguous_dma(reason="biases as columns"):
                for col, tile in ((s_b1.rearrange("(h p) -> p h", p=P), b1_col[:, 0:H]),
                                  (e_b1.rearrange("e p -> p e"), b1_col[:, H:H + EX]),
                                  (s_b2.rearrange("(a p) -> p a", p=P), b2_col[:, 0:1]),
                                  (e_b2.rearrange("e p -> (e p)").rearrange("(h q) -> q h", h=H), b2_col[:, 1:1 + H]),
                                  (b_qkv[2 * D:3 * D].rearrange("(h p) -> p h", p=P), bv_col[:, :])):
                    act.dma_start(tile, col).then_inc(s["bias_in"], 16)

            act.wait_ge(s["idx_ready"], 6)

            def ln_act(c):
                act.wait_ge(s["ln_done"], c + 1)
                act.activation(rstd[:, :], mv[:, :, 1], ACT.Sqrt, bias=eps_ln[:, 0:1]).then_inc(s["sd_ready"], 1)
                act.wait_ge(s["xn_ready"], c + 1)
                if not isinstance(c, int) or c:
                    act.wait_ge(s["tab_out"], c * 16)
                act.activation(tabc[:, :, 0:D], xnc, ACT.Copy).then_inc(s["hi_ready"], 1)

            ln_act(0)
            with act.Fori(1, NC_P) as c:
                ln_act(c)

            act.wait_ge(s["edges_got"], 48)
            act.activation(srcf_g, src_g, ACT.Copy).then_inc(s["srcf_ready"], 1)
            for k in range(5):
                act.wait_ge(s["turned"], 5 + k + 1)
                b0, nb = 4 * k, min(4, BLOCKS - 4 * k)
                bank = banks[(5 + k) % 8]
                act.activation(idx_t[:, :, b0:b0 + nb].rearrange("p g b -> p b g"),
                               bank[:, 0:nb * P].rearrange("p (b c) -> p b c", c=P)[:, :, 0:NG], ACT.Copy)\
                    .then_inc(s["turned_s"], 1)

            RH = R // 2
            for k in range(4):
                h, r0 = k // 2, (k % 2) * RH
                act.wait_ge(s["rel_in"], (k + 1) * 16)
                act.activation(wr[:, 0, h, r0:r0 + RH, :], wstage[:, 0:RH, :], ACT.Copy, scale=SCALE)\
                    .then_inc(s["prep_act"], 1)
                act.activation(wr[:, 2, h, r0:r0 + RH, :], wstage[:, 0:RH, :], ACT.Copy)\
                    .then_inc(s["prep_act"], 1)

            def hi_part(t, g, q):
                n0 = g * GN + q * BANK_N
                act.wait_ge(s["blocks_used"], t * TB + g * BLOCKS + (LAST0, BLOCKS - 1)[q] + 1)
                if g + q == 0 and (not isinstance(t, int) or t):
                    act.wait_ge(s["w_done"], t)
                for h in range(H):
                    act.activation(s_hi[:, h, :, n0:n0 + BANK_N].rearrange("p r n -> p n r"),
                                   banks[2 * q + h][:, :].rearrange("p (n r) -> p n r", r=R),
                                   ACT.Copy, scale=1.0 / SCALE).then_inc(s["hi_done"], 1)

            def m_act(m, step):
                later = not isinstance(m, int) or m > 0
                if step == "xt":
                    act.wait_ge(s["m_turned"], m + 1)
                    if later:
                        act.wait_ge(s["m_xnt_out"], m * 16)
                    act.activation(xnt_m, B7[:, 0:D], ACT.Copy).then_inc(s["m_xnt"], 1)
                elif step == "sq":
                    act.wait_ge(s["m_k"], m + 1)
                    if later:
                        act.wait_ge(s["m_sum"], m)
                    act.activation(q2, B5[:, D:2 * D], ACT.Square, accum_out=stat[:, 3:4]).then_inc(s["m_q2"], 1)
                    act.activation(k2, B5[:, 0:D], ACT.Square, accum_out=stat[:, 0:1]).then_inc(s["m_k2"], 1)
                    act.wait_ge(s["m_q2"], m + 1)
                    act.activation(q4, q2, ACT.Square, accum_out=stat[:, 4:5]).then_inc(s["m_q4"], 1)
                    act.wait_ge(s["m_q4"], m + 1)
                    act.activation(stat[:, 5:6], stat[:, 4:5], ACT.Sqrt).then_inc(s["m_nb"], 1)
                elif step == "k4":
                    act.wait_ge(s["m_k2n"], m + 1)
                    act.activation(k4, k2n, ACT.Square).then_inc(s["m_k4"], 1)
                else:
                    act.wait_ge(s["m_qt"], m + 1)
                    if later:
                        act.wait_ge(s["m_q_out"], m * 16)
                    act.activation(q2nt, B7[:, D:2 * D], ACT.Copy).then_inc(s["m_qtc"], 1)

            M_AT = {1: "xt", 4: "sq", 6: "k4", 10: "qt"}

            def g_and_m(t, ms):
                for b in range(TB):
                    if b % MSLOT in M_AT and ms[b // MSLOT] is not None:
                        m_act(ms[b // MSLOT], M_AT[b % MSLOT])
                    if b % BLOCKS == LAST0:
                        hi_part(t, b // BLOCKS, 0)
                    if b % BLOCKS == BLOCKS - 1:
                        hi_part(t, b // BLOCKS, 1)

            g_and_m(0, (None, None, 0))
            with act.Fori(1, L1 - 1) as t:
                g_and_m(t, (MS * t - 2, MS * t - 1, MS * t))
            g_and_m(L1 - 1, (T - 3, T - 2, T - 1))

            act.wait_ge(s["mix_dve"], 3)
            act.activation(pcol[:, 4:6], pcol[:, 0:2], ACT.Sqrt).then_inc(s["mix_act"], 1)

            def p_act(p, step):
                if step == "sd":
                    act.wait_ge(s["p_ln"], p + 1)
                    act.activation(stat[:, 6:7], stat[:, 17:18], ACT.Sqrt, bias=eps_ln[:, 0:1])\
                        .then_inc(s["p_sd"], 1)
                elif step == "xt":
                    act.wait_ge(s["p_xt"], p + 1)
                    act.activation(xn2t, B6[:, 0:D], ACT.Copy).then_inc(s["p_xtc"], 1)
                elif step == "h1s":
                    act.wait_ge(s["p_h1s"], p + 1)
                    for j in range(H):
                        act.activation(h1[:, j, :], B6[:, j * P:(j + 1) * P], ACT.Relu,
                                       bias=b1_col[:, j:j + 1]).then_inc(s["p_h1"], 1)
                elif step == "h1e":
                    act.wait_ge(s["p_h1e"], p + 1)
                    for j in range(EX):
                        act.activation(h1[:, H + j, :], B5[:, j * P:(j + 1) * P], ACT.Relu,
                                       bias=b1_col[:, H + j:H + j + 1]).then_inc(s["p_h1"], 1)
                elif step == "exp":
                    act.wait_ge(s["p_max"], p + 1)
                    act.activation(gate[:, 4:8], gate[:, 0:4], ACT.Exp, bias=stat[:, 8:9],
                                   accum_out=stat[:, 9:10]).then_inc(s["p_exp"], 1)
                elif step == "exp2":
                    act.wait_ge(s["p_gmax"], p + 1)
                    act.activation(gate[:, 12:16], gate[:, 8:12], ACT.Exp, bias=stat[:, 11:12])\
                        .then_inc(s["p_exp2"], 1)
                elif step == "h2":
                    act.wait_ge(s["p_l2"], p + 1)
                    act.activation(h2s, B6[:, 0:P], ACT.Relu, bias=b2_col[:, 0:1]).then_inc(s["p_h2"], 1)
                    for j in range(H):
                        act.activation(h2[:, j * P:(j + 1) * P], B6[:, (1 + j) * P:(2 + j) * P], ACT.Relu,
                                       bias=b2_col[:, 1 + j:2 + j]).then_inc(s["p_h2"], 1)

            STEPS = ["sd", "xt", "exp", "h1s", "exp2", "h1e", "h2"]
            AT = [2, 9, 11, 12, 13, 14, 19]

            def g_and_p(t, half, p0):
                for b in range(TB):
                    slot = half * TB + b
                    for k, a in enumerate(AT):
                        if slot % PSLOT == a:
                            p_act(p0 + slot // PSLOT, STEPS[k])
                    if b % BLOCKS == LAST0:
                        hi_part(t, b // BLOCKS, 0)
                    if b % BLOCKS == BLOCKS - 1:
                        hi_part(t, b // BLOCKS, 1)

            g_and_p(L1, 0, 0)
            g_and_p(L1 + 1, 1, 0)
            with act.Fori(1, J2) as j:
                g_and_p(2 * j + L1, 0, PS * j)
                g_and_p(2 * j + (L1 + 1), 1, PS * j)
            for k in STEPS:
                p_act(T - 1, k)

        @block.vector
        def _(dve):
            chain = {"n": 0}

            def link(ins):
                chain["n"] += 1
                ins.then_inc(s["dve_c"], 1)
                dve.wait_ge(s["dve_c"], chain["n"])

            def ln_dve(c):
                last = isinstance(c, int) and c == NC_P - 1
                if last:
                    dve.wait_ge(s["hi_ready"], c)
                    dve.memset(xc[96:P, CH - 1, :], 0.0).then_inc(s["pad_made"], 1)
                dve.wait_ge(s["x_in"], (c + 1 + last) * 16)
                K = 2 * CH + 1
                base = c * K
                for j in range(CH):
                    dve.bn_stats(st[:, j, :], xc[:, j, :]).then_inc(s["dve_p"], 1)
                dve.wait_ge(s["dve_p"], base + CH)
                dve.memset(carrier[:, :], 0.0)
                for j in range(CH):
                    nxt_i = dve.bn_aggr(mv[:, j, :], st[:, j, :])
                    nxt_i.then_inc(s["dve_p"], 1)
                dve.wait_ge(s["dve_p"], base + 2 * CH)
                dve.nop().then_inc(s["ln_done"], 1)
                dve.wait_ge(s["sd_ready"], c + 1)
                dve.reciprocal(rstd[:, :], rstd[:, :]).then_inc(s["dve_p"], 1)
                dve.wait_ge(s["dve_p"], base + 2 * CH + 1)
                if not isinstance(c, int) or c:
                    dve.wait_ge(s["xn_out"], c * 16)
                    dve.wait_ge(s["tab_out"], c * 16)
                for j in range(CH):
                    ins = dve.tensor_scalar(xnc[:, j, :], xc[:, j, :], mv[:, j, 0:1], rstd[:, j:j + 1],
                                            ALU.subtract, ALU.mult)
                ins.then_inc(s["xn_ready"], 1)
                dve.wait_ge(s["hi_ready"], c + 1)
                dve.tensor_tensor(tabc[:, :, D:2 * D], xnc, tabc[:, :, 0:D], ALU.subtract)\
                    .then_inc(s["lo_ready"], 1)

            ln_dve(0)
            with dve.Fori(1, NC_P - 1) as c:
                ln_dve(c)
            ln_dve(NC_P - 1)

            first_node = group_c[0:NG, 2 * BLOCKS:2 * BLOCKS + 1]
            dve.wait_ge(s["consts_in"], 64)
            dve.wait_ge(s["rows_in"], 16)
            dve.wait_ge(s["idx_ready"], 6)
            dve.tensor_copy(rfb[:, :], rows[:, 0:1].to_broadcast([ROWS, NG])).then_inc(s["rf_ready"], 1)
            dve.wait_ge(s["next_in"], 16)
            nxt_f = nxt.bitcast(F32)
            link(dve.tensor_tensor(nxt_f, nxt, rows, ALU.subtract))
            link(dve.tensor_reduce(ec[0:ROWS, 0:1], nxt_f, AX.X, ALU.min))
            link(dve.tensor_scalar(bad[0:ROWS, 0:1], ec[0:ROWS, 0:1], 0.0, None, ALU.is_lt))
            dve.wait_ge(s["rf_wide"], 1)
            link(dve.tensor_scalar(rfb[0:NG, 0:NG], banks[0][0:NG, 0:NG], first_node, None, ALU.is_lt, ALU.add,
                                   accum_out=ec[0:NG, 1:2]))
            link(dve.tensor_scalar(rfb[0:NG, 0:ROWS - NG], banks[0][0:NG, NG:ROWS], first_node, None, ALU.is_lt,
                                   ALU.add, accum_out=ec[0:NG, 2:3]))
            link(dve.tensor_tensor(ec[0:NG, 3:4], ec[0:NG, 1:2], ec[0:NG, 2:3], ALU.add))
            link(dve.tensor_scalar(ec[0:NG, 4:5], ec[0:NG, 3:4], -1.0, 0.0, ALU.add, ALU.max))
            dve.tensor_copy(ei[0:NG, 0:1], ec[0:NG, 4:5]).then_inc(s["row_ready"], 1)
            dve.wait_ge(s["row_got"], 16)
            row_f = srcf_g[:, 0:ROW]
            link(dve.tensor_copy(row_f, key_g[:, 0:ROW].bitcast(I32)))
            link(dve.tensor_scalar(key_g[:, 0:ROW], row_f, first_node, None, ALU.is_lt, ALU.add,
                                   accum_out=ec[0:NG, 5:6]))
            dve.scalar_tensor_tensor(ei[0:NG, 1:2], ec[0:NG, 4:5], float(ROW), ec[0:NG, 5:6], ALU.mult, ALU.add)\
                .then_inc(s["start_ready"], 1)
            dve.wait_ge(s["edges_got"], 48)
            rel = key_g
            link(dve.tensor_scalar(rel, dst_g, first_node, None, ALU.subtract))
            inb = dst_g.bitcast(F32)
            link(dve.scalar_tensor_tensor(inb, rel, float(GN), rel, ALU.is_lt, ALU.mult))
            link(dve.tensor_reduce(gate[0:NG, 0:BLOCKS], inb.rearrange("p (b c) -> p b c", c=P), AX.X, ALU.max))
            link(dve.tensor_tensor(gate[0:NG, 0:BLOCKS], gate[0:NG, 0:BLOCKS], group_c[0:NG, BLOCKS:2 * BLOCKS],
                                   ALU.is_ge))
            link(dve.tensor_tensor(gate[0:NG, BLOCKS:2 * BLOCKS],
                                   rel.rearrange("p (b c) -> p b c", c=P)[:, :, 0], group_c[0:NG, 0:BLOCKS],
                                   ALU.is_lt))
            link(dve.tensor_reduce(bad[0:NG, 1:2], gate[0:NG, 0:2 * BLOCKS], AX.X, ALU.add))
            dve.tensor_scalar(bad[0:NG, 2:3], rel[:, CAP - 1:CAP], float(GN), None, ALU.is_lt)\
                .then_inc(s["bad_ready"], 1)
            dve.wait_ge(s["flag_sum"], 1)
            link(dve.tensor_reduce(flag_f[:, :], banks[5][0:1, 0:4], AX.X, ALU.add))
            dve.tensor_copy(flag[:, :], flag_f[:, :]).then_inc(s["flag_ready"], 1)
            dve.scalar_tensor_tensor(key_g, rel, float(R), typ_g, ALU.mult, ALU.add).then_inc(s["edges_kf"], 1)
            for k in range(5):
                dve.wait_ge(s["turned"], k + 1)
                b0, nb = 4 * k, min(4, BLOCKS - 4 * k)
                dve.tensor_copy(key_t[:, 0:NG, b0:b0 + nb].rearrange("p g b -> p b g"),
                                banks[k][:, 0:nb * P].rearrange("p (b c) -> p b c", c=P)[:, :, 0:NG])\
                    .then_inc(s["turned_k"], 1)
            dve.wait_ge(s["turned_s"], 5)
            dve.memset(gate[:, :], 1.0).then_inc(s["prep_dve"], 1)

            RH = R // 2
            for k in range(4):
                h, r0 = k // 2, (k % 2) * RH
                dve.wait_ge(s["prep_act"], 2 * k + 2)
                dve.scalar_tensor_tensor(wr[:, 1, h, r0:r0 + RH, :].rearrange("p r d -> p (r d)"),
                                         wstage[:, 0:RH, :].rearrange("p r d -> p (r d)"), SCALE,
                                         wr[:, 0, h, r0:r0 + RH, :].rearrange("p r d -> p (r d)"),
                                         ALU.mult, ALU.subtract).then_inc(s["rel_lo"], 1)

            dve.wait_ge(s["weights_in"], 11 * 16)
            dve.wait_ge(s["bias_in"], 12 * 16)
            for h in range(H):
                for c, dest in ((0, wkq[:, h, D:2 * D]), (1, wkq[:, h, 0:D])):
                    link(dve.tensor_reduce(ec[:, 6:7], wq_s[:, h, c * D:(c + 1) * D], AX.X, ALU.add))
                    link(dve.tensor_scalar(ec[:, 7:8], ec[:, 6:7], 1.0 / D, None, ALU.mult))
                    link(dve.tensor_scalar(dest, wq_s[:, h, c * D:(c + 1) * D], ec[:, 7:8], None, ALU.subtract))
            for row in (bias_row[0:1, 0:D], bias_row[0:1, D:2 * D]):
                link(dve.tensor_reduce(ec[0:1, 6:7], row, AX.X, ALU.add))
                link(dve.tensor_scalar(ec[0:1, 7:8], ec[0:1, 6:7], 1.0 / D, None, ALU.mult))
                link(dve.tensor_scalar(row, row, ec[0:1, 7:8], None, ALU.subtract))
            dve.wait_ge(s["mixw_pe"], 1)
            link(dve.tensor_copy(wvt_s, B5[:, :].rearrange("p (a b) -> p a b", b=D)))
            for h in range(H):
                link(dve.tensor_copy(bvb[:, h, :], bv_col[:, h:h + 1].to_broadcast([P, P])))
            dve.nop().then_inc(s["prep_dve"], 1)
            dve.wait_ge(s["mixw_pe"], 2)
            link(dve.tensor_copy(wvo[:, :, :], B6[:, :].rearrange("p (a b) -> p a b", b=D)))
            link(dve.tensor_copy(bvo_b[:, :], B7[:, 0:D]))
            link(dve.tensor_tensor(bias_row[0:1, 2 * D:3 * D], bias_row[0:1, 2 * D:3 * D], bvo_b[0:1, :], ALU.add))
            link(dve.memset(ones16[:, :], 1.0))
            link(dve.tensor_copy(bias_part[0:1, 0, :], bias_row[0:1, :]))
            link(dve.tensor_tensor(bias_left[0:1, :], bias_row[0:1, :], bias_part[0:1, 0, :], ALU.subtract))
            link(dve.tensor_copy(bias_part[0:1, 1, :], bias_left[0:1, :]))
            link(dve.tensor_tensor(bias_part[0:1, 2, :], bias_left[0:1, :], bias_part[0:1, 1, :], ALU.subtract))
            link(dve.memset(work[:, 9:11, :], 0.0))
            link(dve.memset(key_t[:, NG:NG + GT, :], -1.0))
            dve.nop().then_inc(s["mix_dve"], 1)

            def keys(t, b0, b1, n):
                for g in range(b0 // BLOCKS, (b1 - 1) // BLOCKS + 1):
                    lo, hi = max(b0, g * BLOCKS), min(b1, (g + 1) * BLOCKS)
                    ins = dve.tensor_copy(key_now[:, lo:hi], key_t[:, bass.ds(GT * t + g, 1), lo - g * BLOCKS:hi - g * BLOCKS]
                                          .rearrange("p o b -> p (o b)"))
                ins.then_inc(s["keys_ready"], 1)
                dve.wait_ge(s["keys_ready"], n)

            def one_hot(t, b):
                lo, hi = WIN[b % BLOCKS]
                w = (hi - lo) * R
                if b >= OH or not isinstance(t, int) or t:
                    dve.wait_ge(s["blocks_used"], t * TB + b - OH + 1)
                dve.tensor_scalar(hot[:, b % OH, 0:w], iota16[:, lo * R:hi * R], key_now[:, b:b + 1],
                                  hot_v[:, b % BLOCKS:b % BLOCKS + 1], ALU.is_equal, ALU.mult)\
                    .then_inc(s["hot_ready"], 1)

            def next_hot(t, b):
                if b == 0:
                    keys(t, AHEAD, TB, 2 * t + 2)
                if b == TB - AHEAD:
                    keys(t + 1, 0, AHEAD, 2 * t + 3)
                if b < TB - AHEAD:
                    one_hot(t, b + AHEAD)
                else:
                    one_hot(t + 1, b + AHEAD - TB)

            def lo_part(t, g, q):
                n0 = g * GN + q * BANK_N
                for h in range(H):
                    dve.wait_ge(s["hi_done"], (4 * t + 2 * g + q) * H + h + 1)
                    dve.scalar_tensor_tensor(
                        s_lo[:, h, :, n0:n0 + BANK_N].rearrange("p r n -> p n r"),
                        s_hi[:, h, :, n0:n0 + BANK_N].rearrange("p r n -> p n r"), -SCALE,
                        banks[2 * q + h][:, :].rearrange("p (n r) -> p n r", r=R), ALU.mult, ALU.add)\
                        .then_inc(s["lo_done"], 1)

            def u_part(t):
                dve.wait_ge(s["w_done"], t + 1)
                if not isinstance(t, int) or t:
                    dve.wait_ge(s["u_out"], t * 16)
                dve.scalar_tensor_tensor(u_g[:, :], GB[:, D:2 * D], 0.0, x_g[:, :], ALU.max, ALU.add)\
                    .then_inc(s["u_half"], 1)
                dve.wait_ge(s["u_half"], t + 1)
                dve.tensor_tensor(u_g[:, :], u_g[:, :], GB[:, 0:D], ALU.add).then_inc(s["u_ready"], 1)

            NM = 6

            def m_dve(m, step, mask):
                inside = post_c[:, 16 + P * H:17 + P * H] if mask else ones[:, 0:1]
                later = not isinstance(m, int) or m > 0

                def mlink(n, ins):
                    ins.then_inc(s["dve_m"], 1)
                    dve.wait_ge(s["dve_m"], m * NM + n)

                if step == "k":
                    dve.wait_ge(s["m_k2"], m + 1)
                    mlink(1, dve.tensor_scalar(stat[:, 1:2], stat[:, 0:1], EPS_DIV, None, ALU.add))
                    mlink(2, dve.reciprocal(stat[:, 2:3], stat[:, 1:2]))
                    if later:
                        dve.wait_ge(s["m_used"], m)
                    dve.tensor_scalar(k2n, k2, stat[:, 2:3], inside, ALU.mult, ALU.mult).then_inc(s["m_k2n"], 1)
                    dve.wait_ge(s["m_nb"], m + 1)
                    mlink(3, dve.tensor_scalar(stat[:, 6:7], stat[:, 3:4], EPS_DIV, None, ALU.add))
                    mlink(4, dve.reciprocal(stat[:, 7:8], stat[:, 6:7]))
                    mlink(5, dve.tensor_scalar(stat[:, 8:9], stat[:, 5:6], stat[:, 7:8], EPS_NORM, ALU.mult, ALU.max))
                    mlink(6, dve.reciprocal(stat[:, 9:10], stat[:, 8:9]))
                    if later:
                        dve.wait_ge(s["m_qt"], m)
                    dve.tensor_scalar(q2n, q2, stat[:, 7:8], stat[:, 9:10], ALU.mult, ALU.mult)\
                        .then_inc(s["m_q2n"], 1)
                else:
                    if later:
                        dve.wait_ge(s["m_sum"], m)
                    dve.tensor_tensor(k2n_sum, k2n_sum, k2n, ALU.add)
                    dve.wait_ge(s["m_k4"], m + 1)
                    dve.tensor_tensor(k4_sum, k4_sum, k4, ALU.add).then_inc(s["m_sum"], 1)

            M_AT = {5: "k", 8: "sum"}

            def g_and_m(t, ms, u_late=True):
                for b in range(TB):
                    next_hot(t, b)
                    if b == U_AT and u_late:
                        u_part(t - 1)
                    if b % MSLOT in M_AT and ms[b // MSLOT] is not None:
                        m = ms[b // MSLOT]
                        m_dve(m, M_AT[b % MSLOT], isinstance(m, int) and m == T - 1)
                    if b % BLOCKS == LAST0 + 1:
                        lo_part(t, b // BLOCKS, 0)
                    if b == BLOCKS:
                        lo_part(t, 0, 1)
                lo_part(t, 1, 1)

            general = dve.value_load(flag[0:1, 0:1])
            with dve.If(general > 0):
                with dve.Fori(0, NEB) as k:
                    NL = 6

                    def step(n, ins):
                        ins.then_inc(s["dve_g"], 1)
                        dve.wait_ge(s["dve_g"], k * NL + n)

                    for j in range(3):
                        dve.wait_ge(s[f"gp_in{j}"], k * 16 + 16)
                    step(1, dve.scalar_tensor_tensor(gp_f[:, 0:1], gp_i[:, 1:2], float(R), gp_i[:, 2:3], ALU.mult,
                                                     ALU.add))
                    dve.tensor_copy(gp_keys, gp_f[:, 0:1].to_broadcast([P, P]))
                    dve.tensor_copy(gp_i[:, 3:4], gp_f[:, 0:1]).then_inc(s["gp_key"], 1)
                    dve.wait_ge(s["gp_wide"], k + 1)
                    step(2, dve.tensor_scalar(gp_same, banks[0][:, 0:P], gp_f[:, 0:1], None, ALU.is_equal))
                    dve.nop().then_inc(s["gp_made"], 1)
                    step(3, dve.tensor_tensor(gp_earlier, gp_same, post_c[:, POST_C - P:], ALU.mult))
                    step(4, dve.tensor_reduce(gp_f[:, 1:2], gp_earlier, AX.X, ALU.max))
                    step(5, dve.tensor_scalar(gp_f[:, 2:3], gp_f[:, 1:2], float(2 ** 20), gp_f[:, 0:1], ALU.mult,
                                              ALU.add))
                    dve.wait_ge(s["gp_sum"], k + 1)
                    dve.wait_ge(s["gp_got"], k * 32 + 32)
                    step(6, dve.tensor_tensor(gp_new, gp_was, banks[1][:, 0:D], ALU.add))
                    dve.tensor_copy(gp_i[:, 4:5], gp_f[:, 2:3]).then_inc(s["gp_new"], 1)
                dve.memset(gp_parts, 0.0).then_inc(s["dve_g"], 1)
                dve.wait_ge(s["dve_g"], NEB * 6 + 1)
                with dve.Fori(0, NG * PAIRS // P) as k:
                    NR = 3

                    def step(n, ins):
                        ins.then_inc(s["dve_g"], 1)
                        dve.wait_ge(s["dve_g"], k * NR + (NEB * 6 + 1 + n))

                    dve.wait_ge(s["gp_row_in"], k * 16 + 16)
                    step(1, dve.tensor_scalar(gp_parts[:, 0, 0:D], gp_was, 1.0 / SCALE, None, ALU.mult))
                    step(2, dve.scalar_tensor_tensor(gp_left, gp_parts[:, 0, 0:D], -SCALE, gp_was, ALU.mult, ALU.add))
                    step(3, dve.tensor_copy(gp_parts[:, 1, 0:D], gp_left))
                    dve.tensor_tensor(gp_parts[:, 1, D:2 * D], gp_left, gp_parts[:, 1, 0:D], ALU.subtract)\
                        .then_inc(s["gp_row_made"], 1)
                dve.wait_ge(s["gp_done"], 1)
                dve.memset(carrier[:, :], 0.0)

            keys(0, 0, AHEAD, 1)
            for b in range(AHEAD):
                one_hot(0, b)
            g_and_m(0, (None, None, 0), u_late=False)
            g_and_m(1, (1, 2, 3))
            with dve.Fori(2, L1 - 1) as t:
                g_and_m(t, (MS * t - 2, MS * t - 1, MS * t))
            g_and_m(L1 - 1, (T - 3, T - 2, T - 1))
            u_part(L1 - 1)

            dve.wait_ge(s["m_used"], T)
            dve.wait_ge(s["m_xnt_out"], T * 16)
            yt = work[:, 0:2, :]
            dve.wait_ge(s["m_sum"], T)
            link(dve.tensor_copy(yt, B6[:, :].rearrange("p (a b) -> p a b", b=D)))
            dve.wait_ge(s["mix_pe"], 1)
            link(dve.tensor_copy(pcol[:, 0:4], B7[:, 0:4]))
            dve.nop().then_inc(s["mix_dve"], 2)
            dve.wait_ge(s["mix_act"], 1)
            link(dve.tensor_scalar(pcol[:, 4:6], pcol[:, 4:6], EPS_NORM, None, ALU.max))
            link(dve.reciprocal(pcol[:, 6:8], pcol[:, 4:6]))
            link(dve.tensor_scalar(pcol[:, 6:8], pcol[:, 6:8], 1.0 / sqrt(N), None, ALU.mult))
            dve.wait_ge(s["mix_pe"], 2)
            for h in range(H):
                link(dve.scalar_tensor_tensor(m1[:, h, :], bvo_b[:, :], pcol[:, 2 + h:3 + h],
                                              B5[:, h * D:(h + 1) * D], ALU.mult, ALU.add))
                link(dve.tensor_scalar(m1[:, h, :], m1[:, h, :], pcol[:, 6 + h:7 + h], None, ALU.mult))
            dve.nop().then_inc(s["mix_dve"], 2)

            NPC = 16
            pchain = {"n": 0}

            def plink(p, ins):
                pchain["n"] += 1
                ins.then_inc(s["dve_c2"], 1)
                dve.wait_ge(s["dve_c2"], p * NPC + pchain["n"])

            def p_dve(p, step):
                if step == "x1":
                    pchain["n"] = 0
                    dve.wait_ge(s["p_mix"], p + 1)
                    dve.wait_ge(s["p_in"], (p + 1) * 32)
                    dve.tensor_tensor(x1, B5[:, 0:D], u_p, ALU.add).then_inc(s["p_x1"], 1)
                    dve.wait_ge(s["p_x1"], p + 1)
                    pchain["n"] += 1
                    dve.bn_stats(stat[:, 18:24], x1).then_inc(s["dve_c2"], 1)
                    dve.wait_ge(s["dve_c2"], p * NPC + pchain["n"])
                    dve.memset(carrier[:, :], 0.0)
                    dve.bn_aggr(stat[:, 16:18], stat[:, 18:24]).then_inc(s["p_ln"], 1)
                elif step == "xn2":
                    dve.wait_ge(s["p_sd"], p + 1)
                    plink(p, dve.reciprocal(stat[:, 7:8], stat[:, 6:7]))
                    dve.tensor_scalar(xn2, x1, stat[:, 16:17], stat[:, 7:8], ALU.subtract, ALU.mult)\
                        .then_inc(s["p_xn2"], 1)
                elif step == "max":
                    dve.wait_ge(s["p_log"], p + 1)
                    plink(p, dve.tensor_copy(gate[:, 0:4], B7[:, 0:4]))
                    plink(p, dve.tensor_reduce(stat[:, 10:11], gate[:, 0:4], AX.X, ALU.max))
                    dve.tensor_scalar(stat[:, 8:9], stat[:, 10:11], -1.0, None, ALU.mult).then_inc(s["p_max"], 1)
                elif step == "gate":
                    dve.wait_ge(s["p_exp"], p + 1)
                    plink(p, dve.reciprocal(stat[:, 12:13], stat[:, 9:10]))
                    plink(p, dve.tensor_scalar(gate[:, 8:12], gate[:, 4:8], stat[:, 12:13], None, ALU.mult))
                    plink(p, dve.tensor_reduce(stat[:, 13:14], gate[:, 8:12], AX.X, ALU.max))
                    dve.tensor_scalar(stat[:, 11:12], stat[:, 13:14], -1.0, None, ALU.mult).then_inc(s["p_gmax"], 1)
                    other = gate[:, 8:12].unsqueeze(1).to_broadcast([P, EX, EX])
                    own = gate[:, 8:12].unsqueeze(2).to_broadcast([P, EX, EX])
                    gt = gate[:, 16:32].rearrange("p (a b) -> p a b", b=EX)
                    eq = gate[:, 32:48].rearrange("p (a b) -> p a b", b=EX)
                    before = post_c[:, 0:16].rearrange("p (a b) -> p a b", b=EX)
                    plink(p, dve.tensor_tensor(gt, other, own, ALU.is_gt))
                    plink(p, dve.tensor_tensor(eq, other, own, ALU.is_equal))
                    plink(p, dve.tensor_tensor(eq, eq, before, ALU.mult))
                    plink(p, dve.tensor_tensor(gt, gt, eq, ALU.add))
                    plink(p, dve.tensor_reduce(gate[:, 48:52], gt, AX.X, ALU.add))
                    plink(p, dve.tensor_scalar(gate[:, 52:56], gate[:, 48:52], 2.0, None, ALU.is_lt))
                elif step == "gate2":
                    dve.wait_ge(s["p_exp2"], p + 1)
                    plink(p, dve.tensor_tensor(gate[:, 56:60], gate[:, 52:56], gate[:, 12:16], ALU.mult))
                    plink(p, dve.tensor_reduce(stat[:, 14:15], gate[:, 56:60], AX.X, ALU.add))
                    plink(p, dve.reciprocal(stat[:, 15:16], stat[:, 14:15]))
                    dve.tensor_scalar(gate[:, 60:64], gate[:, 56:60], stat[:, 15:16], None, ALU.mult)\
                        .then_inc(s["p_w5"], 1)
                elif step == "wt":
                    dve.wait_ge(s["p_wt"], p + 1)
                    dve.tensor_copy(w5t[:, :], B7[0:EX + 1, D:D + P]).then_inc(s["p_wtc"], 1)
                elif step == "h2g":
                    dve.wait_ge(s["p_h2"], 3 * p + 3)
                    dve.wait_ge(s["p_wb"], p + 1)
                    dve.tensor_tensor(h2g, h2, B7[:, 0:D], ALU.mult).then_inc(s["p_h2g"], 1)
                elif step == "out":
                    dve.wait_ge(s["p_l3"], p + 1)
                    if not isinstance(p, int) or p:
                        dve.wait_ge(s["out_done"], p * 16)
                    dve.tensor_tensor(o_p, x1, B5[:, 0:D], ALU.add).then_inc(s["p_out"], 1)

            STEPS = ["x1", "xn2", "max", "gate", "gate2", "wt", "h2g", "out"]
            AT = [1, 6, 10, 11, 14, 16, 20, 23]

            def g_and_p(t, half, p0, u_late=True):
                for b in range(TB):
                    slot = half * TB + b
                    next_hot(t, b)
                    if b == U_AT and u_late:
                        u_part(t - 1)
                    for k, a in enumerate(AT):
                        if slot % PSLOT == a:
                            p_dve(p0 + slot // PSLOT, STEPS[k])
                    if b % BLOCKS == LAST0 + 1:
                        lo_part(t, b // BLOCKS, 0)
                    if b == BLOCKS:
                        lo_part(t, 0, 1)
                lo_part(t, 1, 1)

            g_and_p(L1, 0, 0, u_late=False)
            g_and_p(L1 + 1, 1, 0)
            with dve.Fori(1, J2) as j:
                g_and_p(2 * j + L1, 0, PS * j)
                g_and_p(2 * j + (L1 + 1), 1, PS * j)
            u_part(T - 1)
            for k in STEPS:
                p_dve(T - 1, k)
            assert pchain["n"] == NPC

        @block.tensor
        def _(pe):
            mm = nc.tensor.matmul

            pe.wait_ge(s["consts_in"], 64)
            pe.wait_ge(s["rf_ready"], 1)
            mm(banks[0][0:NG, 0:ROWS], rfb[:, 0:NG], ident[0:ROWS, 0:ROWS], start=True, stop=True)\
                .then_inc(s["rf_wide"], 1)

            def turn(k, source, bank):
                for j in range(min(4, BLOCKS - 4 * k)):
                    b = 4 * k + j
                    last = nc.tensor.transpose(bank[:, j * P:j * P + NG], source[:, b * P:(b + 1) * P],
                                               ident[0:NG, 0:NG])
                last.then_inc(s["turned"], 1)

            pe.wait_ge(s["bad_ready"], 1)
            pe.wait_ge(s["idx_ready"], 6)
            mm(banks[5][0:1, 0:4], ones[:, 0:1], bad[:, :], start=True, stop=True).then_inc(s["flag_sum"], 1)
            pe.wait_ge(s["flag_ready"], 1)
            pe.wait_ge(s["edges_kf"], 1)
            for k in range(5):
                turn(k, key_g, banks[k])
            pe.wait_ge(s["srcf_ready"], 1)
            for k in range(5):
                if 5 + k >= 8:
                    pe.wait_ge(s["turned_k"], 5 + k - 8 + 1)
                turn(k, srcf_g, banks[(5 + k) % 8])
            pe.wait_ge(s["turned_s"], 5)

            pe.wait_ge(s["weights_in"], 11 * 16)
            for hc in range(H):
                for hr in range(H):
                    last = nc.tensor.transpose(B5[:, hc * D + hr * P:hc * D + (hr + 1) * P],
                                               wq_s[:, hr, 2 * D + hc * P:2 * D + (hc + 1) * P], ident[:, :])
            last.then_inc(s["mixw_pe"], 1)
            pe.wait_ge(s["prep_dve"], 2)
            for hr in range(H):
                for k in range(H):
                    mm(B6[:, hr * D:(hr + 1) * D], wvt_s[:, k, hr * P:(hr + 1) * P], wo_s[:, k, :],
                       start=(k == 0), stop=(k == H - 1))
            for k in range(H):
                last = mm(B7[:, 0:D], bvb[:, k, :], wo_s[:, k, :], start=(k == 0), stop=(k == H - 1))
            last.then_inc(s["mixw_pe"], 1)
            pe.wait_ge(s["mix_dve"], 1)
            mm(B6[:, :], zeros[:, 0:P], zeros[:, :], start=True, stop=True).then_inc(s["mixw_pe"], 1)

            def agg(t, b):
                g, bb = b // BLOCKS, b % BLOCKS
                lo, hi = WIN[bb]
                if b % RB == 0:
                    pe.wait_ge(got[b // RB], (t + 1) * RB * 16)
                n_before = 4 * t + 2 * g
                if bb == 0 and (b or not isinstance(t, int) or t):
                    pe.wait_ge(s["lo_done"], (n_before - 1) * H)
                if bb == FIRST1 and (b >= BLOCKS or not isinstance(t, int) or t):
                    pe.wait_ge(s["lo_done"], n_before * H)
                pe.wait_ge(s["hot_ready"], t * TB + b + 1)
                for q in range(2):
                    l, r = max(lo, q * BANK_N), min(hi, (q + 1) * BANK_N)
                    if l >= r:
                        continue
                    first = 0 if q == 0 else FIRST1
                    for h in range(H):
                        for part in range(2):
                            last = mm(banks[2 * q + h][:, (l - q * BANK_N) * R:(r - q * BANK_N) * R],
                                      ring[:, b, part * D + h * P:part * D + (h + 1) * P],
                                      hot[:, b % OH, (l - lo) * R:(r - lo) * R],
                                      start=(bb == first and part == 0), stop=True, skip_group_check=True)
                last.then_inc(s["blocks_used"], 1)

            def relations(t):
                pe.wait_ge(s["xg_in"], (t + 1) * 32)
                if not isinstance(t, int) or t:
                    pe.wait_ge(s["u_ready"], t)
                mm(GB[:, :], ones16[:, :], bias16[:, 2 * D:4 * D], start=True, stop=False)
                for h in range(H):
                    mm(GB[:, :], xnt_g[:, h, :], wown[:, h, :], start=False, stop=False)
                for h in range(H):
                    pe.wait_ge(s["hi_done"], (4 * t + 3) * H + h + 1)
                    for r in range(R):
                        for w in (0, 1):
                            mm(GB[:, D:2 * D], s_hi[:, h, r, :], wr[:, w, h, r, :], start=False, stop=False)
                    pe.wait_ge(s["lo_done"], (4 * t + 3) * H + h + 1)
                    for r in range(R):
                        last = mm(GB[:, D:2 * D], s_lo[:, h, r, :], wr[:, 2, h, r, :], start=False,
                                  stop=(h == H - 1 and r == R - 1))
                last.then_inc(s["w_done"], 1)

            def m_pe(m, step):
                later = not isinstance(m, int) or m > 0
                if step == "xt":
                    pe.wait_ge(s["m_in"], (m + 1) * 16)
                    if later:
                        pe.wait_ge(s["m_qtc"], m)
                    for h in range(H):
                        last = nc.tensor.transpose(B7[:, h * P:(h + 1) * P], xn_m[:, h * P:(h + 1) * P], ident[:, :])
                    last.then_inc(s["m_turned"], 1)
                elif step == "kq":
                    pe.wait_ge(s["m_xnt"], m + 1)
                    if later:
                        pe.wait_ge(s["m_k2"], m)
                    mm(B5[:, :], ones16[:, :], bias16[:, 0:2 * D], start=True, stop=False)
                    for h in range(H):
                        last = mm(B5[:, :], xnt_m[:, h * P:(h + 1) * P], wkq[:, h, :], start=False,
                                  stop=(h == H - 1))
                    last.then_inc(s["m_k"], 1)
                elif step == "sum":
                    pe.wait_ge(s["m_k2n"], m + 1)
                    for h in range(H):
                        last = mm(B6[:, h * D:(h + 1) * D], xn_m[:, h * P:(h + 1) * P], k2n, start=False, stop=True,
                                  skip_group_check=True)
                    last.then_inc(s["m_used"], 1)
                else:
                    pe.wait_ge(s["m_q2n"], m + 1)
                    for h in range(H):
                        last = nc.tensor.transpose(B7[:, D + h * P:D + (h + 1) * P], q2n[:, h * P:(h + 1) * P],
                                                   ident[:, :])
                    last.then_inc(s["m_qt"], 1)

            M_AT = {0: "xt", 2: "kq", 7: "sum", 9: "qt"}

            def g_and_m(t, ms):
                for b in range(TB):
                    agg(t, b)
                    if b % MSLOT in M_AT and ms[b // MSLOT] is not None:
                        m_pe(ms[b // MSLOT], M_AT[b % MSLOT])
                relations(t)

            pe.wait_ge(s["bias_in"], 12 * 16)
            pe.wait_ge(s["bias_parts"], 3 * 16)
            pe.wait_ge(s["rel_lo"], 4)
            general = pe.value_load(flag[0:1, 0:1])
            with pe.If(general > 0):
                with pe.Fori(0, NEB) as k:
                    pe.wait_ge(s["gp_key"], k + 1)
                    mm(banks[0][:, 0:P], gp_keys, ident[:, :], start=True, stop=True).then_inc(s["gp_wide"], 1)
                    pe.wait_ge(s["gp_made"], k + 1)
                    pe.wait_ge(s["gp_got"], k * 32 + 32)
                    mm(banks[1][:, 0:D], gp_same, gp_rows[:, 0:D], start=True, stop=False)
                    mm(banks[1][:, 0:D], gp_same, gp_rows[:, D:2 * D], start=False, stop=True)\
                        .then_inc(s["gp_sum"], 1)
            g_and_m(0, (None, None, 0))
            with pe.Fori(1, L1 - 1) as t:
                g_and_m(t, (MS * t - 2, MS * t - 1, MS * t))
            g_and_m(L1 - 1, (T - 3, T - 2, T - 1))

            pe.wait_ge(s["m_sum"], T)
            pe.wait_ge(s["m_qtc"], T)
            for j, own in ((0, k4_sum), (2, k2n_sum)):
                for h in range(H):
                    last = mm(B7[:, j + h:j + h + 1], own[:, h * P:(h + 1) * P], ones[:, 0:1], start=True, stop=True)
            last.then_inc(s["mix_pe"], 1)
            pe.wait_ge(s["mix_dve"], 3)
            yt = work[:, 0:2, :]
            for hc in range(H):
                for k in range(H):
                    last = mm(B5[:, hc * D:(hc + 1) * D], yt[:, k, hc * P:(hc + 1) * P], wvo[:, k, :],
                              start=(k == 0), stop=(k == H - 1))
            last.then_inc(s["mix_pe"], 1)
            pe.wait_ge(s["mix_dve"], 5)

            def p_pe(p, step):
                if step == "mix":
                    pe.wait_ge(s["p_in"], (p + 1) * 32)
                    if not isinstance(p, int) or p:
                        pe.wait_ge(s["p_out"], p)
                    for h in range(H):
                        last = mm(B5[:, 0:D], q2nt_p[:, h * P:(h + 1) * P], m1[:, h, :], start=(h == 0),
                                  stop=(h == H - 1))
                    last.then_inc(s["p_mix"], 1)
                elif step == "xt":
                    pe.wait_ge(s["p_xn2"], p + 1)
                    for h in range(H):
                        last = nc.tensor.transpose(B6[:, h * P:(h + 1) * P], xn2[:, h * P:(h + 1) * P], ident[:, :])
                    last.then_inc(s["p_xt"], 1)
                elif step == "l1":
                    pe.wait_ge(s["p_xtc"], p + 1)
                    mm(B7[:, 0:EX], ones16[:, :], bias16[:, 4 * D:BIAS], start=True, stop=False)
                    for h in range(H):
                        last = mm(B7[:, 0:EX], xn2t[:, h * P:(h + 1) * P], gw[:, h, :], start=False, stop=(h == H - 1))
                    last.then_inc(s["p_log"], 1)
                    for j in range(H):
                        for h in range(H):
                            last = mm(B6[:, j * P:(j + 1) * P], sw1[:, h, j * P:(j + 1) * P],
                                      xn2t[:, h * P:(h + 1) * P], start=(h == 0), stop=(h == H - 1))
                    last.then_inc(s["p_h1s"], 1)
                    for j in range(EX):
                        for h in range(H):
                            last = mm(B5[:, j * P:(j + 1) * P], ew1[:, h, j, :],
                                      xn2t[:, h * P:(h + 1) * P], start=(h == 0), stop=(h == H - 1))
                    last.then_inc(s["p_h1e"], 1)
                elif step == "wt":
                    pe.wait_ge(s["p_w5"], p + 1)
                    nc.tensor.transpose(B7[0:EX + 1, D:D + P], gate[:, 60:65], ident[:, :]).then_inc(s["p_wt"], 1)
                elif step == "l2":
                    pe.wait_ge(s["p_wtc"], p + 1)
                    for j in range(H):
                        last = mm(B7[:, j * P:(j + 1) * P], post_c[0:EX, 16 + j * P:16 + (j + 1) * P], w5t[0:EX, :],
                                  start=True, stop=True)
                    last.then_inc(s["p_wb"], 1)
                    pe.wait_ge(s["p_h1"], (p + 1) * (H + EX))
                    for h in range(H):
                        mm(B6[:, 0:P], sw2[:, h, :], h1[:, h, :], start=(h == 0), stop=(h == H - 1))
                    for e in range(EX):
                        o = (e % 2) * EH2
                        last = mm(B6[o:o + EH2, (1 + e // 2) * P:(2 + e // 2) * P], ew2[:, e, :], h1[:, H + e, :],
                                  start=True, stop=True)
                    last.then_inc(s["p_l2"], 1)
                elif step == "l3":
                    pe.wait_ge(s["p_h2g"], p + 1)
                    mm(B5[:, 0:D], w5t[:, :], b3[:, :], start=True, stop=False)
                    mm(B5[:, 0:D], h2s, sw3[:, :], start=False, stop=False)
                    for j in range(H):
                        last = mm(B5[:, 0:D], h2g[:, j * P:(j + 1) * P], ew3[:, j, :], start=False, stop=(j == H - 1))
                    last.then_inc(s["p_l3"], 1)

            STEPS = ["mix", "xt", "l1", "wt", "l2", "l3"]
            AT = [0, 9, 10, 16, 18, 22]

            def g_and_p(t, half, p0):
                for b in range(TB):
                    slot = half * TB + b
                    agg(t, b)
                    for k, a in enumerate(AT):
                        if slot % PSLOT == a:
                            p_pe(p0 + slot // PSLOT, STEPS[k])
                relations(t)

            g_and_p(L1, 0, 0)
            g_and_p(L1 + 1, 1, 0)
            with pe.Fori(1, J2) as j:
                g_and_p(2 * j + L1, 0, PS * j)
                g_and_p(2 * j + (L1 + 1), 1, PS * j)
            for k in STEPS:
                p_pe(T - 1, k)


_INS = ["x", "src", "dst", "edge_type_16", "L0_gnn_W_rel", "L0_gnn_W_self", "L0_gnn_bias", "L0_mix_W_qkv",
        "L0_mix_b_qkv", "L0_mix_W_out", "L0_mix_b_out", "L0_ffn_sW1", "L0_ffn_sb1", "L0_ffn_sW2", "L0_ffn_sb2",
        "L0_ffn_sW3", "L0_ffn_sb3", "L0_ffn_eW1", "L0_ffn_eb1", "L0_ffn_eW2", "L0_ffn_eb2", "L0_ffn_eW3",
        "L0_ffn_eb3", "L0_ffn_gW", "L0_ffn_gb"]


def consts():
    ident = np.eye(P, dtype=np.float32)
    iota = np.tile(np.arange(PAIRS, dtype=np.float16), (P, 1))
    group = np.zeros((P, 2 * BLOCKS + 1), np.float32)
    group[:, 0:BLOCKS] = [lo for lo, _ in WIN]
    group[:, BLOCKS:2 * BLOCKS] = [hi for _, hi in WIN]
    group[:, 2 * BLOCKS] = GN * np.arange(P)
    post = np.zeros((P, POST_C), np.float32)
    post[:, 0:16] = np.tril(np.ones((EX, EX), np.float32), -1).reshape(1, 16)
    for e in range(EX):
        post[e, 16 + (e // 2) * P + (e % 2) * EH2:16 + (e // 2) * P + (e % 2 + 1) * EH2] = 1.0
    post[0:TAIL, 16 + P * H] = 1.0
    post[:, POST_C - P:] = np.tril(np.ones((P, P), np.float32), -1)
    return {"c_ident": ident, "c_iota": iota, "c_group": group, "c_post": post}


def kernel(**inputs):
    import concourse.bacc as bacc
    from concourse.bass_utils import run_bass_kernel_spmd

    nc = bacc.Bacc("TRN2", target_bir_lowering=False, num_devices=1)
    arrays, args = {}, []
    for name, a in [(n, inputs[n]) for n in _INS] + list(consts().items()):
        a = np.ascontiguousarray(a)
        arrays[name] = a
        args.append(nc.dram_tensor(name, a.shape, mybir.dt.from_np(a.dtype), kind="ExternalInput").ap())
    args.append(nc.dram_tensor("out", (N, D), F32, kind="ExternalOutput").ap())
    build(nc, *args)
    r = run_bass_kernel_spmd(nc, [arrays], core_ids=[0])
    return r.results[0]["out"]
```

```python
from contextlib import ExitStack
from math import ceil, floor, sqrt

import numpy as np
import concourse.bass as bass
from concourse import mybir
from concourse.alu_op_type import AluOpType as ALU

F32 = mybir.dt.float32
F16 = mybir.dt.float16
I32 = mybir.dt.int32
ACT = mybir.ActivationFunctionType
AX = mybir.AxisListType

P = 128
D = 256
H = D // P
R = 16
N = 6250
E = 206250
T = -(-N // P)
TAIL = N - (T - 1) * P
NP = T * P
GN = 64
GT = P // GN
NG = T * GT
PAIRS = GN * R
DEG = E / N
BLOCKS = 18
CAP = BLOCKS * P
TB = GT * BLOCKS
BANK_N = 32
ROWS, ROW = 125, E // 125
EPAD = E + CAP
PADDST = 8191
SCALE = 64.0
EPS_LN, EPS_DIV, EPS_NORM = 1e-5, 1e-7, 1e-12
Z = 4.3
CH = 7
NEB = -(-E // P)
RH = R // 4
REL_LOADS = H * R // RH
MS = 3
L1 = 1 + -(-(T - 1) // MS)
PS = 3
J2 = (T - L1) // 2
EX, EH1, EH2 = 4, 128, 64
BIAS = 4 * D + EX
POST_C = 16 + P * H + 1 + P
RB = 6
OH = 12
U_AT = 3
AHEAD = 8
MSLOT = TB // MS
PSLOT = 2 * TB // PS


PE_AT = ((0, 1, 3, 10, 12, 17), (0, 9, 10, 16, 18, 22), (0, 9, 10, 16, 18, 22))
ACT_AT = ((1, 2, 5, 5, 7, 8, 13), (2, 9, 11, 12, 13, 14, 19), (2, 9, 11, 12, 13, 14, 19))
DVE_AT = ((0, 2, 4, 6, 8, 10, 14, 18), (1, 6, 10, 11, 14, 16, 20, 23), (1, 6, 10, 11, 14, 16, 20, 23))


def windows():
    out = []
    for b in range(BLOCKS):
        lo = floor(P * b / DEG - Z * sqrt((DEG - 1) * P * b / DEG) / DEG)
        hi = ceil(P * (b + 1) / DEG + Z * sqrt((DEG - 1) * P * (b + 1) / DEG) / DEG) + 1
        if b < 2 * (GN // 8):
            lo, hi = min(lo, 8 * (b // 2)), max(hi, 8 * (b // 2) + 8)
        out.append((max(lo, 0), min(hi, GN)))
    return out


WIN = windows()
WMAX = max(hi - lo for lo, hi in WIN) * R
LAST0 = max(b for b, (lo, hi) in enumerate(WIN) if lo < BANK_N)
FIRST1 = min(b for b, (lo, hi) in enumerate(WIN) if hi > BANK_N)


def build(nc, x, src, dst, etype, w_rel, w_self, g_bias, w_qkv, b_qkv, w_out, b_out, s_w1, s_b1,
          s_w2, s_b2, s_w3, s_b3, e_w1, e_b1, e_w2, e_b2, e_w3, e_b3, g_w, g_b,
          c_ident, c_iota, c_group, c_post, c_pad, out):
    ctx = ExitStack()
    with ctx:
        def sb(name, shape, dt=F32):
            return ctx.enter_context(nc.sbuf_tensor(name, shape, dt))

        def sem(name):
            return ctx.enter_context(nc.semaphore(name))

        table = nc.dram_tensor("table", (NP, 2 * D), F16).ap()
        sums_t = nc.dram_tensor("sums_t", (2 * NG * PAIRS, 2 * D), F16).ap()
        sums_d = nc.dram_tensor("sums_d", (NG * PAIRS, D), F32).ap()
        xn_d = nc.dram_tensor("xn_d", (NP, D), F32).ap()
        xnt_d = nc.dram_tensor("xnt_d", (T, P, D), F32).ap()
        q2nt_d = nc.dram_tensor("q2nt_d", (T, P, D), F32).ap()
        u_d = nc.dram_tensor("u_d", (T, P, D), F32).ap()
        src_p = nc.dram_tensor("src_p", (EPAD,), I32).ap()
        dst_p = nc.dram_tensor("dst_p", (EPAD,), I32).ap()
        typ_p = nc.dram_tensor("typ_p", (EPAD,), I32).ap()

        ident = sb("ident", [P, P])
        iota16 = sb("iota16", [P, PAIRS], F16)
        group_c = sb("group_c", [P, 2 * BLOCKS + 1])
        post_c = sb("post_c", [P, POST_C])
        ones = sb("ones", [P, P])
        zeros = sb("zeros", [P, 512])
        eps_ln = sb("eps_ln", [P, 1])
        wr = sb("wr", [P, 3, H, R, D], F16)
        wown = sb("wown", [P, H, 2 * D])
        wvo = wown[:, :, 0:D]
        wkq = sb("wkq", [P, H, 2 * D])
        m1 = sb("m1", [P, H, D])
        sw1 = sb("sw1", [P, H, D])
        ew1 = sb("ew1", [P, H, EX, EH1])
        sw2 = sb("sw2", [P, H, P])
        ew2 = sb("ew2", [P, EX, EH2])
        sw3 = sb("sw3", [P, D])
        ew3 = sb("ew3", [P, H, D])
        gw = sb("gw", [P, H, EX])
        bias_row = sb("bias_row", [1, BIAS])
        bias_left = sb("bias_left", [1, BIAS])
        bias_part = sb("bias_part", [1, 3, BIAS], F16)
        bias16 = sb("bias16", [3, BIAS], F16)
        ones16 = sb("ones16", [3, P], F16)
        b3 = sb("b3", [EX + 1, D])
        b1_col = sb("b1_col", [P, H + EX])
        b2_col = sb("b2_col", [P, 1 + H])

        idx_t = sb("idx_t", [P, NG, BLOCKS], I32)
        key_t = sb("key_t", [P, NG + GT, BLOCKS])
        hot_v = sb("hot_v", [P, BLOCKS])
        idx_now = sb("idx_now", [P, TB], I32)
        key_now = sb("key_now", [P, TB])
        ring = sb("ring", [P, TB, 2 * D], F16)
        hot = sb("hot", [P, OH, WMAX], F16)
        s_hi = sb("s_hi", [P, H, R, P], F16)
        s_lo = sb("s_lo", [P, H, R, P], F16)
        xnt_g = sb("xnt_g", [P, H, P])
        x_g = sb("x_g", [P, D])
        u_g = sb("u_g", [P, D])

        work = sb("work", [P, 20, D])
        (xn_m, xnt_m, k2, k2n, k4, q2, q4, q2n, q2nt, k2n_sum, k4_sum) = (work[:, j, :] for j in range(11))
        (u_p, q2nt_p, x1, xn2, xn2t, h2, h2g, o_p) = (work[:, j, :] for j in range(8))
        h1 = work[:, 12:15, :].rearrange("p a (b n) -> p (a b) n", n=P)
        h2s = work[:, 15, 0:P]
        stat = sb("stat", [P, 32])
        gate = sb("gate", [P, 96])
        w5t = sb("w5t", [EX + 1, P])

        ring_f = ring[:, :, :].rearrange("p a b -> p (a b)").bitcast(F32)
        s_f, s_f2 = (own[:, :, :, :].rearrange("p a b c -> p (a b c)").bitcast(F32) for own in (s_hi, s_lo))

        def chunk(flat, width):
            return flat.rearrange("p (a b) -> p a b", b=width)

        xc = (chunk(ring_f[:, 0:CH * D], D), chunk(s_f[:, 0:CH * D], D))
        xnc = (chunk(ring_f[:, CH * D:2 * CH * D], D), chunk(s_f2[:, 0:CH * D], D))
        tabc = (chunk(ring[:, :, :].rearrange("p a b -> p (a b)")[:, 4 * CH * D:6 * CH * D], 2 * D),
                chunk(work[:, 12:12 + CH, :].rearrange("p a b -> p (a b)").bitcast(F16), 2 * D))
        rows = ring_f[0:ROWS, 3 * CH * D:3 * CH * D + ROW].bitcast(I32)
        nxt = ring_f[0:ROWS, 3 * CH * D + ROW:3 * CH * D + 2 * ROW].bitcast(I32)
        wr_f = wr[:, :, :, :, :].rearrange("p a b c d -> p (a b c d)").bitcast(F32)
        src_g, dst_g, typ_g = (wr_f[0:NG, j * CAP:(j + 1) * CAP].bitcast(I32) for j in range(3))
        key_g, srcf_g = (wr_f[0:NG, j * CAP:(j + 1) * CAP] for j in (3, 4))
        wstage = (work[:, 12:12 + RH, :], work[:, 12 + RH:12 + 2 * RH, :])
        st = sb("st", [P, CH, 6])
        mv = sb("mv", [P, CH, 2])
        rstd = sb("rstd", [P, CH])
        ec = sb("ec", [P, 8])
        ei = sb("ei", [P, 2], I32)
        rfb = sb("rfb", [ROWS, NG])
        bad = sb("bad", [P, 4])
        wvt_s = work[:, 2:4, :]
        wo_s = work[:, 4:6, :]
        wq_s = work[:, 6:12, :].rearrange("p (h c) d -> p h (c d)", h=H)
        bv_col = sb("bv_col", [P, H])
        bvb = sb("bvb", [P, H, P])
        bvo_b = sb("bvo_b", [P, D])
        pcol = sb("pcol", [P, 8])
        carrier = sb("carrier", [P, 1])
        flag = sb("flag", [1, 1], I32)
        flag_f = sb("flag_f", [1, 1])

        gp_i = sb("gp_i", [P, 5], I32)
        gp_f = sb("gp_f", [P, 3])
        gp_rows = ring[:, 0, :]
        gp_was, gp_new = ring_f[:, D:2 * D], ring_f[:, 2 * D:3 * D]
        gp_same = ring[:, 3, 0:P]
        gp_earlier = ring_f[:, 4 * D:4 * D + P]
        gp_keys = ring_f[:, 4 * D + P:5 * D]
        gp_parts = ring[:, 6:8, :]
        gp_left = ring_f[:, 8 * D:9 * D]

        banks = [ctx.enter_context(nc.psum_tensor(f"bank{i}", [P, 512], F32)) for i in range(8)]
        GB = banks[4]
        B5, B6, B7 = banks[5:8]

        names = """consts_in x_in0 x_in1 weights_in mixing_in bias_in rel_in0 rel_in1 pad_made pads_in edges_pad rows_in next_in
            ln_done sd_ready xn_ready hi_ready lo_ready xn_out0 xn_out1 tab_out0 tab_out1
            rf_ready rf_wide row_ready row_got start_ready edges_got edges_kf srcf_ready
            turned turned_k turned_s prep_dve prep_act rel_lo mixw_pe
            idx_ready keys_ready hot_ready blocks_used hi_done lo_done w_done xg_in u_half u_ready u_out
            bias_parts batches bad_ready flag_sum flag_ready gp_clear gp_in0 gp_in1 gp_in2 gp_key gp_wide gp_made gp_got gp_sum gp_new gp_out
            gp_row_in gp_row_made gp_row_out gp_done dve_g m_qtc m_q_out m_qt m_q2 m_q4 m_nb m_q2n m_sum m_in m_turned m_xnt m_xnt_out m_k m_k2 m_k2n m_k4 m_used m_all
            mix_dve mix_act mix_pe
            p_in p_q p_q2 p_q4 p_nb p_sd p_q2n p_qt p_qtc p_mix p_x1 p_ln p_xn2 p_xt p_xtc p_log p_h1s p_h1e p_h1 p_max p_exp
            p_gmax p_exp2 p_w5 p_wt p_wtc p_wb p_l2 p_h2 p_h2g p_l3 p_out out_done
            dve_c dve_c2 dve_p dve_m act_c""".split()
        s = {n: sem(n) for n in names}
        x_in, xn_out, tab_out, rel_in = ([s[f"{n}{buf}"] for buf in range(2)]
                                         for n in ("x_in", "xn_out", "tab_out", "rel_in"))
        got = [sem(f"got{i}") for i in range(TB // RB)]

        block = ctx.enter_context(nc.Block())

        def chunk_rows(c):
            return slice(c * CH * P, (c + 1) * CH * P)

        NC_P = T // CH
        CHUNKS = (NC_P - NC_P // 2, NC_P // 2)
        assert NC_P % 2

        @block.sync
        def _(sp):
            sp.dma_start(rows, dst.rearrange("(r c) -> r c", c=ROW)).then_inc(s["rows_in"], 16)

            def ln_in(n, buf):
                c = 2 * n + buf
                own = xc[buf]
                if isinstance(c, int) and c == NC_P - 1:
                    sp.dma_start(own[:, 0:CH - 1, :], x[(NC_P - 1) * CH * P:(T - 1) * P, :]
                                 .rearrange("(j p) d -> p j d", p=P)).then_inc(x_in[buf], 16)
                    sp.wait_ge(s["pad_made"], 1)
                    sp.dma_start(own[0:TAIL, CH - 1, :], x[(T - 1) * P:N, :]).then_inc(x_in[buf], 16)
                else:
                    sp.dma_start(own, x[bass.ds(c * (CH * P), CH * P), :]
                                 .rearrange("(j p) d -> p j d", p=P)).then_inc(x_in[buf], 16)

            def ln_out(n, buf, fetch=True):
                c = 2 * n + buf
                sp.wait_ge(s["xn_ready"], c + 1)
                sp.dma_start(xn_d[bass.ds(c * (CH * P), CH * P), :].rearrange("(j p) d -> p j d", p=P),
                             xnc[buf]).then_inc(xn_out[buf], 16)
                if fetch:
                    ln_in(n + 1, buf)
                sp.wait_ge(s["lo_ready"], c + 1)
                sp.dma_start(table[bass.ds(c * (CH * P), CH * P), :].rearrange("(j p) d -> p j d", p=P),
                             tabc[buf]).then_inc(tab_out[buf], 16)

            ln_in(0, 0)
            sp.dma_start(group_c[:, :], c_group).then_inc(s["consts_in"], 16)
            sp.dma_start(ident[:, :], c_ident).then_inc(s["consts_in"], 16)
            ln_in(0, 1)
            for k, (full, own) in enumerate(((dst_p, dst), (src_p, src), (typ_p, etype))):
                sp.dma_start(full[0:E].rearrange("(r c) -> r c", c=ROW),
                             own.rearrange("(r c) -> r c", c=ROW)).then_inc(s["edges_pad"], 16)
                sp.dma_start(full[E:EPAD].rearrange("(r c) -> r c", c=P),
                             c_pad[k, :].rearrange("(r c) -> r c", c=P)).then_inc(s["edges_pad"], 16)
            sp.dma_start(iota16[:, :], c_iota).then_inc(s["consts_in"], 16)
            sp.dma_start(post_c[:, :], c_post).then_inc(s["consts_in"], 16)
            with sp.Fori(0, NC_P // 2 - 1) as k:
                ln_out(k, 0)
                ln_out(k, 1)
            def rel_load(k):
                h, r0 = k * RH // R, k * RH % R
                if k >= 2:
                    sp.wait_ge(s["rel_lo"], k - 1)
                sp.dma_start(wstage[k % 2], w_rel[r0:r0 + RH, h * P:(h + 1) * P, :].rearrange("r p c -> p r c"))\
                  .then_inc(rel_in[k % 2], 16)

            ln_out(NC_P // 2 - 1, 0)
            sp.dma_start(wq_s, w_qkv.rearrange("(h p) c -> p h c", p=P)).then_inc(s["mixing_in"], 16)
            sp.dma_start(wo_s, w_out.rearrange("(h p) c -> p h c", p=P)).then_inc(s["mixing_in"], 16)
            ln_out(NC_P // 2 - 1, 1, fetch=False)
            sp.wait_ge(tab_out[1], CHUNKS[1] * 16)
            rel_load(0)
            rel_load(1)
            ln_out(NC_P // 2, 0, fetch=False)

            def m_load(m):
                if not isinstance(m, int) or m:
                    sp.wait_ge(s["m_used"], m)
                sp.dma_start(xn_m, xn_d[bass.ds(m * P, P), :]).then_inc(s["m_in"], 16)

            def m_store(m):
                sp.wait_ge(s["m_xnt"], m + 1)
                sp.dma_start(xnt_d[bass.ds(m, 1), :, :].rearrange("o p d -> (o p) d"), xnt_m)\
                  .then_inc(s["m_xnt_out"], 16)

            def m_store_q(m):
                sp.wait_ge(s["m_qtc"], m + 1)
                sp.dma_start(q2nt_d[bass.ds(m, 1), :, :].rearrange("o p d -> (o p) d"), q2nt)\
                  .then_inc(s["m_q_out"], 16)

            def g_load(t, m_now):
                sp.wait_ge(s["m_xnt_out"], m_now * 16)
                if not isinstance(t, int) or t:
                    sp.wait_ge(s["u_ready"], t)
                sp.dma_start(xnt_g[:, :, :].rearrange("p h n -> p (h n)"),
                             xnt_d[bass.ds(t, 1), :, :].rearrange("o p d -> (o p) d"))\
                  .then_inc(s["xg_in"], 16)
                if isinstance(t, int) and t == T - 1:
                    sp.dma_start(x_g[0:TAIL, :], x[(T - 1) * P:N, :]).then_inc(s["xg_in"], 16)
                else:
                    sp.dma_start(x_g[:, :], x[bass.ds(t * P, P), :]).then_inc(s["xg_in"], 16)

            def g_store(t):
                sp.wait_ge(s["u_ready"], t + 1)
                sp.dma_start(u_d[bass.ds(t, 1), :, :].rearrange("o p d -> (o p) d"), u_g[:, :])\
                  .then_inc(s["u_out"], 16)

            for dram, tile in ((w_self, wown[:, :, D:2 * D]), (s_w1, sw1[:, :, :]), (s_w2, sw2[:, :, :]),
                               (g_w, gw[:, :, :])):
                sp.dma_start(tile, dram.rearrange("(h p) c -> p h c", p=P))\
                  .then_inc(s["weights_in"], 16)
            for k in range(2, REL_LOADS):
                rel_load(k)
            for h in range(H):
                sp.dma_start(ew1[:, h, :, :], e_w1[:, h * P:(h + 1) * P, :].rearrange("e p c -> p e c"))\
                  .then_inc(s["weights_in"], 16)
            sp.dma_start(ew2[:, :, :], e_w2.rearrange("e p c -> p e c")).then_inc(s["weights_in"], 16)
            sp.dma_start(sw3[:, :], s_w3).then_inc(s["weights_in"], 16)
            sp.dma_start(ew3[:, :, :], e_w3.rearrange("e p c -> (e p) c").rearrange("(h q) c -> q h c", h=H))\
              .then_inc(s["weights_in"], 16)

            sp.wait_ge(s["mix_dve"], 1)
            for k in range(3):
                sp.dma_start(bias16[k:k + 1, :], bias_part[0:1, k, :]).then_inc(s["bias_parts"], 16)
            for buf in range(2):
                sp.wait_ge(xn_out[buf], CHUNKS[buf] * 16)
            sp.wait_ge(s["mixw_pe"], 3)

            def sp_g_and_m(t):
                m = MS * t - 2
                m_store(m)
                m_load(m + 1)
                m_store_q(m)
                m_store(m + 1)
                g_load(t, m + 2)
                m_load(m + 2)
                m_store_q(m + 1)
                m_store(m + 2)
                if not isinstance(t, int) or t < L1 - 1:
                    m_load(m + 3)
                m_store_q(m + 2)
                g_store(t)

            m_load(0)
            m_store(0)
            g_load(0, 1)
            m_load(1)
            m_store_q(0)
            g_store(0)
            with sp.Fori(1, L1 - 1) as i:
                sp_g_and_m(i)
            sp_g_and_m(L1 - 1)

            def p_load(p, stored):
                if not isinstance(p, int) or p:
                    sp.wait_ge(s["p_x1"], p)
                sp.dma_start(q2nt_p, q2nt_d[bass.ds(p, 1), :, :].rearrange("o p d -> (o p) d"))\
                  .then_inc(s["p_in"], 16)
                sp.wait_ge(s["u_out"], stored * 16)
                sp.dma_start(u_p, u_d[bass.ds(p, 1), :, :].rearrange("o p d -> (o p) d"))\
                  .then_inc(s["p_in"], 16)

            def p_store(p):
                sp.wait_ge(s["p_out"], p + 1)
                if isinstance(p, int) and p == T - 1:
                    sp.dma_start(out[(T - 1) * P:N, :], o_p[0:TAIL, :]).then_inc(s["out_done"], 16)
                else:
                    sp.dma_start(out[bass.ds(p * P, P), :], o_p).then_inc(s["out_done"], 16)

            sp.wait_ge(s["mix_dve"], 5)
            sp.wait_ge(s["m_q_out"], T * 16)

            def sp_g_and_p(j):
                t, p = 2 * j + L1, PS * j
                g_load(t, T)
                p_load(p + 1, t)
                p_store(p)
                g_store(t)
                g_load(t + 1, T)
                p_load(p + 2, t + 1)
                p_store(p + 1)
                if not isinstance(j, int) or j < J2 - 1:
                    p_load(p + 3, t + 1)
                p_store(p + 2)
                g_store(t + 1)

            p_load(0, L1)
            sp_g_and_p(0)
            with sp.Fori(1, J2 - 1) as j:
                sp_g_and_p(j)
            sp_g_and_p(J2 - 1)
            p_load(T - 1, T)
            p_store(T - 1)
            sp.wait_ge(s["out_done"], T * 16)
            for buf in range(2):
                sp.wait_ge(tab_out[buf], CHUNKS[buf] * 16)

        @block.gpsimd
        def _(pool):
            pool.memset(ones[:, :], 1.0).then_inc(s["idx_ready"], 1)
            pool.memset(zeros[:, :], 0.0).then_inc(s["idx_ready"], 1)
            pool.memset(hot_v[:, :], 1.0).then_inc(s["idx_ready"], 1)
            pool.memset(bad[:, :], 0.0).then_inc(s["idx_ready"], 1)
            pool.memset(gate[:, :], 1.0).then_inc(s["idx_ready"], 1)
            pool.memset(eps_ln[:, :], EPS_LN).then_inc(s["idx_ready"], 1)

            def ln_pool(n, buf):
                c = 2 * n + buf
                pool.wait_ge(s["hi_ready"], c + 1)
                pool.tensor_tensor(tabc[buf][:, :, D:2 * D], xnc[buf], tabc[buf][:, :, 0:D], ALU.subtract)\
                    .then_inc(s["lo_ready"], 1)

            ln_pool(0, 0)
            pool.wait_ge(s["row_ready"], 1)
            pool.indirect_dma_start(key_g[:, 0:ROW].bitcast(I32), None,
                                    dst.rearrange("(r c) -> r c", c=ROW),
                                    bass.IndirectOffsetOnAxis(ap=ei[0:NG, 0:1], axis=0),
                                    bounds_check=ROWS - 1, oob_is_err=False).then_inc(s["row_got"], 16)
            ln_pool(0, 1)
            pool.wait_ge(s["edges_pad"], 96)
            pool.wait_ge(s["start_ready"], 1)
            for full, own in ((dst_p, dst_g), (src_p, src_g), (typ_p, typ_g)):
                pool.indirect_dma_start(own, None,
                                        full[0:(EPAD // CAP) * CAP].rearrange("(r c) -> r c", c=CAP),
                                        bass.IndirectOffsetOnAxis(ap=ei[0:NG, 1:2], axis=1),
                                        bounds_check=E, oob_is_err=False).then_inc(s["edges_got"], 16)
            with pool.Fori(1, NC_P // 2) as k:
                ln_pool(k, 0)
                ln_pool(k, 1)
            ln_pool(NC_P // 2, 0)
            pool.wait_ge(s["turned_s"], 5)
            for buf in range(2):
                pool.wait_ge(tab_out[buf], CHUNKS[buf] * 16)
            for buf in range(2):
                pool.wait_ge(xn_out[buf], CHUNKS[buf] * 16)

            def gather(t, own):
                for g in range(GT):
                    if not isinstance(t, int) or t:
                        for r in range(g * BLOCKS // RB, (g + 1) * BLOCKS // RB):
                            pool.wait_ge(got[r], t * (RB * 16))
                    pool.tensor_copy(idx_now[:, g * BLOCKS:(g + 1) * BLOCKS],
                                     idx_t[:, bass.ds(GT * t + g, 1), :].rearrange("p o b -> p (o b)"))\
                        .then_inc(s["idx_ready"], 1)
                    pool.wait_ge(s["idx_ready"], GT * t + g + 7)
                    for b in range(g * BLOCKS, (g + 1) * BLOCKS):
                        if b % RB == 0:
                            if not isinstance(t, int) or t:
                                pool.wait_ge(s["blocks_used"], (t - 1) * TB + b + RB)
                                pool.sem_inc(s["batches"], 1)
                        pool.indirect_dma_start(ring[:, b, :], None, own,
                                                bass.IndirectOffsetOnAxis(ap=idx_now[:, b:b + 1], axis=0),
                                                bounds_check=own.shape[0] - 1, oob_is_err=False)\
                            .then_inc(got[b // RB], 16)

            pool.wait_ge(s["flag_ready"], 1)
            general = pool.value_load(flag[0:1, 0:1])
            with pool.If(general > 0):
                with pool.Fori(0, NG * PAIRS // (2 * P)) as k:
                    pool.dma_start(sums_d[bass.ds(k * (2 * P), 2 * P), :].rearrange("(p a) d -> p (a d)", a=2),
                                   zeros[:, :]).then_inc(s["gp_clear"], 16)
                pool.wait_ge(s["gp_clear"], NG * PAIRS // (2 * P) * 16)
                with pool.Fori(0, NEB) as k:
                    for j, full in enumerate((src_p, dst_p, typ_p)):
                        pool.dma_start(gp_i[:, j:j + 1], full[bass.ds(k * P, P)].rearrange("(p a) -> p a", a=1))\
                            .then_inc(s[f"gp_in{j}"], 16)
                    pool.wait_ge(s["gp_key"], k + 1)
                    pool.sem_inc(s["batches"], 1)
                    pool.indirect_dma_start(gp_rows, None, table[:, :],
                                            bass.IndirectOffsetOnAxis(ap=gp_i[:, 0:1], axis=0),
                                            bounds_check=NP - 1, oob_is_err=False).then_inc(s["gp_got"], 16)
                    pool.indirect_dma_start(gp_was, None, sums_d[:, :],
                                            bass.IndirectOffsetOnAxis(ap=gp_i[:, 3:4], axis=0),
                                            bounds_check=NG * PAIRS - 1, oob_is_err=False).then_inc(s["gp_got"], 16)
                    pool.wait_ge(s["gp_new"], k + 1)
                    pool.sem_inc(s["batches"], 1)
                    pool.indirect_dma_start(sums_d[:, :], bass.IndirectOffsetOnAxis(ap=gp_i[:, 4:5], axis=0), gp_new,
                                            None, bounds_check=NG * PAIRS - 1, oob_is_err=False)\
                        .then_inc(s["gp_out"], 16)
                    pool.wait_ge(s["gp_out"], k * 16 + 16)
                    pool.sem_inc(s["batches"], 1)
                with pool.Fori(0, NG * PAIRS // P) as k:
                    pool.dma_start(gp_was, sums_d[bass.ds(k * P, P), :]).then_inc(s["gp_row_in"], 16)
                    pool.wait_ge(s["gp_row_made"], k + 1)
                    pool.sem_inc(s["batches"], 1)
                    pool.dma_start(sums_t[bass.ds(k * (2 * P), 2 * P), :].rearrange("(p a) d -> p a d", a=2),
                                   gp_parts).then_inc(s["gp_row_out"], 16)
                    pool.wait_ge(s["gp_row_out"], k * 16 + 16)
                    pool.sem_inc(s["batches"], 1)
                blocks8 = idx_t[:, :, 0:2 * (GN // 8)].rearrange("p g (c a) -> p g c a", a=2)
                pool.iota(blocks8, [[2 * PAIRS, NG], [2 * P, GN // 8], [1, 2]], base=0, channel_multiplier=2)
                pool.iota(key_t[:, 0:NG, 0:2 * (GN // 8)].rearrange("p g (c a) -> p g c a", a=2),
                          [[0, NG], [P, GN // 8], [0, 2]], base=0, channel_multiplier=1,
                          allow_small_or_imprecise_dtypes=True)
                pool.memset(idx_t[:, :, 2 * (GN // 8):BLOCKS], 0)
                pool.memset(key_t[:, 0:NG, 2 * (GN // 8):BLOCKS], -1.0)
                pool.memset(hot_v[:, 0:2 * (GN // 8):2], SCALE)
                pool.drain().then_inc(s["gp_done"], 1)
                pool.wait_ge(s["gp_done"], 1)

                gather(0, sums_t)
                with pool.Fori(1, T) as t:
                    gather(t, sums_t)
            with pool.If(general < 1):
                gather(0, table)
                with pool.Fori(1, T) as t:
                    gather(t, table)

        @block.scalar
        def _(act):
            for row, tile in ((b_qkv[D:2 * D], bias_row[0:1, 0:D]), (b_qkv[0:D], bias_row[0:1, D:2 * D]),
                              (b_out, bias_row[0:1, 2 * D:3 * D]), (g_bias, bias_row[0:1, 3 * D:4 * D]),
                              (g_b, bias_row[0:1, 4 * D:BIAS]), (s_b3, b3[EX:EX + 1, :])):
                act.dma_start(tile, row.rearrange("(a c) -> a c", a=1)).then_inc(s["bias_in"], 16)
            act.dma_start(b3[0:EX, :], e_b3).then_inc(s["bias_in"], 16)
            with nc.allow_non_contiguous_dma(reason="biases as columns"):
                for col, tile in ((s_b1.rearrange("(h p) -> p h", p=P), b1_col[:, 0:H]),
                                  (e_b1.rearrange("e p -> p e"), b1_col[:, H:H + EX]),
                                  (s_b2.rearrange("(a p) -> p a", p=P), b2_col[:, 0:1]),
                                  (e_b2.rearrange("e p -> (e p)").rearrange("(h q) -> q h", h=H), b2_col[:, 1:1 + H]),
                                  (b_qkv[2 * D:3 * D].rearrange("(h p) -> p h", p=P), bv_col[:, :])):
                    act.dma_start(tile, col).then_inc(s["bias_in"], 16)

            act.wait_ge(s["idx_ready"], 6)

            def ln_act(n, buf):
                c = 2 * n + buf
                act.wait_ge(s["ln_done"], c + 1)
                act.activation(rstd[:, :], mv[:, :, 1], ACT.Sqrt, bias=eps_ln[:, 0:1]).then_inc(s["sd_ready"], 1)
                act.wait_ge(s["xn_ready"], c + 1)
                if not isinstance(n, int) or n:
                    act.wait_ge(tab_out[buf], n * 16)
                act.activation(tabc[buf][:, :, 0:D], xnc[buf], ACT.Copy).then_inc(s["hi_ready"], 1)

            ln_act(0, 0)
            ln_act(0, 1)
            act.wait_ge(s["edges_pad"], 96)
            act.dma_start(nxt, dst_p[1:E + 1].rearrange("(r c) -> r c", c=ROW)).then_inc(s["next_in"], 16)
            with act.Fori(1, NC_P // 2) as k:
                ln_act(k, 0)
                ln_act(k, 1)

            act.wait_ge(s["edges_got"], 48)
            act.activation(srcf_g, src_g, ACT.Copy).then_inc(s["srcf_ready"], 1)
            ln_act(NC_P // 2, 0)
            for k in range(5):
                act.wait_ge(s["turned"], k + 1)
                b0, nb = 4 * k, min(4, BLOCKS - 4 * k)
                act.activation(idx_t[:, :, b0:b0 + nb].rearrange("p g b -> p b g"),
                               banks[k][:, 0:nb * P].rearrange("p (b c) -> p b c", c=P)[:, :, 0:NG], ACT.Copy)\
                    .then_inc(s["turned_s"], 1)

            act.wait_ge(s["turned_k"], 5)
            for k in range(REL_LOADS):
                h, r0 = k * RH // R, k * RH % R
                act.wait_ge(rel_in[k % 2], (k // 2 + 1) * 16)
                act.activation(wr[:, 0, h, r0:r0 + RH, :], wstage[k % 2], ACT.Copy, scale=SCALE)\
                    .then_inc(s["prep_act"], 1)
                act.activation(wr[:, 2, h, r0:r0 + RH, :], wstage[k % 2], ACT.Copy)\
                    .then_inc(s["prep_act"], 1)

            def hi_part(t, g, q):
                n0 = g * GN + q * BANK_N
                act.wait_ge(s["blocks_used"], t * TB + g * BLOCKS + (LAST0, BLOCKS - 1)[q] + 1)
                if g + q == 0 and (not isinstance(t, int) or t):
                    act.wait_ge(s["w_done"], t)
                for h in range(H):
                    act.activation(s_hi[:, h, :, n0:n0 + BANK_N].rearrange("p r n -> p n r"),
                                   banks[2 * q + h][:, :].rearrange("p (n r) -> p n r", r=R),
                                   ACT.Copy, scale=1.0 / SCALE).then_inc(s["hi_done"], 1)

            def m_act(m, step):
                later = not isinstance(m, int) or m > 0
                if step == "xt":
                    act.wait_ge(s["m_turned"], m + 1)
                    if later:
                        act.wait_ge(s["m_xnt_out"], m * 16)
                    act.activation(xnt_m, B7[:, 0:D], ACT.Copy).then_inc(s["m_xnt"], 1)
                elif step == "sq":
                    act.wait_ge(s["m_k"], m + 1)
                    if later:
                        act.wait_ge(s["m_sum"], m)
                    act.activation(q2, B5[:, D:2 * D], ACT.Square, accum_out=stat[:, 3:4]).then_inc(s["m_q2"], 1)
                    act.activation(k2, B5[:, 0:D], ACT.Square, accum_out=stat[:, 0:1]).then_inc(s["m_k2"], 1)
                    act.wait_ge(s["m_q2"], m + 1)
                    act.activation(q4, q2, ACT.Square, accum_out=stat[:, 4:5]).then_inc(s["m_q4"], 1)
                    act.wait_ge(s["m_q4"], m + 1)
                    act.activation(stat[:, 5:6], stat[:, 4:5], ACT.Sqrt).then_inc(s["m_nb"], 1)
                elif step == "k4":
                    act.wait_ge(s["m_k2n"], m + 1)
                    act.activation(k4, k2n, ACT.Square).then_inc(s["m_k4"], 1)
                else:
                    act.wait_ge(s["m_qt"], m + 1)
                    if later:
                        act.wait_ge(s["m_q_out"], m * 16)
                    act.activation(q2nt, B7[:, D:2 * D], ACT.Copy).then_inc(s["m_qtc"], 1)

            M_AT = {1: "xt", 4: "sq", 6: "k4", 10: "qt"}

            def g_and_m(t, ms):
                for b in range(TB):
                    if b % MSLOT in M_AT and ms[b // MSLOT] is not None:
                        m_act(ms[b // MSLOT], M_AT[b % MSLOT])
                    if b % BLOCKS == LAST0:
                        hi_part(t, b // BLOCKS, 0)
                    if b % BLOCKS == BLOCKS - 1:
                        hi_part(t, b // BLOCKS, 1)

            g_and_m(0, (None, None, 0))
            with act.Fori(1, L1 - 1) as t:
                g_and_m(t, (MS * t - 2, MS * t - 1, MS * t))
            g_and_m(L1 - 1, (T - 3, T - 2, T - 1))

            act.wait_ge(s["mix_dve"], 3)
            act.activation(pcol[:, 4:6], pcol[:, 0:2], ACT.Sqrt).then_inc(s["mix_act"], 1)

            def p_act(p, step):
                if step == "sd":
                    act.wait_ge(s["p_ln"], p + 1)
                    act.activation(stat[:, 6:7], stat[:, 17:18], ACT.Sqrt, bias=eps_ln[:, 0:1])\
                        .then_inc(s["p_sd"], 1)
                elif step == "xt":
                    act.wait_ge(s["p_xt"], p + 1)
                    act.activation(xn2t, B6[:, 0:D], ACT.Copy).then_inc(s["p_xtc"], 1)
                elif step == "h1s":
                    act.wait_ge(s["p_h1s"], p + 1)
                    for j in range(H):
                        act.activation(h1[:, j, :], B6[:, j * P:(j + 1) * P], ACT.Relu,
                                       bias=b1_col[:, j:j + 1]).then_inc(s["p_h1"], 1)
                elif step == "h1e":
                    act.wait_ge(s["p_h1e"], p + 1)
                    for j in range(EX):
                        act.activation(h1[:, H + j, :], B5[:, j * P:(j + 1) * P], ACT.Relu,
                                       bias=b1_col[:, H + j:H + j + 1]).then_inc(s["p_h1"], 1)
                elif step == "exp":
                    act.wait_ge(s["p_max"], p + 1)
                    act.activation(gate[:, 4:8], gate[:, 0:4], ACT.Exp, bias=stat[:, 8:9],
                                   accum_out=stat[:, 9:10]).then_inc(s["p_exp"], 1)
                elif step == "exp2":
                    act.wait_ge(s["p_gmax"], p + 1)
                    act.activation(gate[:, 12:16], gate[:, 8:12], ACT.Exp, bias=stat[:, 11:12])\
                        .then_inc(s["p_exp2"], 1)
                elif step == "h2":
                    act.wait_ge(s["p_l2"], p + 1)
                    act.activation(h2s, B6[:, 0:P], ACT.Relu, bias=b2_col[:, 0:1]).then_inc(s["p_h2"], 1)
                    for j in range(H):
                        act.activation(h2[:, j * P:(j + 1) * P], B6[:, (1 + j) * P:(2 + j) * P], ACT.Relu,
                                       bias=b2_col[:, 1 + j:2 + j]).then_inc(s["p_h2"], 1)

            STEPS = ["sd", "xt", "exp", "h1s", "exp2", "h1e", "h2"]
            AT = ACT_AT

            def g_and_p(t, half, p0):
                for b in range(TB):
                    slot = half * TB + b
                    for k, a in enumerate(AT[slot // PSLOT]):
                        if slot % PSLOT == a:
                            p_act(p0 + slot // PSLOT, STEPS[k])
                    if b % BLOCKS == LAST0:
                        hi_part(t, b // BLOCKS, 0)
                    if b % BLOCKS == BLOCKS - 1:
                        hi_part(t, b // BLOCKS, 1)

            g_and_p(L1, 0, 0)
            g_and_p(L1 + 1, 1, 0)
            with act.Fori(1, J2) as j:
                g_and_p(2 * j + L1, 0, PS * j)
                g_and_p(2 * j + (L1 + 1), 1, PS * j)
            for k in STEPS:
                p_act(T - 1, k)

        @block.vector
        def _(dve):
            chain = {"n": 0}

            def link(ins):
                chain["n"] += 1
                ins.then_inc(s["dve_c"], 1)
                dve.wait_ge(s["dve_c"], chain["n"])

            def ln_dve(n, buf):
                c = 2 * n + buf
                last = isinstance(n, int) and c == NC_P - 1
                dve.wait_ge(x_in[buf], (n + 1 + last) * 16)
                K = 2 * CH + 1
                base = c * K
                for j in range(CH):
                    dve.bn_stats(st[:, j, :], xc[buf][:, j, :]).then_inc(s["dve_p"], 1)
                dve.wait_ge(s["dve_p"], base + CH)
                dve.memset(carrier[:, :], 0.0)
                for j in range(CH):
                    dve.bn_aggr(mv[:, j, :], st[:, j, :]).then_inc(s["dve_p"], 1)
                dve.wait_ge(s["dve_p"], base + 2 * CH)
                dve.nop().then_inc(s["ln_done"], 1)
                dve.wait_ge(s["sd_ready"], c + 1)
                dve.reciprocal(rstd[:, :], rstd[:, :]).then_inc(s["dve_p"], 1)
                dve.wait_ge(s["dve_p"], base + 2 * CH + 1)
                if not isinstance(n, int) or n:
                    dve.wait_ge(xn_out[buf], n * 16)
                    dve.wait_ge(s["lo_ready"], c - 1)
                for j in range(CH):
                    ins = dve.tensor_scalar(xnc[buf][:, j, :], xc[buf][:, j, :], mv[:, j, 0:1], rstd[:, j:j + 1],
                                            ALU.subtract, ALU.mult)
                ins.then_inc(s["xn_ready"], 1)

            first_node = group_c[0:NG, 2 * BLOCKS:2 * BLOCKS + 1]
            dve.wait_ge(s["rows_in"], 16)
            dve.tensor_copy(rfb[:, :], rows[:, 0:1].to_broadcast([ROWS, NG])).then_inc(s["rf_ready"], 1)
            ln_dve(0, 0)
            dve.wait_ge(s["consts_in"], 64)
            dve.wait_ge(s["idx_ready"], 6)
            dve.wait_ge(s["rf_wide"], 1)
            link(dve.tensor_scalar(rfb[0:NG, 0:NG], banks[0][0:NG, 0:NG], first_node, None, ALU.is_lt, ALU.add,
                                   accum_out=ec[0:NG, 1:2]))
            link(dve.tensor_scalar(rfb[0:NG, 0:ROWS - NG], banks[0][0:NG, NG:ROWS], first_node, None, ALU.is_lt,
                                   ALU.add, accum_out=ec[0:NG, 2:3]))
            link(dve.tensor_tensor(ec[0:NG, 3:4], ec[0:NG, 1:2], ec[0:NG, 2:3], ALU.add))
            link(dve.tensor_scalar(ec[0:NG, 4:5], ec[0:NG, 3:4], -1.0, 0.0, ALU.add, ALU.max))
            dve.tensor_copy(ei[0:NG, 0:1], ec[0:NG, 4:5]).then_inc(s["row_ready"], 1)
            ln_dve(0, 1)
            dve.wait_ge(s["row_got"], 16)
            row_f = srcf_g[:, 0:ROW]
            link(dve.tensor_copy(row_f, key_g[:, 0:ROW].bitcast(I32)))
            link(dve.tensor_scalar(key_g[:, 0:ROW], row_f, first_node, None, ALU.is_lt, ALU.add,
                                   accum_out=ec[0:NG, 5:6]))
            dve.scalar_tensor_tensor(ei[0:NG, 1:2], ec[0:NG, 4:5], float(ROW), ec[0:NG, 5:6], ALU.mult, ALU.add)\
                .then_inc(s["start_ready"], 1)
            with dve.Fori(1, NC_P // 2) as k:
                ln_dve(k, 0)
                ln_dve(k, 1)
            dve.memset(xc[0][96:P, CH - 1, :], 0.0).then_inc(s["pad_made"], 1)

            dve.wait_ge(s["edges_got"], 48)
            rel = dst_g.bitcast(F32)
            link(dve.tensor_scalar(rel, dst_g, first_node, None, ALU.subtract))
            dve.scalar_tensor_tensor(key_g, rel, float(R), typ_g, ALU.mult, ALU.add).then_inc(s["edges_kf"], 1)
            in_block = rel.rearrange("p (b c) -> p b c", c=P)
            link(dve.tensor_tensor(gate[0:NG, 0:BLOCKS], in_block[:, :, P - 1], group_c[0:NG, BLOCKS:2 * BLOCKS],
                                   ALU.is_ge))
            link(dve.tensor_tensor(gate[0:NG, BLOCKS:2 * BLOCKS], in_block[:, :, 0], group_c[0:NG, 0:BLOCKS],
                                   ALU.is_lt))
            link(dve.tensor_reduce(bad[0:NG, 1:2], gate[0:NG, 0:2 * BLOCKS], AX.X, ALU.add))
            link(dve.tensor_scalar(bad[0:NG, 2:3], rel[:, CAP - 1:CAP], float(GN), None, ALU.is_lt))
            ln_dve(NC_P // 2, 0)
            dve.wait_ge(s["next_in"], 16)
            nxt_f = nxt.bitcast(F32)
            link(dve.tensor_tensor(nxt_f, nxt, rows, ALU.subtract))
            link(dve.tensor_reduce(ec[0:ROWS, 0:1], nxt_f, AX.X, ALU.min))
            dve.tensor_scalar(bad[0:ROWS, 0:1], ec[0:ROWS, 0:1], 0.0, None, ALU.is_lt).then_inc(s["bad_ready"], 1)
            dve.wait_ge(s["flag_sum"], 1)
            link(dve.tensor_reduce(flag_f[:, :], banks[2][0:1, 0:4], AX.X, ALU.add))
            dve.tensor_copy(flag[:, :], flag_f[:, :]).then_inc(s["flag_ready"], 1)
            for k in range(5):
                dve.wait_ge(s["turned"], 5 + k + 1)
                b0, nb = 4 * k, min(4, BLOCKS - 4 * k)
                dve.tensor_copy(key_t[:, 0:NG, b0:b0 + nb].rearrange("p g b -> p b g"),
                                banks[(5 + k) % 8][:, 0:nb * P].rearrange("p (b c) -> p b c", c=P)[:, :, 0:NG])\
                    .then_inc(s["turned_k"], 1)
            dve.wait_ge(s["turned_k"], 5)
            dve.memset(gate[:, :], 1.0).then_inc(s["prep_dve"], 1)
            dve.memset(key_t[:, NG:NG + GT, :], -1.0).then_inc(s["prep_dve"], 1)
            dve.wait_ge(s["prep_dve"], 2)
            for buf in range(2):
                dve.wait_ge(xn_out[buf], CHUNKS[buf] * 16)

            def weights_dve(step):
                if step < REL_LOADS:
                    h, r0 = step * RH // R, step * RH % R
                    dve.wait_ge(s["prep_act"], 2 * step + 2)
                    dve.scalar_tensor_tensor(wr[:, 1, h, r0:r0 + RH, :].rearrange("p r d -> p (r d)"),
                                             wstage[step % 2].rearrange("p r d -> p (r d)"), SCALE,
                                             wr[:, 0, h, r0:r0 + RH, :].rearrange("p r d -> p (r d)"),
                                             ALU.mult, ALU.subtract).then_inc(s["rel_lo"], 1)
                elif step < REL_LOADS + H:
                    h = step - REL_LOADS
                    dve.wait_ge(s["mixing_in"], 2 * 16)
                    for c, dest in ((0, wkq[:, h, D:2 * D]), (1, wkq[:, h, 0:D])):
                        link(dve.tensor_reduce(ec[:, 6:7], wq_s[:, h, c * D:(c + 1) * D], AX.X, ALU.add))
                        link(dve.tensor_scalar(ec[:, 7:8], ec[:, 6:7], 1.0 / D, None, ALU.mult))
                        link(dve.tensor_scalar(dest, wq_s[:, h, c * D:(c + 1) * D], ec[:, 7:8], None,
                                               ALU.subtract))
                elif step == REL_LOADS + H:
                    dve.wait_ge(s["bias_in"], 12 * 16)
                    for row in (bias_row[0:1, 0:D], bias_row[0:1, D:2 * D]):
                        link(dve.tensor_reduce(ec[0:1, 6:7], row, AX.X, ALU.add))
                        link(dve.tensor_scalar(ec[0:1, 7:8], ec[0:1, 6:7], 1.0 / D, None, ALU.mult))
                        link(dve.tensor_scalar(row, row, ec[0:1, 7:8], None, ALU.subtract))
                elif step == REL_LOADS + H + 1:
                    dve.wait_ge(s["mixw_pe"], 2)
                    link(dve.tensor_copy(wvo, B6[:, :].rearrange("p (a b) -> p a b", b=D)))
                    link(dve.tensor_copy(bvo_b[:, :], B7[:, 0:D]))
                    link(dve.tensor_tensor(bias_row[0:1, 2 * D:3 * D], bias_row[0:1, 2 * D:3 * D], bvo_b[0:1, :],
                                           ALU.add))
                    link(dve.memset(ones16[:, :], 1.0))
                    link(dve.tensor_copy(bias_part[0:1, 0, :], bias_row[0:1, :]))
                else:
                    link(dve.tensor_tensor(bias_left[0:1, :], bias_row[0:1, :], bias_part[0:1, 0, :], ALU.subtract))
                    link(dve.tensor_copy(bias_part[0:1, 1, :], bias_left[0:1, :]))
                    link(dve.tensor_tensor(bias_part[0:1, 2, :], bias_left[0:1, :], bias_part[0:1, 1, :],
                                           ALU.subtract))
                    link(dve.memset(work[:, 9:11, :], 0.0))
                    dve.nop().then_inc(s["mix_dve"], 1)

            def keys(t, b0, b1, n):
                for g in range(b0 // BLOCKS, (b1 - 1) // BLOCKS + 1):
                    lo, hi = max(b0, g * BLOCKS), min(b1, (g + 1) * BLOCKS)
                    ins = dve.tensor_copy(key_now[:, lo:hi], key_t[:, bass.ds(GT * t + g, 1), lo - g * BLOCKS:hi - g * BLOCKS]
                                          .rearrange("p o b -> p (o b)"))
                ins.then_inc(s["keys_ready"], 1)
                dve.wait_ge(s["keys_ready"], n)

            def one_hot(t, b):
                lo, hi = WIN[b % BLOCKS]
                w = (hi - lo) * R
                if b >= OH or not isinstance(t, int) or t:
                    dve.wait_ge(s["blocks_used"], t * TB + b - OH + 1)
                dve.tensor_scalar(hot[:, b % OH, 0:w], iota16[:, lo * R:hi * R], key_now[:, b:b + 1],
                                  hot_v[:, b % BLOCKS:b % BLOCKS + 1], ALU.is_equal, ALU.mult)\
                    .then_inc(s["hot_ready"], 1)

            def next_hot(t, b):
                if b == 0:
                    keys(t, AHEAD, TB, 2 * t + 2)
                if b == TB - AHEAD:
                    keys(t + 1, 0, AHEAD, 2 * t + 3)
                if b < TB - AHEAD:
                    one_hot(t, b + AHEAD)
                else:
                    one_hot(t + 1, b + AHEAD - TB)

            def lo_part(t, g, q):
                n0 = g * GN + q * BANK_N
                for h in range(H):
                    dve.wait_ge(s["hi_done"], (4 * t + 2 * g + q) * H + h + 1)
                    dve.scalar_tensor_tensor(
                        s_lo[:, h, :, n0:n0 + BANK_N].rearrange("p r n -> p n r"),
                        s_hi[:, h, :, n0:n0 + BANK_N].rearrange("p r n -> p n r"), -SCALE,
                        banks[2 * q + h][:, :].rearrange("p (n r) -> p n r", r=R), ALU.mult, ALU.add)\
                        .then_inc(s["lo_done"], 1)

            def u_part(t):
                dve.wait_ge(s["w_done"], t + 1)
                if not isinstance(t, int) or t:
                    dve.wait_ge(s["u_out"], t * 16)
                dve.scalar_tensor_tensor(u_g[:, :], GB[:, D:2 * D], 0.0, x_g[:, :], ALU.max, ALU.add)\
                    .then_inc(s["u_half"], 1)
                dve.wait_ge(s["u_half"], t + 1)
                dve.tensor_tensor(u_g[:, :], u_g[:, :], GB[:, 0:D], ALU.add).then_inc(s["u_ready"], 1)

            NM = 6

            def m_dve(m, step, mask):
                inside = post_c[:, 16 + P * H:17 + P * H] if mask else ones[:, 0:1]
                later = not isinstance(m, int) or m > 0

                def mlink(n, ins):
                    ins.then_inc(s["dve_m"], 1)
                    dve.wait_ge(s["dve_m"], m * NM + n)

                if step == "k":
                    dve.wait_ge(s["m_k2"], m + 1)
                    mlink(1, dve.tensor_scalar(stat[:, 1:2], stat[:, 0:1], EPS_DIV, None, ALU.add))
                    mlink(2, dve.reciprocal(stat[:, 2:3], stat[:, 1:2]))
                    if later:
                        dve.wait_ge(s["m_used"], m)
                    dve.tensor_scalar(k2n, k2, stat[:, 2:3], inside, ALU.mult, ALU.mult).then_inc(s["m_k2n"], 1)
                    dve.wait_ge(s["m_nb"], m + 1)
                    mlink(3, dve.tensor_scalar(stat[:, 6:7], stat[:, 3:4], EPS_DIV, None, ALU.add))
                    mlink(4, dve.reciprocal(stat[:, 7:8], stat[:, 6:7]))
                    mlink(5, dve.tensor_scalar(stat[:, 8:9], stat[:, 5:6], stat[:, 7:8], EPS_NORM, ALU.mult, ALU.max))
                    mlink(6, dve.reciprocal(stat[:, 9:10], stat[:, 8:9]))
                    if later:
                        dve.wait_ge(s["m_qt"], m)
                    dve.tensor_scalar(q2n, q2, stat[:, 7:8], stat[:, 9:10], ALU.mult, ALU.mult)\
                        .then_inc(s["m_q2n"], 1)
                else:
                    if later:
                        dve.wait_ge(s["m_sum"], m)
                    dve.tensor_tensor(k2n_sum, k2n_sum, k2n, ALU.add)
                    dve.wait_ge(s["m_k4"], m + 1)
                    dve.tensor_tensor(k4_sum, k4_sum, k4, ALU.add).then_inc(s["m_sum"], 1)

            M_AT = {5: "k", 8: "sum"}
            WEIGHTS_AT = [0, 1, 2, 3, 4, 5, 6, 7, 8, 9, 11, 12, 14]

            def g_and_m(t, ms, u_late=True, weights=False):
                for b in range(TB):
                    next_hot(t, b)
                    if b == U_AT and u_late:
                        u_part(t - 1)
                    if weights and b in WEIGHTS_AT:
                        weights_dve(WEIGHTS_AT.index(b))
                    if b % MSLOT in M_AT and ms[b // MSLOT] is not None:
                        m = ms[b // MSLOT]
                        m_dve(m, M_AT[b % MSLOT], isinstance(m, int) and m == T - 1)
                    if b % BLOCKS == LAST0 + 1:
                        lo_part(t, b // BLOCKS, 0)
                    if b == BLOCKS:
                        lo_part(t, 0, 1)
                lo_part(t, 1, 1)

            general = dve.value_load(flag[0:1, 0:1])
            with dve.If(general > 0):
                with dve.Fori(0, NEB) as k:
                    NL = 6

                    def step(n, ins):
                        ins.then_inc(s["dve_g"], 1)
                        dve.wait_ge(s["dve_g"], k * NL + n)

                    for j in range(3):
                        dve.wait_ge(s[f"gp_in{j}"], k * 16 + 16)
                    step(1, dve.scalar_tensor_tensor(gp_f[:, 0:1], gp_i[:, 1:2], float(R), gp_i[:, 2:3], ALU.mult,
                                                     ALU.add))
                    dve.tensor_copy(gp_keys, gp_f[:, 0:1].to_broadcast([P, P]))
                    dve.tensor_copy(gp_i[:, 3:4], gp_f[:, 0:1]).then_inc(s["gp_key"], 1)
                    dve.wait_ge(s["gp_wide"], k + 1)
                    step(2, dve.tensor_scalar(gp_same, banks[0][:, 0:P], gp_f[:, 0:1], None, ALU.is_equal))
                    dve.nop().then_inc(s["gp_made"], 1)
                    step(3, dve.tensor_tensor(gp_earlier, gp_same, post_c[:, POST_C - P:], ALU.mult))
                    step(4, dve.tensor_reduce(gp_f[:, 1:2], gp_earlier, AX.X, ALU.max))
                    step(5, dve.tensor_scalar(gp_f[:, 2:3], gp_f[:, 1:2], float(2 ** 20), gp_f[:, 0:1], ALU.mult,
                                              ALU.add))
                    dve.wait_ge(s["gp_sum"], k + 1)
                    dve.wait_ge(s["gp_got"], k * 32 + 32)
                    step(6, dve.tensor_tensor(gp_new, gp_was, banks[1][:, 0:D], ALU.add))
                    dve.tensor_copy(gp_i[:, 4:5], gp_f[:, 2:3]).then_inc(s["gp_new"], 1)
                dve.memset(gp_parts, 0.0).then_inc(s["dve_g"], 1)
                dve.wait_ge(s["dve_g"], NEB * 6 + 1)
                with dve.Fori(0, NG * PAIRS // P) as k:
                    NR = 3

                    def step(n, ins):
                        ins.then_inc(s["dve_g"], 1)
                        dve.wait_ge(s["dve_g"], k * NR + (NEB * 6 + 1 + n))

                    dve.wait_ge(s["gp_row_in"], k * 16 + 16)
                    step(1, dve.tensor_scalar(gp_parts[:, 0, 0:D], gp_was, 1.0 / SCALE, None, ALU.mult))
                    step(2, dve.scalar_tensor_tensor(gp_left, gp_parts[:, 0, 0:D], -SCALE, gp_was, ALU.mult, ALU.add))
                    step(3, dve.tensor_copy(gp_parts[:, 1, 0:D], gp_left))
                    dve.tensor_tensor(gp_parts[:, 1, D:2 * D], gp_left, gp_parts[:, 1, 0:D], ALU.subtract)\
                        .then_inc(s["gp_row_made"], 1)
                dve.wait_ge(s["gp_done"], 1)
                dve.memset(carrier[:, :], 0.0)

            keys(0, 0, AHEAD, 1)
            for b in range(AHEAD):
                one_hot(0, b)
            dve.wait_ge(s["bias_in"], 12 * 16)
            dve.wait_ge(s["mixw_pe"], 1)
            link(dve.tensor_copy(wvt_s, B5[:, :].rearrange("p (a b) -> p a b", b=D)))
            for h in range(H):
                link(dve.tensor_copy(bvb[:, h, :], bv_col[:, h:h + 1].to_broadcast([P, P])))
            dve.nop().then_inc(s["prep_dve"], 1)
            g_and_m(0, (None, None, 0), u_late=False, weights=True)
            g_and_m(1, (1, 2, 3))
            with dve.Fori(2, L1 - 1) as t:
                g_and_m(t, (MS * t - 2, MS * t - 1, MS * t))
            g_and_m(L1 - 1, (T - 3, T - 2, T - 1))
            u_part(L1 - 1)

            dve.wait_ge(s["m_used"], T)
            dve.wait_ge(s["m_xnt_out"], T * 16)
            yt = work[:, 0:2, :]
            dve.wait_ge(s["m_sum"], T)
            link(dve.tensor_copy(yt, B6[:, :].rearrange("p (a b) -> p a b", b=D)))
            dve.wait_ge(s["mix_pe"], 1)
            link(dve.tensor_copy(pcol[:, 0:4], B7[:, 0:4]))
            dve.nop().then_inc(s["mix_dve"], 2)
            dve.wait_ge(s["mix_act"], 1)
            link(dve.tensor_scalar(pcol[:, 4:6], pcol[:, 4:6], EPS_NORM, None, ALU.max))
            link(dve.reciprocal(pcol[:, 6:8], pcol[:, 4:6]))
            link(dve.tensor_scalar(pcol[:, 6:8], pcol[:, 6:8], 1.0 / sqrt(N), None, ALU.mult))
            dve.wait_ge(s["mix_pe"], 2)
            for h in range(H):
                link(dve.scalar_tensor_tensor(m1[:, h, :], bvo_b[:, :], pcol[:, 2 + h:3 + h],
                                              B5[:, h * D:(h + 1) * D], ALU.mult, ALU.add))
                link(dve.tensor_scalar(m1[:, h, :], m1[:, h, :], pcol[:, 6 + h:7 + h], None, ALU.mult))
            dve.nop().then_inc(s["mix_dve"], 2)

            NPC = 16
            pchain = {"n": 0}

            def plink(p, ins):
                pchain["n"] += 1
                ins.then_inc(s["dve_c2"], 1)
                dve.wait_ge(s["dve_c2"], p * NPC + pchain["n"])

            def p_dve(p, step):
                if step == "x1":
                    pchain["n"] = 0
                    dve.wait_ge(s["p_mix"], p + 1)
                    dve.wait_ge(s["p_in"], (p + 1) * 32)
                    dve.tensor_tensor(x1, B5[:, 0:D], u_p, ALU.add).then_inc(s["p_x1"], 1)
                    dve.wait_ge(s["p_x1"], p + 1)
                    pchain["n"] += 1
                    dve.bn_stats(stat[:, 18:24], x1).then_inc(s["dve_c2"], 1)
                    dve.wait_ge(s["dve_c2"], p * NPC + pchain["n"])
                    dve.memset(carrier[:, :], 0.0)
                    dve.bn_aggr(stat[:, 16:18], stat[:, 18:24]).then_inc(s["p_ln"], 1)
                elif step == "xn2":
                    dve.wait_ge(s["p_sd"], p + 1)
                    plink(p, dve.reciprocal(stat[:, 7:8], stat[:, 6:7]))
                    dve.tensor_scalar(xn2, x1, stat[:, 16:17], stat[:, 7:8], ALU.subtract, ALU.mult)\
                        .then_inc(s["p_xn2"], 1)
                elif step == "max":
                    dve.wait_ge(s["p_log"], p + 1)
                    plink(p, dve.tensor_copy(gate[:, 0:4], B7[:, 0:4]))
                    plink(p, dve.tensor_reduce(stat[:, 10:11], gate[:, 0:4], AX.X, ALU.max))
                    dve.tensor_scalar(stat[:, 8:9], stat[:, 10:11], -1.0, None, ALU.mult).then_inc(s["p_max"], 1)
                elif step == "gate":
                    dve.wait_ge(s["p_exp"], p + 1)
                    plink(p, dve.reciprocal(stat[:, 12:13], stat[:, 9:10]))
                    plink(p, dve.tensor_scalar(gate[:, 8:12], gate[:, 4:8], stat[:, 12:13], None, ALU.mult))
                    plink(p, dve.tensor_reduce(stat[:, 13:14], gate[:, 8:12], AX.X, ALU.max))
                    dve.tensor_scalar(stat[:, 11:12], stat[:, 13:14], -1.0, None, ALU.mult).then_inc(s["p_gmax"], 1)
                    other = gate[:, 8:12].unsqueeze(1).to_broadcast([P, EX, EX])
                    own = gate[:, 8:12].unsqueeze(2).to_broadcast([P, EX, EX])
                    gt = gate[:, 16:32].rearrange("p (a b) -> p a b", b=EX)
                    eq = gate[:, 32:48].rearrange("p (a b) -> p a b", b=EX)
                    before = post_c[:, 0:16].rearrange("p (a b) -> p a b", b=EX)
                    plink(p, dve.tensor_tensor(gt, other, own, ALU.is_gt))
                    plink(p, dve.tensor_tensor(eq, other, own, ALU.is_equal))
                    plink(p, dve.tensor_tensor(eq, eq, before, ALU.mult))
                    plink(p, dve.tensor_tensor(gt, gt, eq, ALU.add))
                    plink(p, dve.tensor_reduce(gate[:, 48:52], gt, AX.X, ALU.add))
                    plink(p, dve.tensor_scalar(gate[:, 52:56], gate[:, 48:52], 2.0, None, ALU.is_lt))
                elif step == "gate2":
                    dve.wait_ge(s["p_exp2"], p + 1)
                    plink(p, dve.tensor_tensor(gate[:, 56:60], gate[:, 52:56], gate[:, 12:16], ALU.mult))
                    plink(p, dve.tensor_reduce(stat[:, 14:15], gate[:, 56:60], AX.X, ALU.add))
                    plink(p, dve.reciprocal(stat[:, 15:16], stat[:, 14:15]))
                    dve.tensor_scalar(gate[:, 60:64], gate[:, 56:60], stat[:, 15:16], None, ALU.mult)\
                        .then_inc(s["p_w5"], 1)
                elif step == "wt":
                    dve.wait_ge(s["p_wt"], p + 1)
                    dve.tensor_copy(w5t[:, :], B7[0:EX + 1, D:D + P]).then_inc(s["p_wtc"], 1)
                elif step == "h2g":
                    dve.wait_ge(s["p_h2"], 3 * p + 3)
                    dve.wait_ge(s["p_wb"], p + 1)
                    dve.tensor_tensor(h2g, h2, B7[:, 0:D], ALU.mult).then_inc(s["p_h2g"], 1)
                elif step == "out":
                    dve.wait_ge(s["p_l3"], p + 1)
                    if not isinstance(p, int) or p:
                        dve.wait_ge(s["out_done"], p * 16)
                    dve.tensor_tensor(o_p, x1, B5[:, 0:D], ALU.add).then_inc(s["p_out"], 1)

            STEPS = ["x1", "xn2", "max", "gate", "gate2", "wt", "h2g", "out"]
            AT = DVE_AT

            def g_and_p(t, half, p0, u_late=True):
                for b in range(TB):
                    slot = half * TB + b
                    next_hot(t, b)
                    if b == U_AT and u_late:
                        u_part(t - 1)
                    for k, a in enumerate(AT[slot // PSLOT]):
                        if slot % PSLOT == a:
                            p_dve(p0 + slot // PSLOT, STEPS[k])
                    if b % BLOCKS == LAST0 + 1:
                        lo_part(t, b // BLOCKS, 0)
                    if b == BLOCKS:
                        lo_part(t, 0, 1)
                lo_part(t, 1, 1)

            g_and_p(L1, 0, 0, u_late=False)
            g_and_p(L1 + 1, 1, 0)
            with dve.Fori(1, J2) as j:
                g_and_p(2 * j + L1, 0, PS * j)
                g_and_p(2 * j + (L1 + 1), 1, PS * j)
            u_part(T - 1)
            for k in STEPS:
                p_dve(T - 1, k)
            assert pchain["n"] == NPC

        @block.tensor
        def _(pe):
            mm = nc.tensor.matmul

            pe.wait_ge(s["consts_in"], 64)
            pe.wait_ge(s["rf_ready"], 1)
            mm(banks[0][0:NG, 0:ROWS], rfb[:, 0:NG], ident[0:ROWS, 0:ROWS], start=True, stop=True)\
                .then_inc(s["rf_wide"], 1)

            def turn(k, source, bank):
                for j in range(min(4, BLOCKS - 4 * k)):
                    b = 4 * k + j
                    last = nc.tensor.transpose(bank[:, j * P:j * P + NG], source[:, b * P:(b + 1) * P],
                                               ident[0:NG, 0:NG])
                last.then_inc(s["turned"], 1)

            pe.wait_ge(s["srcf_ready"], 1)
            for k in range(5):
                turn(k, srcf_g, banks[k])
            pe.wait_ge(s["edges_kf"], 1)
            for k in range(5):
                if 5 + k >= 8:
                    pe.wait_ge(s["turned_s"], 5 + k - 8 + 1)
                turn(k, key_g, banks[(5 + k) % 8])
            pe.wait_ge(s["bad_ready"], 1)
            pe.wait_ge(s["idx_ready"], 6)
            pe.wait_ge(s["turned_s"], 5)
            mm(banks[2][0:1, 0:4], ones[:, 0:1], bad[:, :], start=True, stop=True).then_inc(s["flag_sum"], 1)
            pe.wait_ge(s["flag_ready"], 1)
            pe.wait_ge(s["turned_k"], 5)

            def weights_pe(step):
                if step == 0:
                    pe.wait_ge(s["mixing_in"], 2 * 16)
                    for hc in range(H):
                        for hr in range(H):
                            last = nc.tensor.transpose(B5[:, hc * D + hr * P:hc * D + (hr + 1) * P],
                                                       wq_s[:, hr, 2 * D + hc * P:2 * D + (hc + 1) * P],
                                                       ident[:, :])
                    last.then_inc(s["mixw_pe"], 1)
                elif step == 1:
                    pe.wait_ge(s["prep_dve"], 3)
                    for hr in range(H):
                        for k in range(H):
                            mm(B6[:, hr * D:(hr + 1) * D], wvt_s[:, k, hr * P:(hr + 1) * P], wo_s[:, k, :],
                               start=(k == 0), stop=(k == H - 1))
                    for k in range(H):
                        last = mm(B7[:, 0:D], bvb[:, k, :], wo_s[:, k, :], start=(k == 0), stop=(k == H - 1))
                    last.then_inc(s["mixw_pe"], 1)
                else:
                    pe.wait_ge(s["mix_dve"], 1)
                    mm(B6[:, :], zeros[:, 0:P], zeros[:, :], start=True, stop=True).then_inc(s["mixw_pe"], 1)
                    pe.wait_ge(s["bias_parts"], 3 * 16)
                    pe.wait_ge(s["rel_lo"], REL_LOADS)
                    pe.wait_ge(s["weights_in"], 9 * 16)

            def agg(t, b):
                g, bb = b // BLOCKS, b % BLOCKS
                lo, hi = WIN[bb]
                if b % RB == 0:
                    pe.wait_ge(got[b // RB], (t + 1) * RB * 16)
                n_before = 4 * t + 2 * g
                if bb == 0 and (b or not isinstance(t, int) or t):
                    pe.wait_ge(s["lo_done"], (n_before - 1) * H)
                if bb == FIRST1 and (b >= BLOCKS or not isinstance(t, int) or t):
                    pe.wait_ge(s["lo_done"], n_before * H)
                pe.wait_ge(s["hot_ready"], t * TB + b + 1)
                for q in range(2):
                    l, r = max(lo, q * BANK_N), min(hi, (q + 1) * BANK_N)
                    if l >= r:
                        continue
                    first = 0 if q == 0 else FIRST1
                    for h in range(H):
                        for part in range(2):
                            last = mm(banks[2 * q + h][:, (l - q * BANK_N) * R:(r - q * BANK_N) * R],
                                      ring[:, b, part * D + h * P:part * D + (h + 1) * P],
                                      hot[:, b % OH, (l - lo) * R:(r - lo) * R],
                                      start=(bb == first and part == 0), stop=True, skip_group_check=True)
                last.then_inc(s["blocks_used"], 1)

            def relations(t):
                pe.wait_ge(s["xg_in"], (t + 1) * 32)
                if not isinstance(t, int) or t:
                    pe.wait_ge(s["u_ready"], t)
                mm(GB[:, :], ones16[:, :], bias16[:, 2 * D:4 * D], start=True, stop=False)
                for h in range(H):
                    mm(GB[:, :], xnt_g[:, h, :], wown[:, h, :], start=False, stop=False)
                for h in range(H):
                    pe.wait_ge(s["hi_done"], (4 * t + 3) * H + h + 1)
                    for r in range(R):
                        for w in (0, 1):
                            mm(GB[:, D:2 * D], s_hi[:, h, r, :], wr[:, w, h, r, :], start=False, stop=False)
                    pe.wait_ge(s["lo_done"], (4 * t + 3) * H + h + 1)
                    for r in range(R):
                        last = mm(GB[:, D:2 * D], s_lo[:, h, r, :], wr[:, 2, h, r, :], start=False,
                                  stop=(h == H - 1 and r == R - 1))
                last.then_inc(s["w_done"], 1)

            def m_pe(m, step):
                later = not isinstance(m, int) or m > 0
                if step == "xt":
                    pe.wait_ge(s["m_in"], (m + 1) * 16)
                    if later:
                        pe.wait_ge(s["m_qtc"], m)
                    for h in range(H):
                        last = nc.tensor.transpose(B7[:, h * P:(h + 1) * P], xn_m[:, h * P:(h + 1) * P], ident[:, :])
                    last.then_inc(s["m_turned"], 1)
                elif step == "kq":
                    pe.wait_ge(s["m_xnt"], m + 1)
                    if later:
                        pe.wait_ge(s["m_k2"], m)
                    mm(B5[:, :], ones16[:, :], bias16[:, 0:2 * D], start=True, stop=False)
                    for h in range(H):
                        last = mm(B5[:, :], xnt_m[:, h * P:(h + 1) * P], wkq[:, h, :], start=False,
                                  stop=(h == H - 1))
                    last.then_inc(s["m_k"], 1)
                elif step == "sum":
                    pe.wait_ge(s["m_k2n"], m + 1)
                    for h in range(H):
                        last = mm(B6[:, h * D:(h + 1) * D], xn_m[:, h * P:(h + 1) * P], k2n, start=False, stop=True,
                                  skip_group_check=True)
                    last.then_inc(s["m_used"], 1)
                else:
                    pe.wait_ge(s["m_q2n"], m + 1)
                    for h in range(H):
                        last = nc.tensor.transpose(B7[:, D + h * P:D + (h + 1) * P], q2n[:, h * P:(h + 1) * P],
                                                   ident[:, :])
                    last.then_inc(s["m_qt"], 1)

            M_AT = {0: "xt", 2: "kq", 7: "sum", 9: "qt"}

            def g_and_m(t, ms, before=True, weights=False):
                for b in range(TB):
                    agg(t, b)
                    if before and b == 0:
                        relations(t - 1)
                    if weights and b == 18:
                        weights_pe(2)
                    if b % MSLOT in M_AT and ms[b // MSLOT] is not None:
                        m_pe(ms[b // MSLOT], M_AT[b % MSLOT])

            general = pe.value_load(flag[0:1, 0:1])
            with pe.If(general > 0):
                with pe.Fori(0, NEB) as k:
                    pe.wait_ge(s["gp_key"], k + 1)
                    mm(banks[0][:, 0:P], gp_keys, ident[:, :], start=True, stop=True).then_inc(s["gp_wide"], 1)
                    pe.wait_ge(s["gp_made"], k + 1)
                    pe.wait_ge(s["gp_got"], k * 32 + 32)
                    mm(banks[1][:, 0:D], gp_same, gp_rows[:, 0:D], start=True, stop=False)
                    mm(banks[1][:, 0:D], gp_same, gp_rows[:, D:2 * D], start=False, stop=True)\
                        .then_inc(s["gp_sum"], 1)
            weights_pe(0)
            weights_pe(1)
            g_and_m(0, (None, None, 0), before=False, weights=True)
            g_and_m(1, (1, 2, 3))
            with pe.Fori(2, L1 - 1) as t:
                g_and_m(t, (MS * t - 2, MS * t - 1, MS * t))
            g_and_m(L1 - 1, (T - 3, T - 2, T - 1))
            relations(L1 - 1)

            pe.wait_ge(s["m_sum"], T)
            pe.wait_ge(s["m_qtc"], T)
            for j, own in ((0, k4_sum), (2, k2n_sum)):
                for h in range(H):
                    last = mm(B7[:, j + h:j + h + 1], own[:, h * P:(h + 1) * P], ones[:, 0:1], start=True, stop=True)
            last.then_inc(s["mix_pe"], 1)
            pe.wait_ge(s["mix_dve"], 3)
            yt = work[:, 0:2, :]
            for hc in range(H):
                for k in range(H):
                    last = mm(B5[:, hc * D:(hc + 1) * D], yt[:, k, hc * P:(hc + 1) * P], wvo[:, k, :],
                              start=(k == 0), stop=(k == H - 1))
            last.then_inc(s["mix_pe"], 1)
            pe.wait_ge(s["mix_dve"], 5)

            def p_pe(p, step):
                if step == "mix":
                    pe.wait_ge(s["p_in"], (p + 1) * 32)
                    if not isinstance(p, int) or p:
                        pe.wait_ge(s["p_out"], p)
                    for h in range(H):
                        last = mm(B5[:, 0:D], q2nt_p[:, h * P:(h + 1) * P], m1[:, h, :], start=(h == 0),
                                  stop=(h == H - 1))
                    last.then_inc(s["p_mix"], 1)
                elif step == "xt":
                    pe.wait_ge(s["p_xn2"], p + 1)
                    for h in range(H):
                        last = nc.tensor.transpose(B6[:, h * P:(h + 1) * P], xn2[:, h * P:(h + 1) * P], ident[:, :])
                    last.then_inc(s["p_xt"], 1)
                elif step == "l1":
                    pe.wait_ge(s["p_xtc"], p + 1)
                    mm(B7[:, 0:EX], ones16[:, :], bias16[:, 4 * D:BIAS], start=True, stop=False)
                    for h in range(H):
                        last = mm(B7[:, 0:EX], xn2t[:, h * P:(h + 1) * P], gw[:, h, :], start=False, stop=(h == H - 1))
                    last.then_inc(s["p_log"], 1)
                    for j in range(H):
                        for h in range(H):
                            last = mm(B6[:, j * P:(j + 1) * P], sw1[:, h, j * P:(j + 1) * P],
                                      xn2t[:, h * P:(h + 1) * P], start=(h == 0), stop=(h == H - 1))
                    last.then_inc(s["p_h1s"], 1)
                    for j in range(EX):
                        for h in range(H):
                            last = mm(B5[:, j * P:(j + 1) * P], ew1[:, h, j, :],
                                      xn2t[:, h * P:(h + 1) * P], start=(h == 0), stop=(h == H - 1))
                    last.then_inc(s["p_h1e"], 1)
                elif step == "wt":
                    pe.wait_ge(s["p_w5"], p + 1)
                    nc.tensor.transpose(B7[0:EX + 1, D:D + P], gate[:, 60:65], ident[:, :]).then_inc(s["p_wt"], 1)
                elif step == "l2":
                    pe.wait_ge(s["p_wtc"], p + 1)
                    for j in range(H):
                        last = mm(B7[:, j * P:(j + 1) * P], post_c[0:EX, 16 + j * P:16 + (j + 1) * P], w5t[0:EX, :],
                                  start=True, stop=True)
                    last.then_inc(s["p_wb"], 1)
                    pe.wait_ge(s["p_h1"], (p + 1) * (H + EX))
                    for h in range(H):
                        mm(B6[:, 0:P], sw2[:, h, :], h1[:, h, :], start=(h == 0), stop=(h == H - 1))
                    for e in range(EX):
                        o = (e % 2) * EH2
                        last = mm(B6[o:o + EH2, (1 + e // 2) * P:(2 + e // 2) * P], ew2[:, e, :], h1[:, H + e, :],
                                  start=True, stop=True)
                    last.then_inc(s["p_l2"], 1)
                elif step == "l3":
                    pe.wait_ge(s["p_h2g"], p + 1)
                    mm(B5[:, 0:D], w5t[:, :], b3[:, :], start=True, stop=False)
                    mm(B5[:, 0:D], h2s, sw3[:, :], start=False, stop=False)
                    for j in range(H):
                        last = mm(B5[:, 0:D], h2g[:, j * P:(j + 1) * P], ew3[:, j, :], start=False, stop=(j == H - 1))
                    last.then_inc(s["p_l3"], 1)

            STEPS = ["mix", "xt", "l1", "wt", "l2", "l3"]
            AT = PE_AT

            def g_and_p(t, half, p0, before=True):
                for b in range(TB):
                    slot = half * TB + b
                    agg(t, b)
                    for k, a in enumerate(AT[slot // PSLOT]):
                        if slot % PSLOT == a:
                            p_pe(p0 + slot // PSLOT, STEPS[k])
                    if before and b == 0:
                        relations(t - 1)

            g_and_p(L1, 0, 0, before=False)
            g_and_p(L1 + 1, 1, 0)
            with pe.Fori(1, J2) as j:
                g_and_p(2 * j + L1, 0, PS * j)
                g_and_p(2 * j + (L1 + 1), 1, PS * j)
            relations(T - 1)
            for k in STEPS:
                p_pe(T - 1, k)


_INS = ["x", "src", "dst", "edge_type_16", "L0_gnn_W_rel", "L0_gnn_W_self", "L0_gnn_bias", "L0_mix_W_qkv",
        "L0_mix_b_qkv", "L0_mix_W_out", "L0_mix_b_out", "L0_ffn_sW1", "L0_ffn_sb1", "L0_ffn_sW2", "L0_ffn_sb2",
        "L0_ffn_sW3", "L0_ffn_sb3", "L0_ffn_eW1", "L0_ffn_eb1", "L0_ffn_eW2", "L0_ffn_eb2", "L0_ffn_eW3",
        "L0_ffn_eb3", "L0_ffn_gW", "L0_ffn_gb"]


def consts():
    ident = np.eye(P, dtype=np.float32)
    iota = np.tile(np.arange(PAIRS, dtype=np.float16), (P, 1))
    group = np.zeros((P, 2 * BLOCKS + 1), np.float32)
    group[:, 0:BLOCKS] = [lo for lo, _ in WIN]
    group[:, BLOCKS:2 * BLOCKS] = [hi if hi < GN else 2.0 ** 20 for _, hi in WIN]
    group[:, 2 * BLOCKS] = GN * np.arange(P)
    post = np.zeros((P, POST_C), np.float32)
    post[:, 0:16] = np.tril(np.ones((EX, EX), np.float32), -1).reshape(1, 16)
    for e in range(EX):
        post[e, 16 + (e // 2) * P + (e % 2) * EH2:16 + (e // 2) * P + (e % 2 + 1) * EH2] = 1.0
    post[0:TAIL, 16 + P * H] = 1.0
    post[:, POST_C - P:] = np.tril(np.ones((P, P), np.float32), -1)
    pad = np.zeros((3, CAP), np.int32)
    pad[0] = N + (np.arange(CAP) / DEG).astype(np.int32)
    pad[0][pad[0] >= NP] = PADDST
    return {"c_ident": ident, "c_iota": iota, "c_group": group, "c_post": post, "c_pad": pad}


def kernel(**inputs):
    import concourse.bacc as bacc
    from concourse.bass_utils import run_bass_kernel_spmd

    nc = bacc.Bacc("TRN2", target_bir_lowering=False, num_devices=1)
    arrays, args = {}, []
    for name, a in [(n, inputs[n]) for n in _INS] + list(consts().items()):
        a = np.ascontiguousarray(a)
        arrays[name] = a
        args.append(nc.dram_tensor(name, a.shape, mybir.dt.from_np(a.dtype), kind="ExternalInput").ap())
    args.append(nc.dram_tensor("out", (N, D), F32, kind="ExternalOutput").ap())
    build(nc, *args)
    r = run_bass_kernel_spmd(nc, [arrays], core_ids=[0])
    return r.results[0]["out"]
```

```python
from contextlib import ExitStack
from math import ceil, floor, sqrt

import numpy as np
import concourse.bass as bass
from concourse import mybir
from concourse.alu_op_type import AluOpType as ALU

F32 = mybir.dt.float32
F16 = mybir.dt.float16
I32 = mybir.dt.int32
ACT = mybir.ActivationFunctionType
AX = mybir.AxisListType

P = 128
D = 256
H = D // P
R = 16
N = 6250
E = 206250
T = -(-N // P)
TAIL = N - (T - 1) * P
NP = T * P
GN = 64
GT = P // GN
NG = T * GT
PAIRS = GN * R
DEG = E / N
BLOCKS = 18
CAP = BLOCKS * P
TB = GT * BLOCKS
BANK_N = 32
ROWS, ROW = 125, E // 125
EPAD = E + CAP
PADDST = 8191
SCALE = 64.0
EPS_LN, EPS_DIV, EPS_NORM = 1e-5, 1e-7, 1e-12
Z = 4.3
CH = 7
NEB = -(-E // P)
RH = R // 4
REL_LOADS = H * R // RH
MS = 3
L1 = 1 + -(-(T - 1) // MS)
PS = 3
J2 = (T - L1) // 2
EX, EH1, EH2 = 4, 128, 64
BIAS = 4 * D + EX
POST_C = 16 + P * H + 1 + P
RB = 6
OH = 12
U_AT = 3
AHEAD = 8
MSLOT = TB // MS
PSLOT = 2 * TB // PS


PE_AT = ((0, 1, 3, 10, 12, 17), (0, 9, 10, 16, 18, 22), (0, 9, 10, 16, 18, 22))
ACT_AT = ((1, 2, 5, 5, 7, 8, 13), (2, 9, 11, 12, 13, 14, 19), (2, 9, 11, 12, 13, 14, 19))
DVE_AT = ((0, 2, 4, 6, 8, 10, 14, 18), (1, 4, 10, 11, 14, 16, 20, 23), (1, 4, 10, 11, 14, 16, 20, 23))

PE_AT_0 = ((5, 11, 13, 18, 20, 23),) + PE_AT[1:]
ACT_AT_0 = ((7, 11, 13, 13, 14, 15, 21),) + ACT_AT[1:]
DVE_AT_0 = ((6, 9, 13, 13, 15, 18, 22, 23),) + DVE_AT[1:]


def windows():
    out = []
    for b in range(BLOCKS):
        lo = floor(P * b / DEG - Z * sqrt((DEG - 1) * P * b / DEG) / DEG)
        hi = ceil(P * (b + 1) / DEG + Z * sqrt((DEG - 1) * P * (b + 1) / DEG) / DEG) + 1
        if b < 2 * (GN // 8):
            lo, hi = min(lo, 8 * (b // 2)), max(hi, 8 * (b // 2) + 8)
        out.append((max(lo, 0), min(hi, GN)))
    return out


WIN = windows()
W16_ACT_AT = (12, 14)
WMAX = max(hi - lo for lo, hi in WIN) * R
LAST0 = max(b for b, (lo, hi) in enumerate(WIN) if lo < BANK_N)
FIRST1 = min(b for b, (lo, hi) in enumerate(WIN) if hi > BANK_N)


def build(nc, x, src, dst, etype, w_rel, w_self, g_bias, w_qkv, b_qkv, w_out, b_out, s_w1, s_b1,
          s_w2, s_b2, s_w3, s_b3, e_w1, e_b1, e_w2, e_b2, e_w3, e_b3, g_w, g_b,
          c_ident, c_iota, c_group, c_post, c_pad, out):
    ctx = ExitStack()
    with ctx:
        def sb(name, shape, dt=F32):
            return ctx.enter_context(nc.sbuf_tensor(name, shape, dt))

        def sem(name):
            return ctx.enter_context(nc.semaphore(name))

        table = nc.dram_tensor("table", (NP, 2 * D), F16).ap()
        sums_t = nc.dram_tensor("sums_t", (2 * NG * PAIRS, 2 * D), F16).ap()
        sums_d = nc.dram_tensor("sums_d", (NG * PAIRS, D), F32).ap()
        xnt_d = nc.dram_tensor("xnt_d", (T, P, 2 * D), F16).ap()
        q2nt_d = nc.dram_tensor("q2nt_d", (T, P, D), F32).ap()
        u_d = nc.dram_tensor("u_d", (T, P, D), F32).ap()
        src_p = nc.dram_tensor("src_p", (EPAD,), I32).ap()
        dst_p = nc.dram_tensor("dst_p", (EPAD,), I32).ap()
        typ_p = nc.dram_tensor("typ_p", (EPAD,), I32).ap()

        ident = sb("ident", [P, P])
        iota16 = sb("iota16", [P, PAIRS], F16)
        group_c = sb("group_c", [P, 2 * BLOCKS + 1])
        post_c = sb("post_c", [P, POST_C])
        ones = sb("ones", [P, P])
        zeros = sb("zeros", [P, 512])
        eps_ln = sb("eps_ln", [P, 1])
        wr = sb("wr", [P, 3, H, R, D], F16)
        wown = sb("wown", [P, H, 2 * D])
        wvo = wown[:, :, 0:D]
        wkq16 = sb("wkq16", [P, 3, H, 2 * D], F16)
        wown16 = sb("wown16", [P, 3, H, 2 * D], F16)
        wkq = sb("wkq", [P, H, 2 * D])
        m1 = sb("m1", [P, H, D])
        sw1 = sb("sw1", [P, H, D])
        ew1 = sb("ew1", [P, H, EX, EH1])
        sw2 = sb("sw2", [P, H, P])
        ew2 = sb("ew2", [P, EX, EH2])
        sw3 = sb("sw3", [P, D])
        ew3 = sb("ew3", [P, H, D])
        gw = sb("gw", [P, H, EX])
        bias_row = sb("bias_row", [1, BIAS])
        bias_left = sb("bias_left", [1, BIAS])
        bias_part = sb("bias_part", [1, 3, BIAS], F16)
        bias16 = sb("bias16", [3, BIAS], F16)
        ones16 = sb("ones16", [3, P], F16)
        b3 = sb("b3", [EX + 1, D])
        b1_col = sb("b1_col", [P, H + EX])
        b2_col = sb("b2_col", [P, 1 + H])

        idx_t = sb("idx_t", [P, NG + GT, BLOCKS], I32)
        key_t = sb("key_t", [P, NG + GT, BLOCKS])
        hot_v = sb("hot_v", [P, BLOCKS])
        idx_now = sb("idx_now", [P, 2, TB], I32)
        key_now = sb("key_now", [P, TB])
        ring = sb("ring", [P, TB, 2 * D], F16)
        hot = sb("hot", [P, OH, WMAX], F16)
        s_hi = sb("s_hi", [P, H, R, P], F16)
        s_lo = sb("s_lo", [P, H, R, P], F16)
        xnt_g = sb("xnt_g", [P, 2, H, P], F16)
        x_g = sb("x_g", [P, D])
        u_g = sb("u_g", [P, D])

        work = sb("work", [P, 20, D])
        (xn_m, xnt_m, k2, k2n, k4, q2, q4, q2n, q2nt, k2n_sum, k4_sum) = (work[:, j, :] for j in range(11))
        xnt_m = xnt_m.bitcast(F16)
        xn_m = (xn_m, work[:, 13, :], work[:, 14, :])
        tab_m = work[:, 11, :].bitcast(F16)
        (u_p, q2nt_p, x1, xn2, xn2t, h2, h2g, o_p) = (work[:, j, :] for j in range(8))
        h1 = work[:, 12:15, :].rearrange("p a (b n) -> p (a b) n", n=P)
        h2s = work[:, 15, 0:P]
        stat = sb("stat", [P, 32])
        gate = sb("gate", [P, 96])
        w5t = sb("w5t", [EX + 1, P])

        ring_f = ring[:, :, :].rearrange("p a b -> p (a b)").bitcast(F32)
        s_f, s_f2 = (own[:, :, :, :].rearrange("p a b c -> p (a b c)").bitcast(F32) for own in (s_hi, s_lo))

        def chunk(flat, width):
            return flat.rearrange("p (a b) -> p a b", b=width)

        xc = (chunk(ring_f[:, 0:CH * D], D), chunk(s_f[:, 0:CH * D], D))
        xnc = (chunk(ring_f[:, CH * D:2 * CH * D], D), chunk(s_f2[:, 0:CH * D], D))
        tabc = (chunk(ring[:, :, :].rearrange("p a b -> p (a b)")[:, 4 * CH * D:6 * CH * D], 2 * D),
                chunk(work[:, 12:12 + CH, :].rearrange("p a b -> p (a b)").bitcast(F16), 2 * D))
        rows = ring_f[0:ROWS, 3 * CH * D:3 * CH * D + ROW].bitcast(I32)
        nxt = ring_f[0:ROWS, 3 * CH * D + ROW:3 * CH * D + 2 * ROW].bitcast(I32)
        wr_f = wr[:, :, :, :, :].rearrange("p a b c d -> p (a b c d)").bitcast(F32)
        src_g, dst_g, typ_g = (wr_f[0:NG, j * CAP:(j + 1) * CAP].bitcast(I32) for j in range(3))
        key_g, srcf_g = (wr_f[0:NG, j * CAP:(j + 1) * CAP] for j in (3, 4))
        wstage = (work[:, 12:12 + RH, :], work[:, 12 + RH:12 + 2 * RH, :])
        st = sb("st", [P, CH, 6])
        mv = sb("mv", [P, CH, 2])
        rstd = sb("rstd", [P, CH])
        ec = sb("ec", [P, 8])
        ei = sb("ei", [P, 2], I32)
        rfb = sb("rfb", [ROWS, NG])
        bad = sb("bad", [P, 4])
        wvt_s = work[:, 2:4, :]
        wo_s = work[:, 4:6, :]
        wq_s = work[:, 6:12, :].rearrange("p (h c) d -> p h (c d)", h=H)
        bv_col = sb("bv_col", [P, H])
        bvb = sb("bvb", [P, H, P])
        bvo_b = sb("bvo_b", [P, D])
        pcol = sb("pcol", [P, 8])
        carrier = sb("carrier", [P, 1])
        flag = sb("flag", [1, 1], I32)
        flag_f = sb("flag_f", [1, 1])

        gp_i = sb("gp_i", [P, 5], I32)
        gp_f = sb("gp_f", [P, 3])
        gp_rows = ring[:, 0, :]
        gp_was, gp_new = ring_f[:, D:2 * D], ring_f[:, 2 * D:3 * D]
        gp_same = ring[:, 3, 0:P]
        gp_earlier = ring_f[:, 4 * D:4 * D + P]
        gp_keys = ring_f[:, 4 * D + P:5 * D]
        gp_parts = ring[:, 6:8, :]
        gp_left = ring_f[:, 8 * D:9 * D]

        banks = [ctx.enter_context(nc.psum_tensor(f"bank{i}", [P, 512], F32)) for i in range(8)]
        GB = banks[4]
        B5, B6, B7 = banks[5:8]

        names = """search_in consts_in x_in0 x_in1 weights_in mixing_in bias_in rel_in0 rel_in1 pad_made edges_pad
            rows_in next_in ln_done sd_ready xn_ready hi_ready lo_ready tab_out0 tab_out1 rf_ready rf_wide
            row_ready row_got start_ready edges_got edges_kf srcf_ready turned turned_k turned_s prep_dve
            prep_act rel_lo mixw_pe idx_ready keys_ready hot_ready blocks_used hi_done lo_done w_done xg_in
            u_half u_ready u_out bias_parts batches bad_ready flag_sum flag_ready gp_clear gp_in0 gp_in1 gp_in2
            gp_key gp_wide gp_made gp_got gp_sum gp_new gp_out gp_row_in gp_row_made gp_row_out gp_done dve_g
            m_qtc m_q_out m_qt m_q2 m_q4 m_nb m_q2n m_sum m_in m_turned m_xnt m_xnt_out m_k m_k2 m_k2n m_k4
            m_used m_xn m_xh w16_ready w16_hi w16_lo mix_dve mix_act mix_pe p_in p_sd p_mix p_x1 p_ln p_xn2 p_xt
            p_xtc p_log p_h1s p_h1e p_h1 p_max p_exp p_gmax p_exp2 p_w5 p_wt p_wtc p_wb p_l2 p_h2 p_h2g p_l3
            p_out out_done dve_c dve_c2 dve_p dve_m""".split()
        s = {n: sem(n) for n in names}
        x_in, tab_out, rel_in = ([s[f"{n}{buf}"] for buf in range(2)] for n in ("x_in", "tab_out", "rel_in"))
        got = [sem(f"got{i}") for i in range(TB // RB)]

        block = ctx.enter_context(nc.Block())

        def chunk_rows(c):
            return slice(c * CH * P, (c + 1) * CH * P)

        NC_P = T // CH
        CHUNKS = (NC_P - NC_P // 2, NC_P // 2)
        assert NC_P == 7

        @block.sync
        def _(sp):
            sp.dma_start(rows, dst.rearrange("(r c) -> r c", c=ROW)).then_inc(s["rows_in"], 16)

            def ln_in(n, buf):
                c = 2 * n + buf
                own = xc[buf]
                if isinstance(c, int) and c == NC_P - 1:
                    sp.dma_start(own[:, 0:CH - 1, :], x[(NC_P - 1) * CH * P:(T - 1) * P, :]
                                 .rearrange("(j p) d -> p j d", p=P)).then_inc(x_in[buf], 16)
                    sp.wait_ge(s["pad_made"], 1)
                    sp.dma_start(own[0:TAIL, CH - 1, :], x[(T - 1) * P:N, :]).then_inc(x_in[buf], 16)
                else:
                    sp.dma_start(own, x[bass.ds(c * (CH * P), CH * P), :]
                                 .rearrange("(j p) d -> p j d", p=P)).then_inc(x_in[buf], 16)

            def ln_out(n, buf, fetch=True):
                c = 2 * n + buf
                if fetch:
                    sp.wait_ge(s["xn_ready"], c + 1)
                    ln_in(n + 1, buf)
                sp.wait_ge(s["lo_ready"], c + 1)
                sp.dma_start(table[bass.ds(c * (CH * P), CH * P), :].rearrange("(j p) d -> p j d", p=P),
                             tabc[buf]).then_inc(tab_out[buf], 16)

            ln_in(0, 0)
            sp.dma_start(group_c[:, :], c_group).then_inc(s["search_in"], 16)
            sp.dma_start(ident[:, :], c_ident).then_inc(s["search_in"], 16)
            ln_in(0, 1)
            for k, (full, own) in enumerate(((dst_p, dst), (src_p, src), (typ_p, etype))):
                sp.dma_start(full[0:E].rearrange("(r c) -> r c", c=ROW),
                             own.rearrange("(r c) -> r c", c=ROW)).then_inc(s["edges_pad"], 16)
                sp.dma_start(full[E:EPAD].rearrange("(r c) -> r c", c=P),
                             c_pad[k, :].rearrange("(r c) -> r c", c=P)).then_inc(s["edges_pad"], 16)
            sp.dma_start(iota16[:, :], c_iota).then_inc(s["consts_in"], 16)
            sp.dma_start(post_c[:, :], c_post).then_inc(s["consts_in"], 16)
            with sp.Fori(0, NC_P // 2 - 1) as k:
                ln_out(k, 0)
                ln_out(k, 1)
            def rel_load(k):
                h, r0 = k * RH // R, k * RH % R
                if k >= 2:
                    sp.wait_ge(s["rel_lo"], k - 1)
                sp.dma_start(wstage[k % 2], w_rel[r0:r0 + RH, h * P:(h + 1) * P, :].rearrange("r p c -> p r c"))\
                  .then_inc(rel_in[k % 2], 16)

            ln_out(NC_P // 2 - 1, 0)
            sp.dma_start(wq_s, w_qkv.rearrange("(h p) c -> p h c", p=P)).then_inc(s["mixing_in"], 16)
            sp.dma_start(wo_s, w_out.rearrange("(h p) c -> p h c", p=P)).then_inc(s["mixing_in"], 16)
            sp.dma_start(wown[:, :, D:2 * D], w_self.rearrange("(h p) c -> p h c", p=P))\
              .then_inc(s["mixing_in"], 16)
            ln_out(NC_P // 2 - 1, 1, fetch=False)
            ln_out(NC_P // 2, 0, fetch=False)
            sp.wait_ge(tab_out[1], CHUNKS[1] * 16)
            rel_load(0)
            rel_load(1)

            def m_load(m):
                if not isinstance(m, int) or m:
                    sp.wait_ge(s["m_xn"], m)
                sp.dma_start(tab_m, table[bass.ds(m * P, P), :]).then_inc(s["m_in"], 16)

            def m_store(m):
                sp.wait_ge(s["m_xnt"], m + 1)
                sp.dma_start(xnt_d[bass.ds(m, 1), :, :].rearrange("o p d -> (o p) d"), xnt_m)\
                  .then_inc(s["m_xnt_out"], 16)

            def m_store_q(m):
                sp.wait_ge(s["m_qtc"], m + 1)
                sp.dma_start(q2nt_d[bass.ds(m, 1), :, :].rearrange("o p d -> (o p) d"), q2nt)\
                  .then_inc(s["m_q_out"], 16)

            def g_load(t, m_now):
                sp.wait_ge(s["m_xnt_out"], m_now * 16)
                if not isinstance(t, int) or t:
                    sp.wait_ge(s["u_ready"], t)
                sp.dma_start(xnt_g[:, :, :, :].rearrange("p w h n -> p (w h n)"),
                             xnt_d[bass.ds(t, 1), :, :].rearrange("o p d -> (o p) d"))\
                  .then_inc(s["xg_in"], 16)
                if isinstance(t, int) and t == T - 1:
                    sp.dma_start(x_g[0:TAIL, :], x[(T - 1) * P:N, :]).then_inc(s["xg_in"], 16)
                else:
                    sp.dma_start(x_g[:, :], x[bass.ds(t * P, P), :]).then_inc(s["xg_in"], 16)

            def g_store(t):
                sp.wait_ge(s["u_ready"], t + 1)
                sp.dma_start(u_d[bass.ds(t, 1), :, :].rearrange("o p d -> (o p) d"), u_g[:, :])\
                  .then_inc(s["u_out"], 16)

            for dram, tile in ((s_w1, sw1), (s_w2, sw2), (g_w, gw)):
                sp.dma_start(tile[:, :, :], dram.rearrange("(h p) c -> p h c", p=P))\
                  .then_inc(s["weights_in"], 16)
            for k in range(2, REL_LOADS):
                rel_load(k)
            for h in range(H):
                sp.dma_start(ew1[:, h, :, :], e_w1[:, h * P:(h + 1) * P, :].rearrange("e p c -> p e c"))\
                  .then_inc(s["weights_in"], 16)
            sp.dma_start(ew2[:, :, :], e_w2.rearrange("e p c -> p e c")).then_inc(s["weights_in"], 16)
            sp.dma_start(sw3[:, :], s_w3).then_inc(s["weights_in"], 16)
            sp.dma_start(ew3[:, :, :], e_w3.rearrange("e p c -> (e p) c").rearrange("(h q) c -> q h c", h=H))\
              .then_inc(s["weights_in"], 16)

            sp.wait_ge(s["mix_dve"], 1)
            for k in range(3):
                sp.dma_start(bias16[k:k + 1, :], bias_part[0:1, k, :]).then_inc(s["bias_parts"], 16)
            for buf in range(2):
                sp.wait_ge(tab_out[buf], CHUNKS[buf] * 16)
            sp.wait_ge(s["mixw_pe"], 3)

            def sp_g_and_m(t):
                m = MS * t - 2
                m_store(m)
                m_load(m + 2)
                m_store_q(m)
                m_store(m + 1)
                g_load(t, m + 2)
                if not isinstance(t, int) or t < L1 - 1:
                    m_load(m + 3)
                m_store_q(m + 1)
                m_store(m + 2)
                if not isinstance(t, int) or t < L1 - 1:
                    m_load(m + 4)
                m_store_q(m + 2)
                g_store(t)

            m_load(0)
            m_load(1)
            m_store(0)
            g_load(0, 1)
            m_load(2)
            m_store_q(0)
            g_store(0)
            with sp.Fori(1, L1 - 1) as i:
                sp_g_and_m(i)
            sp_g_and_m(L1 - 1)

            def p_load(p, stored):
                if not isinstance(p, int) or p:
                    sp.wait_ge(s["p_x1"], p)
                sp.dma_start(q2nt_p, q2nt_d[bass.ds(p, 1), :, :].rearrange("o p d -> (o p) d"))\
                  .then_inc(s["p_in"], 16)
                if isinstance(p, int) and p == T - 1:
                    return
                sp.wait_ge(s["u_out"], stored * 16)
                sp.dma_start(u_p, u_d[bass.ds(p, 1), :, :].rearrange("o p d -> (o p) d"))\
                  .then_inc(s["p_in"], 16)

            def p_store(p):
                sp.wait_ge(s["p_out"], p + 1)
                if isinstance(p, int) and p == T - 1:
                    sp.dma_start(out[(T - 1) * P:N, :], o_p[0:TAIL, :]).then_inc(s["out_done"], 16)
                else:
                    sp.dma_start(out[bass.ds(p * P, P), :], o_p).then_inc(s["out_done"], 16)

            sp.wait_ge(s["mix_pe"], 2)
            sp.wait_ge(s["m_q_out"], T * 16)

            def sp_g_and_p(j):
                t, p = 2 * j + L1, PS * j
                g_load(t, T)
                p_load(p + 1, t)
                p_store(p)
                g_store(t)
                g_load(t + 1, T)
                p_load(p + 2, t + 1)
                p_store(p + 1)
                p_load(p + 3, t + 1)
                p_store(p + 2)
                if not isinstance(j, int) or j < J2 - 1:
                    g_store(t + 1)

            p_load(0, L1)
            sp_g_and_p(0)
            with sp.Fori(1, J2 - 1) as j:
                sp_g_and_p(j)
            sp_g_and_p(J2 - 1)
            p_store(T - 1)
            sp.wait_ge(s["out_done"], T * 16)
            for buf in range(2):
                sp.wait_ge(tab_out[buf], CHUNKS[buf] * 16)

        @block.gpsimd
        def _(pool):
            pool.memset(ones[:, :], 1.0).then_inc(s["idx_ready"], 1)
            pool.memset(zeros[:, :], 0.0).then_inc(s["idx_ready"], 1)
            pool.memset(hot_v[:, :], 1.0).then_inc(s["idx_ready"], 1)
            pool.memset(idx_t[:, NG:NG + GT, :], 0)
            pool.memset(bad[:, :], 0.0).then_inc(s["idx_ready"], 1)
            pool.memset(gate[:, :], 1.0).then_inc(s["idx_ready"], 1)
            pool.memset(eps_ln[:, :], EPS_LN).then_inc(s["idx_ready"], 1)

            def ln_pool(n, buf):
                c = 2 * n + buf
                pool.wait_ge(s["hi_ready"], c + 1)
                pool.tensor_tensor(tabc[buf][:, :, D:2 * D], xnc[buf], tabc[buf][:, :, 0:D], ALU.subtract)\
                    .then_inc(s["lo_ready"], 1)

            pool.wait_ge(s["row_ready"], 1)
            pool.indirect_dma_start(key_g[:, 0:ROW].bitcast(I32), None,
                                    dst.rearrange("(r c) -> r c", c=ROW),
                                    bass.IndirectOffsetOnAxis(ap=ei[0:NG, 0:1], axis=0),
                                    bounds_check=ROWS - 1, oob_is_err=False).then_inc(s["row_got"], 16)
            ln_pool(0, 0)
            ln_pool(0, 1)
            pool.wait_ge(s["edges_pad"], 96)
            pool.wait_ge(s["start_ready"], 1)
            for full, own in ((dst_p, dst_g), (src_p, src_g), (typ_p, typ_g)):
                pool.indirect_dma_start(own, None,
                                        full[0:(EPAD // CAP) * CAP].rearrange("(r c) -> r c", c=CAP),
                                        bass.IndirectOffsetOnAxis(ap=ei[0:NG, 1:2], axis=1),
                                        bounds_check=E, oob_is_err=False).then_inc(s["edges_got"], 16)
            with pool.Fori(1, NC_P // 2) as k:
                ln_pool(k, 0)
                ln_pool(k, 1)
            ln_pool(NC_P // 2, 0)
            pool.wait_ge(s["turned_s"], 5)
            for buf in range(2):
                pool.wait_ge(tab_out[buf], CHUNKS[buf] * 16)

            def indices(t, parity):
                pool.tensor_copy(idx_now[:, parity, :],
                                 idx_t[:, bass.ds(GT * t, GT), :].rearrange("p g b -> p (g b)"))\
                    .then_inc(s["idx_ready"], 1)

            def gather(t, parity, own):
                pool.wait_ge(s["idx_ready"], t + 7)
                for b in range(TB):
                    if b == BLOCKS:
                        if not isinstance(t, int) or t:
                            for r in range(TB // RB):
                                pool.wait_ge(got[r], t * (RB * 16))
                        indices(t + 1, 1 - parity)
                    if b % RB == 0 and (not isinstance(t, int) or t):
                        pool.wait_ge(s["blocks_used"], (t - 1) * TB + b + RB)
                        pool.sem_inc(s["batches"], 1)
                    pool.indirect_dma_start(ring[:, b, :], None, own,
                                            bass.IndirectOffsetOnAxis(ap=idx_now[:, parity, b:b + 1], axis=0),
                                            bounds_check=own.shape[0] - 1, oob_is_err=False)\
                        .then_inc(got[b // RB], 16)

            def gather_all(own):
                indices(0, 0)
                gather(0, 0, own)
                with pool.Fori(0, T // 2) as k:
                    gather(2 * k + 1, 1, own)
                    gather(2 * k + 2, 0, own)

            pool.wait_ge(s["flag_ready"], 1)
            general = pool.value_load(flag[0:1, 0:1])
            with pool.If(general > 0):
                with pool.Fori(0, NG * PAIRS // (2 * P)) as k:
                    pool.dma_start(sums_d[bass.ds(k * (2 * P), 2 * P), :].rearrange("(p a) d -> p (a d)", a=2),
                                   zeros[:, :]).then_inc(s["gp_clear"], 16)
                pool.wait_ge(s["gp_clear"], NG * PAIRS // (2 * P) * 16)
                with pool.Fori(0, NEB) as k:
                    for j, full in enumerate((src_p, dst_p, typ_p)):
                        pool.dma_start(gp_i[:, j:j + 1], full[bass.ds(k * P, P)].rearrange("(p a) -> p a", a=1))\
                            .then_inc(s[f"gp_in{j}"], 16)
                    pool.wait_ge(s["gp_key"], k + 1)
                    pool.sem_inc(s["batches"], 1)
                    pool.indirect_dma_start(gp_rows, None, table[:, :],
                                            bass.IndirectOffsetOnAxis(ap=gp_i[:, 0:1], axis=0),
                                            bounds_check=NP - 1, oob_is_err=False).then_inc(s["gp_got"], 16)
                    pool.indirect_dma_start(gp_was, None, sums_d[:, :],
                                            bass.IndirectOffsetOnAxis(ap=gp_i[:, 3:4], axis=0),
                                            bounds_check=NG * PAIRS - 1, oob_is_err=False).then_inc(s["gp_got"], 16)
                    pool.wait_ge(s["gp_new"], k + 1)
                    pool.sem_inc(s["batches"], 1)
                    pool.indirect_dma_start(sums_d[:, :], bass.IndirectOffsetOnAxis(ap=gp_i[:, 4:5], axis=0), gp_new,
                                            None, bounds_check=NG * PAIRS - 1, oob_is_err=False)\
                        .then_inc(s["gp_out"], 16)
                    pool.wait_ge(s["gp_out"], k * 16 + 16)
                    pool.sem_inc(s["batches"], 1)
                with pool.Fori(0, NG * PAIRS // P) as k:
                    pool.dma_start(gp_was, sums_d[bass.ds(k * P, P), :]).then_inc(s["gp_row_in"], 16)
                    pool.wait_ge(s["gp_row_made"], k + 1)
                    pool.sem_inc(s["batches"], 1)
                    pool.dma_start(sums_t[bass.ds(k * (2 * P), 2 * P), :].rearrange("(p a) d -> p a d", a=2),
                                   gp_parts).then_inc(s["gp_row_out"], 16)
                    pool.wait_ge(s["gp_row_out"], k * 16 + 16)
                    pool.sem_inc(s["batches"], 1)
                blocks8 = idx_t[:, 0:NG, 0:2 * (GN // 8)].rearrange("p g (c a) -> p g c a", a=2)
                pool.iota(blocks8, [[2 * PAIRS, NG], [2 * P, GN // 8], [1, 2]], base=0, channel_multiplier=2)
                pool.iota(key_t[:, 0:NG, 0:2 * (GN // 8)].rearrange("p g (c a) -> p g c a", a=2),
                          [[0, NG], [P, GN // 8], [0, 2]], base=0, channel_multiplier=1,
                          allow_small_or_imprecise_dtypes=True)
                pool.memset(idx_t[:, 0:NG, 2 * (GN // 8):BLOCKS], 0)
                pool.memset(key_t[:, 0:NG, 2 * (GN // 8):BLOCKS], -1.0)
                pool.memset(hot_v[:, 0:2 * (GN // 8):2], SCALE)
                pool.drain().then_inc(s["gp_done"], 1)
                pool.wait_ge(s["gp_done"], 1)

                gather_all(sums_t)
            with pool.If(general < 1):
                gather_all(table)

        @block.scalar
        def _(act):
            act.wait_ge(s["idx_ready"], 6)

            act.activation(rstd[:, 0:1], eps_ln[:, 0:1], ACT.Sqrt).then_inc(s["sd_ready"], 1)
            act.wait_ge(s["sd_ready"], 1)

            def ln_act(n, buf):
                c = 2 * n + buf
                act.wait_ge(s["ln_done"], c + 1)
                act.activation(rstd[:, :], mv[:, :, 1], ACT.Sqrt, bias=eps_ln[:, 0:1]).then_inc(s["sd_ready"], 1)
                act.wait_ge(s["xn_ready"], c + 1)
                if not isinstance(n, int) or n:
                    act.wait_ge(tab_out[buf], n * 16)
                act.activation(tabc[buf][:, :, 0:D], xnc[buf], ACT.Copy).then_inc(s["hi_ready"], 1)

            ln_act(0, 0)
            ln_act(0, 1)
            for row, tile in ((b_qkv[D:2 * D], bias_row[0:1, 0:D]), (b_qkv[0:D], bias_row[0:1, D:2 * D]),
                              (b_out, bias_row[0:1, 2 * D:3 * D]), (g_bias, bias_row[0:1, 3 * D:4 * D]),
                              (g_b, bias_row[0:1, 4 * D:BIAS]), (s_b3, b3[EX:EX + 1, :])):
                act.dma_start(tile, row.rearrange("(a c) -> a c", a=1)).then_inc(s["bias_in"], 16)
            act.dma_start(b3[0:EX, :], e_b3).then_inc(s["bias_in"], 16)
            act.wait_ge(s["edges_pad"], 96)
            act.dma_start(nxt, dst_p[1:E + 1].rearrange("(r c) -> r c", c=ROW)).then_inc(s["next_in"], 16)
            ln_act(1, 0)
            ln_act(1, 1)
            with nc.allow_non_contiguous_dma(reason="biases as columns"):
                for col, tile in ((s_b1.rearrange("(h p) -> p h", p=P), b1_col[:, 0:H]),
                                  (e_b1.rearrange("e p -> p e"), b1_col[:, H:H + EX]),
                                  (s_b2.rearrange("(a p) -> p a", p=P), b2_col[:, 0:1]),
                                  (e_b2.rearrange("e p -> (e p)").rearrange("(h q) -> q h", h=H), b2_col[:, 1:1 + H]),
                                  (b_qkv[2 * D:3 * D].rearrange("(h p) -> p h", p=P), bv_col[:, :])):
                    act.dma_start(tile, col).then_inc(s["bias_in"], 16)

            act.wait_ge(s["edges_got"], 48)
            act.activation(srcf_g, src_g, ACT.Copy).then_inc(s["srcf_ready"], 1)
            ln_act(2, 0)
            ln_act(2, 1)
            for k in range(5):
                act.wait_ge(s["turned"], k + 1)
                b0, nb = 4 * k, min(4, BLOCKS - 4 * k)
                act.activation(idx_t[:, 0:NG, b0:b0 + nb].rearrange("p g b -> p b g"),
                               banks[k][:, 0:nb * P].rearrange("p (b c) -> p b c", c=P)[:, :, 0:NG], ACT.Copy)\
                    .then_inc(s["turned_s"], 1)

            ln_act(NC_P // 2, 0)

            act.wait_ge(s["turned_k"], 5)
            for k in range(REL_LOADS):
                h, r0 = k * RH // R, k * RH % R
                act.wait_ge(rel_in[k % 2], (k // 2 + 1) * 16)
                act.activation(wr[:, 0, h, r0:r0 + RH, :], wstage[k % 2], ACT.Copy, scale=SCALE)\
                    .then_inc(s["prep_act"], 1)
                act.activation(wr[:, 2, h, r0:r0 + RH, :], wstage[k % 2], ACT.Copy)\
                    .then_inc(s["prep_act"], 1)

            def hi_part(t, g, q):
                n0 = g * GN + q * BANK_N
                act.wait_ge(s["blocks_used"], t * TB + g * BLOCKS + (LAST0, BLOCKS - 1)[q] + 1)
                if g + q == 0 and (not isinstance(t, int) or t):
                    act.wait_ge(s["w_done"], t)
                for h in range(H):
                    act.activation(s_hi[:, h, :, n0:n0 + BANK_N].rearrange("p r n -> p n r"),
                                   banks[2 * q + h][:, :].rearrange("p (n r) -> p n r", r=R),
                                   ACT.Copy, scale=1.0 / SCALE).then_inc(s["hi_done"], 1)

            def m_act(m, step):
                later = not isinstance(m, int) or m > 0
                if step == "xt":
                    act.wait_ge(s["m_turned"], m + 1)
                    if later:
                        act.wait_ge(s["m_xnt_out"], m * 16)
                    act.activation(xnt_m[:, 0:D], B7[:, 0:D], ACT.Copy, scale=1.0 / SCALE).then_inc(s["m_xh"], 1)
                elif step == "sq":
                    act.wait_ge(s["m_k"], m + 1)
                    if later:
                        act.wait_ge(s["m_sum"], m)
                    act.activation(q2, B5[:, D:2 * D], ACT.Square, accum_out=stat[:, 3:4]).then_inc(s["m_q2"], 1)
                    act.activation(k2, B5[:, 0:D], ACT.Square, accum_out=stat[:, 0:1]).then_inc(s["m_k2"], 1)
                    act.wait_ge(s["m_q2"], m + 1)
                    act.activation(q4, q2, ACT.Square, accum_out=stat[:, 4:5]).then_inc(s["m_q4"], 1)
                    act.wait_ge(s["m_q4"], m + 1)
                    act.activation(stat[:, 5:6], stat[:, 4:5], ACT.Sqrt).then_inc(s["m_nb"], 1)
                elif step == "k4":
                    act.wait_ge(s["m_k2n"], m + 1)
                    act.activation(k4, k2n, ACT.Square).then_inc(s["m_k4"], 1)
                else:
                    act.wait_ge(s["m_qt"], m + 1)
                    if later:
                        act.wait_ge(s["m_q_out"], m * 16)
                    act.activation(q2nt, B7[:, D:2 * D], ACT.Copy).then_inc(s["m_qtc"], 1)

            M_AT = {1: "xt", 3: "sq", 7: "k4", 11: "qt"}

            def w16_act(k):
                own, parts = ((wkq, wkq16), (wown, wown16))[k]
                act.wait_ge(s["w16_ready"], k + 1)
                act.activation(parts[:, 0, :, :], own[:, :, :], ACT.Copy, scale=SCALE)\
                    .then_inc(s["w16_hi"], 1)
                act.activation(parts[:, 2, :, :], own[:, :, :], ACT.Copy).then_inc(s["w16_hi"], 1)

            def g_and_m(t, ms, weights=False):
                for b in range(TB):
                    if weights and b in W16_ACT_AT:
                        w16_act(W16_ACT_AT.index(b))
                    if b % MSLOT in M_AT and ms[b // MSLOT] is not None:
                        m_act(ms[b // MSLOT], M_AT[b % MSLOT])
                    if b % BLOCKS == LAST0:
                        hi_part(t, b // BLOCKS, 0)
                    if b % BLOCKS == BLOCKS - 1:
                        hi_part(t, b // BLOCKS, 1)

            g_and_m(0, (None, None, 0), weights=True)
            with act.Fori(1, L1 - 1) as t:
                g_and_m(t, (MS * t - 2, MS * t - 1, MS * t))
            g_and_m(L1 - 1, (T - 3, T - 2, T - 1))

            act.wait_ge(s["mix_dve"], 3)
            act.activation(pcol[:, 4:6], pcol[:, 0:2], ACT.Sqrt).then_inc(s["mix_act"], 1)

            def p_act(p, step):
                if step == "sd":
                    act.wait_ge(s["p_ln"], p + 1)
                    act.activation(stat[:, 6:7], stat[:, 17:18], ACT.Sqrt, bias=eps_ln[:, 0:1])\
                        .then_inc(s["p_sd"], 1)
                elif step == "xt":
                    act.wait_ge(s["p_xt"], p + 1)
                    act.activation(xn2t, B6[:, 0:D], ACT.Copy).then_inc(s["p_xtc"], 1)
                elif step == "h1s":
                    act.wait_ge(s["p_h1s"], p + 1)
                    for j in range(H):
                        act.activation(h1[:, j, :], B6[:, j * P:(j + 1) * P], ACT.Relu,
                                       bias=b1_col[:, j:j + 1]).then_inc(s["p_h1"], 1)
                elif step == "h1e":
                    act.wait_ge(s["p_h1e"], p + 1)
                    for j in range(EX):
                        act.activation(h1[:, H + j, :], B5[:, j * P:(j + 1) * P], ACT.Relu,
                                       bias=b1_col[:, H + j:H + j + 1]).then_inc(s["p_h1"], 1)
                elif step == "exp":
                    act.wait_ge(s["p_max"], p + 1)
                    act.activation(gate[:, 4:8], gate[:, 0:4], ACT.Exp, bias=stat[:, 8:9],
                                   accum_out=stat[:, 9:10]).then_inc(s["p_exp"], 1)
                elif step == "exp2":
                    act.wait_ge(s["p_gmax"], p + 1)
                    act.activation(gate[:, 12:16], gate[:, 8:12], ACT.Exp, bias=stat[:, 11:12])\
                        .then_inc(s["p_exp2"], 1)
                elif step == "h2":
                    act.wait_ge(s["p_l2"], p + 1)
                    act.activation(h2s, B6[:, 0:P], ACT.Relu, bias=b2_col[:, 0:1]).then_inc(s["p_h2"], 1)
                    for j in range(H):
                        act.activation(h2[:, j * P:(j + 1) * P], B6[:, (1 + j) * P:(2 + j) * P], ACT.Relu,
                                       bias=b2_col[:, 1 + j:2 + j]).then_inc(s["p_h2"], 1)

            STEPS = ["sd", "xt", "exp", "h1s", "exp2", "h1e", "h2"]

            def g_and_p(t, half, p0, at=ACT_AT):
                for b in range(TB):
                    slot = half * TB + b
                    for k, a in enumerate(at[slot // PSLOT]):
                        if slot % PSLOT == a:
                            p_act(p0 + slot // PSLOT, STEPS[k])
                    if b % BLOCKS == LAST0:
                        hi_part(t, b // BLOCKS, 0)
                    if b % BLOCKS == BLOCKS - 1:
                        hi_part(t, b // BLOCKS, 1)

            g_and_p(L1, 0, 0, ACT_AT_0)
            g_and_p(L1 + 1, 1, 0, ACT_AT_0)
            with act.Fori(1, J2) as j:
                g_and_p(2 * j + L1, 0, PS * j)
                g_and_p(2 * j + (L1 + 1), 1, PS * j)
            for k in STEPS:
                p_act(T - 1, k)

        @block.vector
        def _(dve):
            chain = {"n": 0}

            def link(ins):
                chain["n"] += 1
                ins.then_inc(s["dve_c"], 1)
                dve.wait_ge(s["dve_c"], chain["n"])

            def ln_dve(n, buf):
                c = 2 * n + buf
                last = isinstance(n, int) and c == NC_P - 1
                dve.wait_ge(x_in[buf], (n + 1 + last) * 16)
                K = 2 * CH + 1
                base = c * K
                for j in range(CH):
                    dve.bn_stats(st[:, j, :], xc[buf][:, j, :]).then_inc(s["dve_p"], 1)
                dve.wait_ge(s["dve_p"], base + CH)
                dve.memset(carrier[:, :], 0.0)
                for j in range(CH):
                    dve.bn_aggr(mv[:, j, :], st[:, j, :]).then_inc(s["dve_p"], 1)
                dve.wait_ge(s["dve_p"], base + 2 * CH)
                dve.nop().then_inc(s["ln_done"], 1)
                dve.wait_ge(s["sd_ready"], c + 2)
                dve.reciprocal(rstd[:, :], rstd[:, :]).then_inc(s["dve_p"], 1)
                dve.wait_ge(s["dve_p"], base + 2 * CH + 1)
                if not isinstance(n, int) or n:
                    dve.wait_ge(s["lo_ready"], c - 1)
                for j in range(CH):
                    ins = dve.tensor_scalar(xnc[buf][:, j, :], xc[buf][:, j, :], mv[:, j, 0:1], rstd[:, j:j + 1],
                                            ALU.subtract, ALU.mult)
                ins.then_inc(s["xn_ready"], 1)

            first_node = group_c[0:NG, 2 * BLOCKS:2 * BLOCKS + 1]
            dve.wait_ge(s["rows_in"], 16)
            dve.tensor_copy(rfb[:, :], rows[:, 0:1].to_broadcast([ROWS, NG])).then_inc(s["rf_ready"], 1)
            ln_dve(0, 0)
            dve.wait_ge(s["search_in"], 32)
            dve.wait_ge(s["idx_ready"], 6)
            dve.wait_ge(s["rf_wide"], 1)
            link(dve.tensor_scalar(rfb[0:NG, 0:NG], banks[0][0:NG, 0:NG], first_node, None, ALU.is_lt, ALU.add,
                                   accum_out=ec[0:NG, 1:2]))
            link(dve.tensor_scalar(rfb[0:NG, 0:ROWS - NG], banks[0][0:NG, NG:ROWS], first_node, None, ALU.is_lt,
                                   ALU.add, accum_out=ec[0:NG, 2:3]))
            link(dve.tensor_tensor(ec[0:NG, 3:4], ec[0:NG, 1:2], ec[0:NG, 2:3], ALU.add))
            link(dve.tensor_scalar(ec[0:NG, 4:5], ec[0:NG, 3:4], -1.0, 0.0, ALU.add, ALU.max))
            dve.tensor_copy(ei[0:NG, 0:1], ec[0:NG, 4:5]).then_inc(s["row_ready"], 1)
            ln_dve(0, 1)
            dve.wait_ge(s["row_got"], 16)
            row_f = srcf_g[:, 0:ROW]
            link(dve.tensor_copy(row_f, key_g[:, 0:ROW].bitcast(I32)))
            link(dve.tensor_scalar(key_g[:, 0:ROW], row_f, first_node, None, ALU.is_lt, ALU.add,
                                   accum_out=ec[0:NG, 5:6]))
            dve.scalar_tensor_tensor(ei[0:NG, 1:2], ec[0:NG, 4:5], float(ROW), ec[0:NG, 5:6], ALU.mult, ALU.add)\
                .then_inc(s["start_ready"], 1)
            ln_dve(1, 0)
            ln_dve(1, 1)

            dve.wait_ge(s["edges_got"], 48)
            rel = dst_g.bitcast(F32)
            link(dve.tensor_scalar(rel, dst_g, first_node, None, ALU.subtract))
            dve.scalar_tensor_tensor(key_g, rel, float(R), typ_g, ALU.mult, ALU.add).then_inc(s["edges_kf"], 1)
            in_block = rel.rearrange("p (b c) -> p b c", c=P)
            link(dve.tensor_tensor(gate[0:NG, 0:BLOCKS], in_block[:, :, P - 1], group_c[0:NG, BLOCKS:2 * BLOCKS],
                                   ALU.is_ge))
            link(dve.tensor_tensor(gate[0:NG, BLOCKS:2 * BLOCKS], in_block[:, :, 0], group_c[0:NG, 0:BLOCKS],
                                   ALU.is_lt))
            link(dve.tensor_reduce(bad[0:NG, 1:2], gate[0:NG, 0:2 * BLOCKS], AX.X, ALU.add))
            link(dve.tensor_scalar(bad[0:NG, 2:3], rel[:, CAP - 1:CAP], float(GN), None, ALU.is_lt))
            ln_dve(2, 0)
            dve.wait_ge(s["xn_ready"], NC_P - 2)
            dve.memset(xc[0][96:P, CH - 1, :], 0.0).then_inc(s["pad_made"], 1)
            ln_dve(2, 1)
            ln_dve(NC_P // 2, 0)
            dve.wait_ge(s["next_in"], 16)
            nxt_f = nxt.bitcast(F32)
            link(dve.tensor_tensor(nxt_f, nxt, rows, ALU.subtract))
            link(dve.tensor_reduce(ec[0:ROWS, 0:1], nxt_f, AX.X, ALU.min))
            dve.tensor_scalar(bad[0:ROWS, 0:1], ec[0:ROWS, 0:1], 0.0, None, ALU.is_lt).then_inc(s["bad_ready"], 1)
            dve.wait_ge(s["flag_sum"], 1)
            link(dve.tensor_reduce(flag_f[:, :], banks[2][0:1, 0:4], AX.X, ALU.add))
            dve.tensor_copy(flag[:, :], flag_f[:, :]).then_inc(s["flag_ready"], 1)
            for k in range(5):
                dve.wait_ge(s["turned"], 5 + k + 1)
                b0, nb = 4 * k, min(4, BLOCKS - 4 * k)
                dve.tensor_copy(key_t[:, 0:NG, b0:b0 + nb].rearrange("p g b -> p b g"),
                                banks[(5 + k) % 8][:, 0:nb * P].rearrange("p (b c) -> p b c", c=P)[:, :, 0:NG])\
                    .then_inc(s["turned_k"], 1)
            dve.wait_ge(s["turned_k"], 5)
            dve.memset(gate[:, :], 1.0).then_inc(s["prep_dve"], 1)
            dve.memset(key_t[:, NG:NG + GT, :], -1.0).then_inc(s["prep_dve"], 1)
            dve.wait_ge(s["prep_dve"], 2)
            dve.wait_ge(s["lo_ready"], NC_P)

            def weights_dve(step):
                if step < REL_LOADS:
                    h, r0 = step * RH // R, step * RH % R
                    dve.wait_ge(s["prep_act"], 2 * step + 2)
                    dve.scalar_tensor_tensor(wr[:, 1, h, r0:r0 + RH, :].rearrange("p r d -> p (r d)"),
                                             wstage[step % 2].rearrange("p r d -> p (r d)"), SCALE,
                                             wr[:, 0, h, r0:r0 + RH, :].rearrange("p r d -> p (r d)"),
                                             ALU.mult, ALU.subtract).then_inc(s["rel_lo"], 1)
                elif step < REL_LOADS + H:
                    h = step - REL_LOADS
                    dve.wait_ge(s["mixing_in"], 3 * 16)
                    for c, dest in ((0, wkq[:, h, D:2 * D]), (1, wkq[:, h, 0:D])):
                        link(dve.tensor_reduce(ec[:, 6:7], wq_s[:, h, c * D:(c + 1) * D], AX.X, ALU.add))
                        link(dve.tensor_scalar(ec[:, 7:8], ec[:, 6:7], 1.0 / D, None, ALU.mult))
                        link(dve.tensor_scalar(dest, wq_s[:, h, c * D:(c + 1) * D], ec[:, 7:8], None,
                                               ALU.subtract))
                    if h == H - 1:
                        dve.nop().then_inc(s["w16_ready"], 1)
                elif step == REL_LOADS + H:
                    dve.wait_ge(s["bias_in"], 12 * 16)
                    for row in (bias_row[0:1, 0:D], bias_row[0:1, D:2 * D]):
                        link(dve.tensor_reduce(ec[0:1, 6:7], row, AX.X, ALU.add))
                        link(dve.tensor_scalar(ec[0:1, 7:8], ec[0:1, 6:7], 1.0 / D, None, ALU.mult))
                        link(dve.tensor_scalar(row, row, ec[0:1, 7:8], None, ALU.subtract))
                elif step == REL_LOADS + H + 1:
                    dve.wait_ge(s["mixw_pe"], 2)
                    link(dve.tensor_copy(wvo, B6[:, :].rearrange("p (a b) -> p a b", b=D)))
                    dve.nop().then_inc(s["w16_ready"], 1)
                    link(dve.tensor_copy(bvo_b[:, :], B7[:, 0:D]))
                    link(dve.tensor_tensor(bias_row[0:1, 2 * D:3 * D], bias_row[0:1, 2 * D:3 * D], bvo_b[0:1, :],
                                           ALU.add))
                    link(dve.memset(ones16[:, :], 1.0))
                    link(dve.tensor_copy(bias_part[0:1, 0, :], bias_row[0:1, :]))
                elif step == REL_LOADS + H + 2:
                    link(dve.tensor_tensor(bias_left[0:1, :], bias_row[0:1, :], bias_part[0:1, 0, :], ALU.subtract))
                    link(dve.tensor_copy(bias_part[0:1, 1, :], bias_left[0:1, :]))
                    link(dve.tensor_tensor(bias_part[0:1, 2, :], bias_left[0:1, :], bias_part[0:1, 1, :],
                                           ALU.subtract))
                    link(dve.memset(work[:, 9:11, :], 0.0))
                    dve.nop().then_inc(s["mix_dve"], 1)
                else:
                    k = step - (REL_LOADS + H + 3)
                    own, parts = ((wkq, wkq16), (wown, wown16))[k]
                    dve.wait_ge(s["w16_hi"], 2 * k + 2)
                    dve.scalar_tensor_tensor(parts[:, 1, :, :].rearrange("p h c -> p (h c)"),
                                             own[:, :, :].rearrange("p h c -> p (h c)"), SCALE,
                                             parts[:, 0, :, :].rearrange("p h c -> p (h c)"),
                                             ALU.mult, ALU.subtract).then_inc(s["w16_lo"], 1)

            def keys(t, b0, b1, n):
                for g in range(b0 // BLOCKS, (b1 - 1) // BLOCKS + 1):
                    lo, hi = max(b0, g * BLOCKS), min(b1, (g + 1) * BLOCKS)
                    own = key_t[:, bass.ds(GT * t + g, 1), lo - g * BLOCKS:hi - g * BLOCKS]
                    ins = dve.tensor_copy(key_now[:, lo:hi], own.rearrange("p o b -> p (o b)"))
                ins.then_inc(s["keys_ready"], 1)
                dve.wait_ge(s["keys_ready"], n)

            def one_hot(t, b):
                lo, hi = WIN[b % BLOCKS]
                w = (hi - lo) * R
                if b >= OH or not isinstance(t, int) or t:
                    dve.wait_ge(s["blocks_used"], t * TB + b - OH + 1)
                dve.tensor_scalar(hot[:, b % OH, 0:w], iota16[:, lo * R:hi * R], key_now[:, b:b + 1],
                                  hot_v[:, b % BLOCKS:b % BLOCKS + 1], ALU.is_equal, ALU.mult)\
                    .then_inc(s["hot_ready"], 1)

            def next_hot(t, b):
                if b == 0:
                    keys(t, AHEAD, TB, 2 * t + 2)
                if b == TB - AHEAD:
                    keys(t + 1, 0, AHEAD, 2 * t + 3)
                if b < TB - AHEAD:
                    one_hot(t, b + AHEAD)
                else:
                    one_hot(t + 1, b + AHEAD - TB)

            def lo_part(t, g, q):
                n0 = g * GN + q * BANK_N
                for h in range(H):
                    dve.wait_ge(s["hi_done"], (4 * t + 2 * g + q) * H + h + 1)
                    dve.scalar_tensor_tensor(
                        s_lo[:, h, :, n0:n0 + BANK_N].rearrange("p r n -> p n r"),
                        s_hi[:, h, :, n0:n0 + BANK_N].rearrange("p r n -> p n r"), -SCALE,
                        banks[2 * q + h][:, :].rearrange("p (n r) -> p n r", r=R), ALU.mult, ALU.add)\
                        .then_inc(s["lo_done"], 1)

            def u_part(t):
                dve.wait_ge(s["w_done"], t + 1)
                if not isinstance(t, int) or t:
                    dve.wait_ge(s["u_out"], t * 16)
                dve.scalar_tensor_tensor(u_g[:, :], GB[:, D:2 * D], 0.0, x_g[:, :], ALU.max, ALU.add)\
                    .then_inc(s["u_half"], 1)
                dve.wait_ge(s["u_half"], t + 1)
                dve.tensor_tensor(u_g[:, :], u_g[:, :], GB[:, 0:D], ALU.add).then_inc(s["u_ready"], 1)

            NM = 6

            def m_dve(m, step, k=0, mask=False):
                inside = post_c[:, 16 + P * H:17 + P * H] if mask else ones[:, 0:1]
                later = not isinstance(m, int) or m > 0

                def mlink(n, ins):
                    ins.then_inc(s["dve_m"], 1)
                    dve.wait_ge(s["dve_m"], m * NM + n)

                if step == "xn":
                    dve.wait_ge(s["m_in"], (m + 1) * 16)
                    if not isinstance(m, int) or m > 2:
                        dve.wait_ge(s["m_used"], m - 2)
                    dve.tensor_tensor(xn_m[k], tab_m[:, 0:D], tab_m[:, D:2 * D], ALU.add).then_inc(s["m_xn"], 1)
                elif step == "xt":
                    dve.wait_ge(s["m_xh"], m + 1)
                    dve.scalar_tensor_tensor(xnt_m[:, D:2 * D], xnt_m[:, 0:D], -SCALE, B7[:, 0:D], ALU.mult,
                                             ALU.add)\
                        .then_inc(s["m_xnt"], 1)
                elif step == "k":
                    dve.wait_ge(s["m_k2"], m + 1)
                    mlink(1, dve.tensor_scalar(stat[:, 1:2], stat[:, 0:1], EPS_DIV, None, ALU.add))
                    mlink(2, dve.reciprocal(stat[:, 2:3], stat[:, 1:2]))
                    if later:
                        dve.wait_ge(s["m_used"], m)
                    dve.tensor_scalar(k2n, k2, stat[:, 2:3], inside, ALU.mult, ALU.mult).then_inc(s["m_k2n"], 1)
                    dve.wait_ge(s["m_nb"], m + 1)
                    mlink(3, dve.tensor_scalar(stat[:, 6:7], stat[:, 3:4], EPS_DIV, None, ALU.add))
                    mlink(4, dve.reciprocal(stat[:, 7:8], stat[:, 6:7]))
                    mlink(5, dve.tensor_scalar(stat[:, 8:9], stat[:, 5:6], stat[:, 7:8], EPS_NORM, ALU.mult, ALU.max))
                    mlink(6, dve.reciprocal(stat[:, 9:10], stat[:, 8:9]))
                    if later:
                        dve.wait_ge(s["m_qt"], m)
                    dve.tensor_scalar(q2n, q2, stat[:, 7:8], stat[:, 9:10], ALU.mult, ALU.mult)\
                        .then_inc(s["m_q2n"], 1)
                else:
                    if later:
                        dve.wait_ge(s["m_sum"], m)
                    dve.tensor_tensor(k2n_sum, k2n_sum, k2n, ALU.add)
                    dve.wait_ge(s["m_k4"], m + 1)
                    dve.tensor_tensor(k4_sum, k4_sum, k4, ALU.add).then_inc(s["m_sum"], 1)

            M_AT = {1: "xt", 2: "xn", 4: "k", 9: "sum"}
            WEIGHTS_AT = [0, 1, 2, 3, 4, 5, 6, 7, 8, 9, 11, 12, 14, 15, 16]

            def g_and_m(t, ms, u_late=True, weights=False):
                for b in range(TB):
                    next_hot(t, b)
                    if b == U_AT and u_late:
                        u_part(t - 1)
                    if weights and b in WEIGHTS_AT:
                        weights_dve(WEIGHTS_AT.index(b))
                    if b % MSLOT in M_AT and ms[b // MSLOT] is not None:
                        m = ms[b // MSLOT]
                        if M_AT[b % MSLOT] != "xn":
                            m_dve(m, M_AT[b % MSLOT], mask=isinstance(m, int) and m == T - 1)
                        elif not isinstance(m, int) or m < T - 1:
                            m_dve(m + 1, "xn", (b // MSLOT + 1) % MS)
                    if weights and b == (MS - 1) * MSLOT - 1:
                        m_dve(0, "xn", MS - 1)
                    if b % BLOCKS == LAST0 + 1:
                        lo_part(t, b // BLOCKS, 0)
                    if b == BLOCKS:
                        lo_part(t, 0, 1)
                lo_part(t, 1, 1)

            dve.wait_ge(s["consts_in"], 32)
            general = dve.value_load(flag[0:1, 0:1])
            with dve.If(general > 0):
                with dve.Fori(0, NEB) as k:
                    NL = 6

                    def step(n, ins):
                        ins.then_inc(s["dve_g"], 1)
                        dve.wait_ge(s["dve_g"], k * NL + n)

                    for j in range(3):
                        dve.wait_ge(s[f"gp_in{j}"], k * 16 + 16)
                    step(1, dve.scalar_tensor_tensor(gp_f[:, 0:1], gp_i[:, 1:2], float(R), gp_i[:, 2:3], ALU.mult,
                                                     ALU.add))
                    dve.tensor_copy(gp_keys, gp_f[:, 0:1].to_broadcast([P, P]))
                    dve.tensor_copy(gp_i[:, 3:4], gp_f[:, 0:1]).then_inc(s["gp_key"], 1)
                    dve.wait_ge(s["gp_wide"], k + 1)
                    step(2, dve.tensor_scalar(gp_same, banks[0][:, 0:P], gp_f[:, 0:1], None, ALU.is_equal))
                    dve.nop().then_inc(s["gp_made"], 1)
                    step(3, dve.tensor_tensor(gp_earlier, gp_same, post_c[:, POST_C - P:], ALU.mult))
                    step(4, dve.tensor_reduce(gp_f[:, 1:2], gp_earlier, AX.X, ALU.max))
                    step(5, dve.tensor_scalar(gp_f[:, 2:3], gp_f[:, 1:2], float(2 ** 20), gp_f[:, 0:1], ALU.mult,
                                              ALU.add))
                    dve.wait_ge(s["gp_sum"], k + 1)
                    dve.wait_ge(s["gp_got"], k * 32 + 32)
                    step(6, dve.tensor_tensor(gp_new, gp_was, banks[1][:, 0:D], ALU.add))
                    dve.tensor_copy(gp_i[:, 4:5], gp_f[:, 2:3]).then_inc(s["gp_new"], 1)
                dve.memset(gp_parts, 0.0).then_inc(s["dve_g"], 1)
                dve.wait_ge(s["dve_g"], NEB * 6 + 1)
                with dve.Fori(0, NG * PAIRS // P) as k:
                    NR = 3

                    def step(n, ins):
                        ins.then_inc(s["dve_g"], 1)
                        dve.wait_ge(s["dve_g"], k * NR + (NEB * 6 + 1 + n))

                    dve.wait_ge(s["gp_row_in"], k * 16 + 16)
                    step(1, dve.tensor_scalar(gp_parts[:, 0, 0:D], gp_was, 1.0 / SCALE, None, ALU.mult))
                    step(2, dve.scalar_tensor_tensor(gp_left, gp_parts[:, 0, 0:D], -SCALE, gp_was, ALU.mult, ALU.add))
                    step(3, dve.tensor_copy(gp_parts[:, 1, 0:D], gp_left))
                    dve.tensor_tensor(gp_parts[:, 1, D:2 * D], gp_left, gp_parts[:, 1, 0:D], ALU.subtract)\
                        .then_inc(s["gp_row_made"], 1)
                dve.wait_ge(s["gp_done"], 1)
                dve.memset(carrier[:, :], 0.0)

            keys(0, 0, AHEAD, 1)
            for b in range(AHEAD):
                one_hot(0, b)
            dve.wait_ge(s["bias_in"], 12 * 16)
            dve.wait_ge(s["mixw_pe"], 1)
            link(dve.tensor_copy(wvt_s, B5[:, :].rearrange("p (a b) -> p a b", b=D)))
            for h in range(H):
                link(dve.tensor_copy(bvb[:, h, :], bv_col[:, h:h + 1].to_broadcast([P, P])))
            dve.nop().then_inc(s["prep_dve"], 1)
            g_and_m(0, (None, None, 0), u_late=False, weights=True)
            g_and_m(1, (1, 2, 3))
            with dve.Fori(2, L1 - 1) as t:
                g_and_m(t, (MS * t - 2, MS * t - 1, MS * t))
            g_and_m(L1 - 1, (T - 3, T - 2, T - 1))

            dve.wait_ge(s["m_used"], T)
            dve.wait_ge(s["m_xnt_out"], T * 16)
            yt = work[:, 0:2, :]
            dve.wait_ge(s["m_sum"], T)
            link(dve.tensor_copy(yt, B6[:, :].rearrange("p (a b) -> p a b", b=D)))
            dve.wait_ge(s["mix_pe"], 1)
            link(dve.tensor_copy(pcol[:, 0:4], B7[:, 0:4]))
            dve.nop().then_inc(s["mix_dve"], 2)
            dve.wait_ge(s["mix_act"], 1)
            link(dve.tensor_scalar(pcol[:, 4:6], pcol[:, 4:6], EPS_NORM, None, ALU.max))
            link(dve.reciprocal(pcol[:, 6:8], pcol[:, 4:6]))
            link(dve.tensor_scalar(pcol[:, 6:8], pcol[:, 6:8], 1.0 / sqrt(N), None, ALU.mult))
            u_part(L1 - 1)
            dve.wait_ge(s["mix_pe"], 2)
            for h in range(H):
                link(dve.scalar_tensor_tensor(m1[:, h, :], bvo_b[:, :], pcol[:, 2 + h:3 + h],
                                              B5[:, h * D:(h + 1) * D], ALU.mult, ALU.add))
                link(dve.tensor_scalar(m1[:, h, :], m1[:, h, :], pcol[:, 6 + h:7 + h], None, ALU.mult))
            dve.nop().then_inc(s["mix_dve"], 2)

            NPC = 16
            pchain = {"n": 0}

            def plink(p, ins):
                pchain["n"] += 1
                ins.then_inc(s["dve_c2"], 1)
                dve.wait_ge(s["dve_c2"], p * NPC + pchain["n"])

            def p_dve(p, step):
                if step == "x1":
                    pchain["n"] = 0
                    dve.wait_ge(s["p_mix"], p + 1)
                    if isinstance(p, int) and p == T - 1:
                        dve.wait_ge(s["u_ready"], T)
                        dve.tensor_tensor(x1, B5[:, 0:D], u_g[:, :], ALU.add).then_inc(s["p_x1"], 1)
                    else:
                        dve.wait_ge(s["p_in"], (p + 1) * 32)
                        dve.tensor_tensor(x1, B5[:, 0:D], u_p, ALU.add).then_inc(s["p_x1"], 1)
                    dve.wait_ge(s["p_x1"], p + 1)
                    pchain["n"] += 1
                    dve.bn_stats(stat[:, 18:24], x1).then_inc(s["dve_c2"], 1)
                    dve.wait_ge(s["dve_c2"], p * NPC + pchain["n"])
                    dve.memset(carrier[:, :], 0.0)
                    dve.bn_aggr(stat[:, 16:18], stat[:, 18:24]).then_inc(s["p_ln"], 1)
                elif step == "xn2":
                    dve.wait_ge(s["p_sd"], p + 1)
                    plink(p, dve.reciprocal(stat[:, 7:8], stat[:, 6:7]))
                    dve.tensor_scalar(xn2, x1, stat[:, 16:17], stat[:, 7:8], ALU.subtract, ALU.mult)\
                        .then_inc(s["p_xn2"], 1)
                elif step == "max":
                    dve.wait_ge(s["p_log"], p + 1)
                    plink(p, dve.tensor_copy(gate[:, 0:4], B7[:, 0:4]))
                    plink(p, dve.tensor_reduce(stat[:, 10:11], gate[:, 0:4], AX.X, ALU.max))
                    dve.tensor_scalar(stat[:, 8:9], stat[:, 10:11], -1.0, None, ALU.mult).then_inc(s["p_max"], 1)
                elif step == "gate":
                    dve.wait_ge(s["p_exp"], p + 1)
                    plink(p, dve.reciprocal(stat[:, 12:13], stat[:, 9:10]))
                    plink(p, dve.tensor_scalar(gate[:, 8:12], gate[:, 4:8], stat[:, 12:13], None, ALU.mult))
                    plink(p, dve.tensor_reduce(stat[:, 13:14], gate[:, 8:12], AX.X, ALU.max))
                    dve.tensor_scalar(stat[:, 11:12], stat[:, 13:14], -1.0, None, ALU.mult).then_inc(s["p_gmax"], 1)
                    other = gate[:, 8:12].unsqueeze(1).to_broadcast([P, EX, EX])
                    own = gate[:, 8:12].unsqueeze(2).to_broadcast([P, EX, EX])
                    gt = gate[:, 16:32].rearrange("p (a b) -> p a b", b=EX)
                    eq = gate[:, 32:48].rearrange("p (a b) -> p a b", b=EX)
                    before = post_c[:, 0:16].rearrange("p (a b) -> p a b", b=EX)
                    plink(p, dve.tensor_tensor(gt, other, own, ALU.is_gt))
                    plink(p, dve.tensor_tensor(eq, other, own, ALU.is_equal))
                    plink(p, dve.tensor_tensor(eq, eq, before, ALU.mult))
                    plink(p, dve.tensor_tensor(gt, gt, eq, ALU.add))
                    plink(p, dve.tensor_reduce(gate[:, 48:52], gt, AX.X, ALU.add))
                    plink(p, dve.tensor_scalar(gate[:, 52:56], gate[:, 48:52], 2.0, None, ALU.is_lt))
                elif step == "gate2":
                    dve.wait_ge(s["p_exp2"], p + 1)
                    plink(p, dve.tensor_tensor(gate[:, 56:60], gate[:, 52:56], gate[:, 12:16], ALU.mult))
                    plink(p, dve.tensor_reduce(stat[:, 14:15], gate[:, 56:60], AX.X, ALU.add))
                    plink(p, dve.reciprocal(stat[:, 15:16], stat[:, 14:15]))
                    dve.tensor_scalar(gate[:, 60:64], gate[:, 56:60], stat[:, 15:16], None, ALU.mult)\
                        .then_inc(s["p_w5"], 1)
                elif step == "wt":
                    dve.wait_ge(s["p_wt"], p + 1)
                    dve.tensor_copy(w5t[:, :], B7[0:EX + 1, D:D + P]).then_inc(s["p_wtc"], 1)
                elif step == "h2g":
                    dve.wait_ge(s["p_h2"], 3 * p + 3)
                    dve.wait_ge(s["p_wb"], p + 1)
                    dve.tensor_tensor(h2g, h2, B7[:, 0:D], ALU.mult).then_inc(s["p_h2g"], 1)
                elif step == "out":
                    dve.wait_ge(s["p_l3"], p + 1)
                    if not isinstance(p, int) or p:
                        dve.wait_ge(s["out_done"], p * 16)
                    dve.tensor_tensor(o_p, x1, B5[:, 0:D], ALU.add).then_inc(s["p_out"], 1)

            STEPS = ["x1", "xn2", "max", "gate", "gate2", "wt", "h2g", "out"]

            def g_and_p(t, half, p0, at=DVE_AT, u_late=True):
                for b in range(TB):
                    slot = half * TB + b
                    next_hot(t, b)
                    if b == U_AT and u_late:
                        u_part(t - 1)
                    for k, a in enumerate(at[slot // PSLOT]):
                        if slot % PSLOT == a:
                            p_dve(p0 + slot // PSLOT, STEPS[k])
                    if b % BLOCKS == LAST0 + 1:
                        lo_part(t, b // BLOCKS, 0)
                    if b == BLOCKS:
                        lo_part(t, 0, 1)
                lo_part(t, 1, 1)

            g_and_p(L1, 0, 0, DVE_AT_0, u_late=False)
            g_and_p(L1 + 1, 1, 0, DVE_AT_0)
            with dve.Fori(1, J2) as j:
                g_and_p(2 * j + L1, 0, PS * j)
                g_and_p(2 * j + (L1 + 1), 1, PS * j)
            u_part(T - 1)
            for k in STEPS:
                p_dve(T - 1, k)
            assert pchain["n"] == NPC

        @block.tensor
        def _(pe):
            mm = nc.tensor.matmul

            pe.wait_ge(s["search_in"], 32)
            pe.wait_ge(s["rf_ready"], 1)
            mm(banks[0][0:NG, 0:ROWS], rfb[:, 0:NG], ident[0:ROWS, 0:ROWS], start=True, stop=True)\
                .then_inc(s["rf_wide"], 1)

            def turn(k, source, bank):
                for j in range(min(4, BLOCKS - 4 * k)):
                    b = 4 * k + j
                    last = nc.tensor.transpose(bank[:, j * P:j * P + NG], source[:, b * P:(b + 1) * P],
                                               ident[0:NG, 0:NG])
                last.then_inc(s["turned"], 1)

            pe.wait_ge(s["srcf_ready"], 1)
            for k in range(5):
                turn(k, srcf_g, banks[k])
            pe.wait_ge(s["edges_kf"], 1)
            for k in range(5):
                if 5 + k >= 8:
                    pe.wait_ge(s["turned_s"], 5 + k - 8 + 1)
                turn(k, key_g, banks[(5 + k) % 8])
            pe.wait_ge(s["bad_ready"], 1)
            pe.wait_ge(s["idx_ready"], 6)
            pe.wait_ge(s["turned_s"], 5)
            mm(banks[2][0:1, 0:4], ones[:, 0:1], bad[:, :], start=True, stop=True).then_inc(s["flag_sum"], 1)
            pe.wait_ge(s["flag_ready"], 1)
            pe.wait_ge(s["turned_k"], 5)

            def weights_pe(step):
                if step == 0:
                    pe.wait_ge(s["mixing_in"], 3 * 16)
                    for hc in range(H):
                        for hr in range(H):
                            last = nc.tensor.transpose(B5[:, hc * D + hr * P:hc * D + (hr + 1) * P],
                                                       wq_s[:, hr, 2 * D + hc * P:2 * D + (hc + 1) * P],
                                                       ident[:, :])
                    last.then_inc(s["mixw_pe"], 1)
                elif step == 1:
                    pe.wait_ge(s["prep_dve"], 3)
                    for hr in range(H):
                        for k in range(H):
                            mm(B6[:, hr * D:(hr + 1) * D], wvt_s[:, k, hr * P:(hr + 1) * P], wo_s[:, k, :],
                               start=(k == 0), stop=(k == H - 1))
                    for k in range(H):
                        last = mm(B7[:, 0:D], bvb[:, k, :], wo_s[:, k, :], start=(k == 0), stop=(k == H - 1))
                    last.then_inc(s["mixw_pe"], 1)
                else:
                    pe.wait_ge(s["mix_dve"], 1)
                    mm(B6[:, :], zeros[:, 0:P], zeros[:, :], start=True, stop=True).then_inc(s["mixw_pe"], 1)
                    pe.wait_ge(s["bias_parts"], 3 * 16)
                    pe.wait_ge(s["rel_lo"], REL_LOADS)
                    pe.wait_ge(s["weights_in"], 8 * 16)
                    pe.wait_ge(s["w16_lo"], 2)

            def agg(t, b):
                g, bb = b // BLOCKS, b % BLOCKS
                lo, hi = WIN[bb]
                if b % RB == 0:
                    pe.wait_ge(got[b // RB], (t + 1) * RB * 16)
                n_before = 4 * t + 2 * g
                if bb == 0 and (b or not isinstance(t, int) or t):
                    pe.wait_ge(s["lo_done"], (n_before - 1) * H)
                if bb == FIRST1 and (b >= BLOCKS or not isinstance(t, int) or t):
                    pe.wait_ge(s["lo_done"], n_before * H)
                pe.wait_ge(s["hot_ready"], t * TB + b + 1)
                for q in range(2):
                    l, r = max(lo, q * BANK_N), min(hi, (q + 1) * BANK_N)
                    if l >= r:
                        continue
                    first = 0 if q == 0 else FIRST1
                    for h in range(H):
                        for part in range(2):
                            last = mm(banks[2 * q + h][:, (l - q * BANK_N) * R:(r - q * BANK_N) * R],
                                      ring[:, b, part * D + h * P:part * D + (h + 1) * P],
                                      hot[:, b % OH, (l - lo) * R:(r - lo) * R],
                                      start=(bb == first and part == 0), stop=True, skip_group_check=True)
                last.then_inc(s["blocks_used"], 1)

            def relations(t):
                pe.wait_ge(s["xg_in"], (t + 1) * 32)
                if not isinstance(t, int) or t:
                    pe.wait_ge(s["u_ready"], t)
                mm(GB[:, :], ones16[:, :], bias16[:, 2 * D:4 * D], start=True, stop=False)
                for h in range(H):
                    for w, part in ((0, 0), (1, 0), (2, 1)):
                        mm(GB[:, :], xnt_g[:, part, h, :], wown16[:, w, h, :], start=False, stop=False)
                for h in range(H):
                    pe.wait_ge(s["hi_done"], (4 * t + 3) * H + h + 1)
                    for r in range(R):
                        for w in (0, 1):
                            mm(GB[:, D:2 * D], s_hi[:, h, r, :], wr[:, w, h, r, :], start=False, stop=False)
                    pe.wait_ge(s["lo_done"], (4 * t + 3) * H + h + 1)
                    for r in range(R):
                        last = mm(GB[:, D:2 * D], s_lo[:, h, r, :], wr[:, 2, h, r, :], start=False,
                                  stop=(h == H - 1 and r == R - 1))
                last.then_inc(s["w_done"], 1)

            def m_pe(m, step, k):
                later = not isinstance(m, int) or m > 0
                if step == "xt":
                    pe.wait_ge(s["m_xn"], m + 1)
                    if later:
                        pe.wait_ge(s["m_qtc"], m)
                    for h in range(H):
                        last = nc.tensor.transpose(B7[:, h * P:(h + 1) * P], xn_m[k][:, h * P:(h + 1) * P], ident[:, :])
                    last.then_inc(s["m_turned"], 1)
                elif step == "kq":
                    pe.wait_ge(s["m_xnt"], m + 1)
                    if later:
                        pe.wait_ge(s["m_k2"], m)
                    mm(B5[:, :], ones16[:, :], bias16[:, 0:2 * D], start=True, stop=False)
                    for h in range(H):
                        for w, part in ((0, 0), (1, 0), (2, 1)):
                            last = mm(B5[:, :], xnt_m[:, part * D + h * P:part * D + (h + 1) * P],
                                      wkq16[:, w, h, :], start=False, stop=(h == H - 1 and w == 2))
                    last.then_inc(s["m_k"], 1)
                elif step == "sum":
                    pe.wait_ge(s["m_k2n"], m + 1)
                    for h in range(H):
                        last = mm(B6[:, h * D:(h + 1) * D], xn_m[k][:, h * P:(h + 1) * P], k2n, start=False, stop=True,
                                  skip_group_check=True)
                    last.then_inc(s["m_used"], 1)
                else:
                    pe.wait_ge(s["m_q2n"], m + 1)
                    for h in range(H):
                        last = nc.tensor.transpose(B7[:, D + h * P:D + (h + 1) * P], q2n[:, h * P:(h + 1) * P],
                                                   ident[:, :])
                    last.then_inc(s["m_qt"], 1)

            M_AT = {0: "xt", 2: "kq", 8: "sum", 11: "qt"}

            def g_and_m(t, ms, before=True, weights=False):
                for b in range(TB):
                    agg(t, b)
                    if before and b == 0:
                        relations(t - 1)
                    if weights and b == 18:
                        weights_pe(2)
                    if b % MSLOT in M_AT and ms[b // MSLOT] is not None:
                        m_pe(ms[b // MSLOT], M_AT[b % MSLOT], b // MSLOT)

            general = pe.value_load(flag[0:1, 0:1])
            with pe.If(general > 0):
                with pe.Fori(0, NEB) as k:
                    pe.wait_ge(s["gp_key"], k + 1)
                    mm(banks[0][:, 0:P], gp_keys, ident[:, :], start=True, stop=True).then_inc(s["gp_wide"], 1)
                    pe.wait_ge(s["gp_made"], k + 1)
                    pe.wait_ge(s["gp_got"], k * 32 + 32)
                    mm(banks[1][:, 0:D], gp_same, gp_rows[:, 0:D], start=True, stop=False)
                    mm(banks[1][:, 0:D], gp_same, gp_rows[:, D:2 * D], start=False, stop=True)\
                        .then_inc(s["gp_sum"], 1)
            weights_pe(0)
            weights_pe(1)
            g_and_m(0, (None, None, 0), before=False, weights=True)
            g_and_m(1, (1, 2, 3))
            with pe.Fori(2, L1 - 1) as t:
                g_and_m(t, (MS * t - 2, MS * t - 1, MS * t))
            g_and_m(L1 - 1, (T - 3, T - 2, T - 1))

            pe.wait_ge(s["m_sum"], T)
            pe.wait_ge(s["m_qtc"], T)
            for j, own in ((0, k4_sum), (2, k2n_sum)):
                for h in range(H):
                    last = mm(B7[:, j + h:j + h + 1], own[:, h * P:(h + 1) * P], ones[:, 0:1], start=True, stop=True)
            last.then_inc(s["mix_pe"], 1)
            relations(L1 - 1)
            pe.wait_ge(s["mix_dve"], 3)
            yt = work[:, 0:2, :]
            for hc in range(H):
                for k in range(H):
                    last = mm(B5[:, hc * D:(hc + 1) * D], yt[:, k, hc * P:(hc + 1) * P], wvo[:, k, :],
                              start=(k == 0), stop=(k == H - 1))
            last.then_inc(s["mix_pe"], 1)

            def p_pe(p, step):
                if step == "mix":
                    if isinstance(p, int) and p == T - 1:
                        pe.wait_ge(s["p_in"], p * 32 + 16)
                    else:
                        pe.wait_ge(s["p_in"], (p + 1) * 32)
                    if not isinstance(p, int) or p:
                        pe.wait_ge(s["p_out"], p)
                    else:
                        pe.wait_ge(s["mix_dve"], 5)
                    for h in range(H):
                        last = mm(B5[:, 0:D], q2nt_p[:, h * P:(h + 1) * P], m1[:, h, :], start=(h == 0),
                                  stop=(h == H - 1))
                    last.then_inc(s["p_mix"], 1)
                elif step == "xt":
                    pe.wait_ge(s["p_xn2"], p + 1)
                    for h in range(H):
                        last = nc.tensor.transpose(B6[:, h * P:(h + 1) * P], xn2[:, h * P:(h + 1) * P], ident[:, :])
                    last.then_inc(s["p_xt"], 1)
                elif step == "l1":
                    pe.wait_ge(s["p_xtc"], p + 1)
                    mm(B7[:, 0:EX], ones16[:, :], bias16[:, 4 * D:BIAS], start=True, stop=False)
                    for h in range(H):
                        last = mm(B7[:, 0:EX], xn2t[:, h * P:(h + 1) * P], gw[:, h, :], start=False, stop=(h == H - 1))
                    last.then_inc(s["p_log"], 1)
                    for j in range(H):
                        for h in range(H):
                            last = mm(B6[:, j * P:(j + 1) * P], sw1[:, h, j * P:(j + 1) * P],
                                      xn2t[:, h * P:(h + 1) * P], start=(h == 0), stop=(h == H - 1))
                    last.then_inc(s["p_h1s"], 1)
                    for j in range(EX):
                        for h in range(H):
                            last = mm(B5[:, j * P:(j + 1) * P], ew1[:, h, j, :],
                                      xn2t[:, h * P:(h + 1) * P], start=(h == 0), stop=(h == H - 1))
                    last.then_inc(s["p_h1e"], 1)
                elif step == "wt":
                    pe.wait_ge(s["p_w5"], p + 1)
                    nc.tensor.transpose(B7[0:EX + 1, D:D + P], gate[:, 60:65], ident[:, :]).then_inc(s["p_wt"], 1)
                elif step == "l2":
                    pe.wait_ge(s["p_wtc"], p + 1)
                    for j in range(H):
                        last = mm(B7[:, j * P:(j + 1) * P], post_c[0:EX, 16 + j * P:16 + (j + 1) * P], w5t[0:EX, :],
                                  start=True, stop=True)
                    last.then_inc(s["p_wb"], 1)
                    pe.wait_ge(s["p_h1"], (p + 1) * (H + EX))
                    for h in range(H):
                        mm(B6[:, 0:P], sw2[:, h, :], h1[:, h, :], start=(h == 0), stop=(h == H - 1))
                    for e in range(EX):
                        o = (e % 2) * EH2
                        last = mm(B6[o:o + EH2, (1 + e // 2) * P:(2 + e // 2) * P], ew2[:, e, :], h1[:, H + e, :],
                                  start=True, stop=True)
                    last.then_inc(s["p_l2"], 1)
                elif step == "l3":
                    pe.wait_ge(s["p_h2g"], p + 1)
                    mm(B5[:, 0:D], w5t[:, :], b3[:, :], start=True, stop=False)
                    mm(B5[:, 0:D], h2s, sw3[:, :], start=False, stop=False)
                    for j in range(H):
                        last = mm(B5[:, 0:D], h2g[:, j * P:(j + 1) * P], ew3[:, j, :], start=False, stop=(j == H - 1))
                    last.then_inc(s["p_l3"], 1)

            STEPS = ["mix", "xt", "l1", "wt", "l2", "l3"]

            def g_and_p(t, half, p0, at=PE_AT, before=True):
                for b in range(TB):
                    slot = half * TB + b
                    agg(t, b)
                    for k, a in enumerate(at[slot // PSLOT]):
                        if slot % PSLOT == a:
                            p_pe(p0 + slot // PSLOT, STEPS[k])
                    if before and b == 0:
                        relations(t - 1)

            g_and_p(L1, 0, 0, PE_AT_0, before=False)
            g_and_p(L1 + 1, 1, 0, PE_AT_0)
            with pe.Fori(1, J2) as j:
                g_and_p(2 * j + L1, 0, PS * j)
                g_and_p(2 * j + (L1 + 1), 1, PS * j)
            p_pe(T - 1, STEPS[0])
            relations(T - 1)
            for k in STEPS[1:]:
                p_pe(T - 1, k)


_INS = ["x", "src", "dst", "edge_type_16", "L0_gnn_W_rel", "L0_gnn_W_self", "L0_gnn_bias", "L0_mix_W_qkv",
        "L0_mix_b_qkv", "L0_mix_W_out", "L0_mix_b_out", "L0_ffn_sW1", "L0_ffn_sb1", "L0_ffn_sW2", "L0_ffn_sb2",
        "L0_ffn_sW3", "L0_ffn_sb3", "L0_ffn_eW1", "L0_ffn_eb1", "L0_ffn_eW2", "L0_ffn_eb2", "L0_ffn_eW3",
        "L0_ffn_eb3", "L0_ffn_gW", "L0_ffn_gb"]


def consts():
    ident = np.eye(P, dtype=np.float32)
    iota = np.tile(np.arange(PAIRS, dtype=np.float16), (P, 1))
    group = np.zeros((P, 2 * BLOCKS + 1), np.float32)
    group[:, 0:BLOCKS] = [lo for lo, _ in WIN]
    group[:, BLOCKS:2 * BLOCKS] = [hi if hi < GN else 2.0 ** 20 for _, hi in WIN]
    group[:, 2 * BLOCKS] = GN * np.arange(P)
    post = np.zeros((P, POST_C), np.float32)
    post[:, 0:16] = np.tril(np.ones((EX, EX), np.float32), -1).reshape(1, 16)
    for e in range(EX):
        post[e, 16 + (e // 2) * P + (e % 2) * EH2:16 + (e // 2) * P + (e % 2 + 1) * EH2] = 1.0
    post[0:TAIL, 16 + P * H] = 1.0
    post[:, POST_C - P:] = np.tril(np.ones((P, P), np.float32), -1)
    pad = np.zeros((3, CAP), np.int32)
    pad[0] = N + (np.arange(CAP) / DEG).astype(np.int32)
    pad[0][pad[0] >= NP] = PADDST
    return {"c_ident": ident, "c_iota": iota, "c_group": group, "c_post": post, "c_pad": pad}


def kernel(**inputs):
    import concourse.bacc as bacc
    from concourse.bass_utils import run_bass_kernel_spmd

    nc = bacc.Bacc("TRN2", target_bir_lowering=False, num_devices=1)
    arrays, args = {}, []
    for name, a in [(n, inputs[n]) for n in _INS] + list(consts().items()):
        a = np.ascontiguousarray(a)
        arrays[name] = a
        args.append(nc.dram_tensor(name, a.shape, mybir.dt.from_np(a.dtype), kind="ExternalInput").ap())
    args.append(nc.dram_tensor("out", (N, D), F32, kind="ExternalOutput").ap())
    build(nc, *args)
    r = run_bass_kernel_spmd(nc, [arrays], core_ids=[0])
    return r.results[0]["out"]
```
